# Optimizing a Trainium2 kernel written in Bass

```python
import numpy as np
import jax
import jax.numpy as jnp

def _softmax(x, axis=-1):
    return jax.nn.softmax(x, axis=axis)

def _gelu(x):
    return jax.nn.gelu(x, approximate=True)

def _silu(x):
    return jax.nn.silu(x)

def _sigmoid(x):
    return jax.nn.sigmoid(x)

def _layernorm(x, axis=-1, eps=1e-05):
    m = jnp.mean(x, axis=axis, keepdims=True)
    v = jnp.var(x, axis=axis, keepdims=True)
    return (x - m) / jnp.sqrt(v + eps)

def _scatter_add(tgt, idx, src, axis=0):
    return tgt.at[idx].add(src)

def _segment_sum(src, seg, n):
    return jax.ops.segment_sum(src, seg, n)
kernel_name = 'mk_sandwich_d1_jaxref_r4_391217'

def setup_inputs(seed: int=0):
    np.random.seed(seed)
    _w = jnp.asarray

    def _L0_attn_setup():
        import jax, jax.numpy as jnp
        import numpy as np
        D_MODEL = 256
        D_STATE = 128
        HEAD_DIM = 64
        EXPAND = 2
        K = 4
        N_GROUPS = 1
        D_INNER = EXPAND * D_MODEL
        N_HEADS = D_INNER // HEAD_DIM
        D_PROJ = 2 * D_INNER + 2 * N_GROUPS * D_STATE + N_HEADS
        EPS = 1e-06

        def _rmsnorm(x, w):
            return x * jax.lax.rsqrt(jnp.mean(x * x, axis=-1, keepdims=True) + EPS) * w
        key = jax.random.key(seed)
        ks = jax.random.split(key, 8)
        B, L = (2, 512)
        x = jax.random.normal(ks[0], (B, L, D_MODEL), jnp.float32)
        norm_w = jnp.ones((D_MODEL,), jnp.float32)
        in_proj_w = jax.random.normal(ks[1], (D_PROJ, D_MODEL), jnp.float32) / np.sqrt(D_MODEL).astype(np.float32)
        conv_w = jax.random.normal(ks[2], (D_INNER, K), jnp.float32) / np.sqrt(K).astype(np.float32)
        conv_b = jnp.zeros((D_INNER,), jnp.float32)
        A_log = jnp.log(jax.random.uniform(ks[3], (N_HEADS,), jnp.float32) * 15.0 + 1.0)
        D = jnp.ones((N_HEADS,), jnp.float32)
        dt_bias = jnp.log(jax.random.uniform(ks[4], (N_HEADS,), jnp.float32) * 0.099 + 0.001)
        out_proj_w = jax.random.normal(ks[5], (D_MODEL, D_INNER), jnp.float32) / np.sqrt(D_INNER).astype(np.float32)
        return dict(x=x, norm_w=norm_w, in_proj_w=in_proj_w, conv_w=conv_w, conv_b=conv_b, A_log=A_log, D=D, dt_bias=dt_bias, out_proj_w=out_proj_w)
    _L0_attn_in = _L0_attn_setup()

    def _L0_ffn_setup():
        import jax, jax.numpy as jnp
        import numpy as np
        H = 16
        E = 8
        EPS = 1e-05

        def _layernorm(x, g, b):
            mu = jnp.mean(x, axis=-1, keepdims=True)
            var = jnp.mean(jnp.square(x - mu), axis=-1, keepdims=True)
            return (x - mu) * jax.lax.rsqrt(var + EPS) * g + b
        key = jax.random.key(seed)
        T, B, C = (256, 8, 256)
        ks = jax.random.split(key, 12)
        s = 0.02
        return {'x': jax.random.normal(ks[0], (T, B, C), jnp.float32), 'in_proj_w': jax.random.normal(ks[1], (3 * C, C), jnp.float32) * s, 'in_proj_b': jnp.zeros((3 * C,), jnp.float32), 'out_w': jax.random.normal(ks[2], (C, C), jnp.float32) * s, 'out_b': jnp.zeros((C,), jnp.float32), 'ln1_g': jnp.ones((C,), jnp.float32), 'ln1_b': jnp.zeros((C,), jnp.float32), 'router_w': jax.random.normal(ks[3], (E, C), jnp.float32) * s, 'router_b': jnp.zeros((E,), jnp.float32), 'w1': jax.random.normal(ks[4], (E, C, C), jnp.float32) * s, 'b1': jnp.zeros((E, C), jnp.float32), 'w2': jax.random.normal(ks[5], (E, C, C), jnp.float32) * s, 'b2': jnp.zeros((E, C), jnp.float32), 'ln2_g': jnp.ones((C,), jnp.float32), 'ln2_b': jnp.zeros((C,), jnp.float32)}
    _L0_ffn_in = _L0_ffn_setup()
    _d = {'L0_attn_x': _L0_attn_in['x'], 'L0_attn_norm_w': _L0_attn_in['norm_w'], 'L0_attn_in_proj_w': _L0_attn_in['in_proj_w'], 'L0_attn_conv_w': _L0_attn_in['conv_w'], 'L0_attn_conv_b': _L0_attn_in['conv_b'], 'L0_attn_A_log': _L0_attn_in['A_log'], 'L0_attn_D': _L0_attn_in['D'], 'L0_attn_dt_bias': _L0_attn_in['dt_bias'], 'L0_attn_out_proj_w': _L0_attn_in['out_proj_w'], 'L0_ffn_in_proj_w': _L0_ffn_in['in_proj_w'], 'L0_ffn_in_proj_b': _L0_ffn_in['in_proj_b'], 'L0_ffn_out_w': _L0_ffn_in['out_w'], 'L0_ffn_out_b': _L0_ffn_in['out_b'], 'L0_ffn_ln1_g': _L0_ffn_in['ln1_g'], 'L0_ffn_ln1_b': _L0_ffn_in['ln1_b'], 'L0_ffn_router_w': _L0_ffn_in['router_w'], 'L0_ffn_router_b': _L0_ffn_in['router_b'], 'L0_ffn_w1': _L0_ffn_in['w1'], 'L0_ffn_b1': _L0_ffn_in['b1'], 'L0_ffn_w2': _L0_ffn_in['w2'], 'L0_ffn_b2': _L0_ffn_in['b2'], 'L0_ffn_ln2_g': _L0_ffn_in['ln2_g'], 'L0_ffn_ln2_b': _L0_ffn_in['ln2_b']}
    _x0 = _d['L0_attn_x']
    _d['L0_attn_x'] = jax.random.normal(jax.random.fold_in(jax.random.key(seed), 1), (8, 1024, 256), dtype=_x0.dtype)
    del _x0
    return _d

def reference(L0_attn_x, L0_attn_norm_w, L0_attn_in_proj_w, L0_attn_conv_w, L0_attn_conv_b, L0_attn_A_log, L0_attn_D, L0_attn_dt_bias, L0_attn_out_proj_w, L0_ffn_in_proj_w, L0_ffn_in_proj_b, L0_ffn_out_w, L0_ffn_out_b, L0_ffn_ln1_g, L0_ffn_ln1_b, L0_ffn_router_w, L0_ffn_router_b, L0_ffn_w1, L0_ffn_b1, L0_ffn_w2, L0_ffn_b2, L0_ffn_ln2_g, L0_ffn_ln2_b):

    def _L0_attn_ref(x, norm_w, in_proj_w, conv_w, conv_b, A_log, D, dt_bias, out_proj_w):
        import jax, jax.numpy as jnp
        import numpy as np
        D_MODEL = 256
        D_STATE = 128
        HEAD_DIM = 64
        EXPAND = 2
        K = 4
        N_GROUPS = 1
        D_INNER = EXPAND * D_MODEL
        N_HEADS = D_INNER // HEAD_DIM
        D_PROJ = 2 * D_INNER + 2 * N_GROUPS * D_STATE + N_HEADS
        EPS = 1e-06

        def _rmsnorm(x, w):
            return x * jax.lax.rsqrt(jnp.mean(x * x, axis=-1, keepdims=True) + EPS) * w
        batch, L, _ = x.shape
        residual = x
        xn = _rmsnorm(x, norm_w)
        proj = jnp.einsum('bld,pd->blp', xn, in_proj_w)
        i = 0
        z = proj[:, :, i:i + D_INNER]
        i += D_INNER
        x_ssm = proj[:, :, i:i + D_INNER]
        i += D_INNER
        bc = N_GROUPS * D_STATE
        Bm = proj[:, :, i:i + bc].reshape(batch, L, N_GROUPS, D_STATE)
        i += bc
        Cm = proj[:, :, i:i + bc].reshape(batch, L, N_GROUPS, D_STATE)
        i += bc
        dt_raw = proj[:, :, i:i + N_HEADS]
        xp = jnp.pad(x_ssm, ((0, 0), (K - 1, 0), (0, 0)))
        x_conv = conv_b
        for k in range(K):
            x_conv = x_conv + xp[:, k:k + L, :] * conv_w[:, k]
        x_conv = jax.nn.silu(x_conv)
        xh = x_conv.reshape(batch, L, N_HEADS, HEAD_DIM)
        dt = jax.nn.softplus(dt_raw + dt_bias)
        dA = jnp.exp(-jnp.exp(A_log) * dt)
        dtx = dt[..., None] * xh
        gidx = jnp.arange(N_HEADS) // (N_HEADS // N_GROUPS)
        Bg = Bm[:, :, gidx, :]
        Cg = Cm[:, :, gidx, :]

        def step(h, inp):
            dA_t, dtx_t, B_t, C_t = inp
            h = h * dA_t[:, :, None, None] + dtx_t[..., None] * B_t[:, :, None, :]
            y_t = jnp.einsum('bhpn,bhn->bhp', h, C_t)
            return (h, y_t)
        h0 = jnp.zeros((batch, N_HEADS, HEAD_DIM, D_STATE), jnp.float32)
        xs = (jnp.swapaxes(dA, 0, 1), jnp.swapaxes(dtx, 0, 1), jnp.swapaxes(Bg, 0, 1), jnp.swapaxes(Cg, 0, 1))
        _, ys = jax.lax.scan(step, h0, xs)
        y = jnp.swapaxes(ys, 0, 1) + D[None, None, :, None] * xh
        y = y.reshape(batch, L, D_INNER) * jax.nn.silu(z)
        return residual + jnp.einsum('bli,di->bld', y, out_proj_w)

    def _L0_ffn_ref(x, in_proj_w, in_proj_b, out_w, out_b, ln1_g, ln1_b, router_w, router_b, w1, b1, w2, b2, ln2_g, ln2_b):
        import jax, jax.numpy as jnp
        import numpy as np
        H = 16
        E = 8
        EPS = 1e-05

        def _layernorm(x, g, b):
            mu = jnp.mean(x, axis=-1, keepdims=True)
            var = jnp.mean(jnp.square(x - mu), axis=-1, keepdims=True)
            return (x - mu) * jax.lax.rsqrt(var + EPS) * g + b
        T, B, C = x.shape
        D = C // H
        qkv = x @ in_proj_w.T + in_proj_b
        q, k, v = jnp.split(qkv, 3, axis=-1)
        q = q.reshape(T, B, H, D)
        k = k.reshape(T, B, H, D)
        v = v.reshape(T, B, H, D)
        scale = 1.0 / np.sqrt(D).astype(np.float32)
        scores = jnp.einsum('tbhd,sbhd->bhts', q, k) * scale
        attn = jax.nn.softmax(scores, axis=-1)
        ctx = jnp.einsum('bhts,sbhd->tbhd', attn, v).reshape(T, B, C)
        attn_out = ctx @ out_w.T + out_b
        h = _layernorm(x + attn_out, ln1_g, ln1_b)
        flat = h.reshape(-1, C)
        logits = flat @ router_w.T + router_b
        probs = jax.nn.softmax(logits, axis=-1)
        _, top_i = jax.lax.top_k(probs, 2)
        assign = jnp.max(top_i, axis=-1)
        out = jnp.zeros_like(flat)
        for e in range(E):
            he = jax.nn.gelu(flat @ w1[e].T + b1[e], approximate=False)
            oe = he @ w2[e].T + b2[e]
            out = jnp.where((assign == e)[:, None], oe, out)
        moe_out = out.reshape(T, B, C)
        return _layernorm(h + moe_out, ln2_g, ln2_b)
    x = L0_attn_x
    x = x + _layernorm(_L0_attn_ref(_layernorm(x, axis=-1), L0_attn_norm_w, L0_attn_in_proj_w, L0_attn_conv_w, L0_attn_conv_b, L0_attn_A_log, L0_attn_D, L0_attn_dt_bias, L0_attn_out_proj_w), axis=-1)
    x = x + _layernorm(_L0_ffn_ref(_layernorm(x, axis=-1), L0_ffn_in_proj_w, L0_ffn_in_proj_b, L0_ffn_out_w, L0_ffn_out_b, L0_ffn_ln1_g, L0_ffn_ln1_b, L0_ffn_router_w, L0_ffn_router_b, L0_ffn_w1, L0_ffn_b1, L0_ffn_w2, L0_ffn_b2, L0_ffn_ln2_g, L0_ffn_ln2_b), axis=-1)
    return x

_drawn_inputs = setup_inputs


def setup_inputs(seed=0):
    import zlib

    import numpy as np

    out = dict(_drawn_inputs(seed))
    spreads = {'L0_attn_norm_w': (1.0, 0.2),
     'L0_attn_conv_b': (0.0, 0.1),
     'L0_attn_D': (1.0, 0.6),
     'L0_ffn_in_proj_b': (0.0, 0.592),
     'L0_ffn_out_b': (0.0, 0.1),
     'L0_ffn_ln1_g': (1.0, 0.2),
     'L0_ffn_ln1_b': (0.0, 0.1),
     'L0_ffn_router_b': (0.0, 0.342),
     'L0_ffn_b1': (0.0, 0.8),
     'L0_ffn_b2': (0.0, 0.1),
     'L0_ffn_ln2_g': (1.0, 0.2),
     'L0_ffn_ln2_b': (0.0, 0.1)}
    factors = {'L0_ffn_in_proj_w': 3.811, 'L0_ffn_out_w': 2.977, 'L0_ffn_w1': 2.995, 'L0_ffn_w2': 2.782}
    for name, (base, spread) in spreads.items():
        noise = np.random.default_rng([zlib.crc32(name.encode()), seed]).standard_normal(out[name].shape)
        drawn = base * np.exp(spread * noise) if base else spread * noise
        out[name] = jnp.asarray(drawn.astype(out[name].dtype))
    for name, factor in factors.items():
        out[name] = (out[name] * factor).astype(out[name].dtype)
    return out
```

```python
from contextlib import ExitStack

import concourse.bass as bass
from concourse import mybir

F32 = mybir.dt.float32
BF16 = mybir.dt.bfloat16
I32 = mybir.dt.int32
ALU = mybir.AluOpType
ACT = mybir.ActivationFunctionType
AX = mybir.AxisListType

P = 128
ROWS, SEQ, DM = 8, 1024, 256
KC = DM // P
DI = 512
XB = DI // P
NST = 128
HD = 64
NH = DI // HD
TAPS = 4
CHUNKS = SEQ // P
PAIRS = ROWS // 2
UNITS = CHUNKS * PAIRS
TILES = 2 * UNITS
AH, AD = 16, DM // 16
EXP = 8
EPS = 1e-5
RMS_EPS = 1e-6
PROJ = 2 * DI + 2 * NST + NH
COL_X, COL_C, COL_B = DI, 2 * DI, 2 * DI + NST
WTOK = NST + NH
SORTED = TILES + EXP
NEG = -1.0e30


class Schedule:

    def __init__(self, lags, units):
        self.lags, self.units = lags, units
        top = max(lags)
        edges = sorted({x for lag in lags for x in (lag, lag + 1, lag + units)} | {top + 1})
        self.segments = list(zip(edges[:-1], edges[1:]))

    def run(self, eng, body):
        for lo, hi in self.segments:
            if hi - lo == 1:
                body(Pass(self, eng, lo, lo, lo))
            else:
                with eng.Fori(lo, hi) as u:
                    body(Pass(self, eng, lo, hi - 1, u))


class Pass:

    def __init__(self, schedule, eng, first, last, u):
        self.schedule, self.eng, self.first, self.last, self.u = schedule, eng, first, last, u
        self.held = {}
        self.steady = all(self.runs(lag) for lag in schedule.lags) and first > max(schedule.lags)

    def runs(self, lag):
        return lag <= self.first and self.last < lag + self.schedule.units

    def _hold(self, key, make, top):
        if isinstance(self.u, int):
            return make(self.u)
        if key not in self.held:
            self.held[key] = self.eng.snap(make(self.u), min_val=0, max_val=top)
        return self.held[key]

    def unit(self, lag):
        return self._hold(("unit", lag), lambda u: u - lag, self.schedule.units - 1)

    def now(self, lag, per=1):
        if self.last < lag:
            return 0
        if self.first >= lag + self.schedule.units:
            return per * self.schedule.units
        return self._hold((lag, per, per), lambda u: (u - lag + 1) * per, per * self.schedule.units)

    def prev(self, lag, per=1, n=0):
        if self.last < lag:
            return 0
        if self.first >= lag + self.schedule.units:
            return per * self.schedule.units
        return self._hold((lag, per, n), lambda u: (u - lag) * per + n, per * self.schedule.units)


MAIN = Schedule([0, 1, 2, 3, 7, 8, 9], UNITS)
A1, A2, A3, B1, B2, B3, B4 = MAIN.lags
MLP = Schedule([0, 1], SORTED // 2)
C1, C2 = MLP.lags


def bank_free(pe, p, latest, *earlier):
    for sem, count in (latest,) if p.steady else (latest,) + earlier:
        pe.wait_ge(sem, count)


def program(nc, a):
    with ExitStack() as ctx:
        def sb(name, shape, dt=F32):
            return ctx.enter_context(nc.sbuf_tensor(name, shape, dt))

        def ps(name, shape):
            return ctx.enter_context(nc.psum_tensor(name, shape, F32))

        def sem(name):
            return ctx.enter_context(nc.semaphore(name))

        w_in = sb("w_in", [P, KC, PROJ])
        w_out = sb("w_out", [P, XB, DM])
        w_qkv = sb("w_qkv", [P, KC, 3 * DM])
        w_o = sb("w_o", [P, KC, DM])
        w_r = sb("w_r", [P, KC, EXP])
        norm_w = sb("norm_w", [P, KC])
        conv_w = sb("conv_w", [P, XB, TAPS])
        conv_b = sb("conv_b", [P, XB])
        dt_bias = sb("dt_bias", [P, NH])
        a_log = sb("a_log", [P, NH])
        neg_a = sb("neg_a", [P, NH])
        d_skip = sb("d_skip", [P, NH])
        qkv_b = sb("qkv_b", [P, 3 * DM])
        o_b = sb("o_b", [P, DM])
        ln1_g = sb("ln1_g", [P, DM])
        ln1_b = sb("ln1_b", [P, DM])
        r_b = sb("r_b", [P, EXP])
        ln2_g = sb("ln2_g", [P, DM])
        ln2_b = sb("ln2_b", [P, DM])
        ident = sb("ident", [P, P])
        upto = sb("upto", [P, P])
        before = sb("before", [P, P])
        ones = sb("ones", [P, P])
        ident_h = sb("ident_h", [P, P], BF16)
        future = sb("future", [P, P], BF16)
        half = sb("half", [P, 4])
        pool_held, dve_held = sb("pool_held", [P, 16]), sb("dve_held", [P, 16])
        zero = sb("zero", [P, DM])
        key = sb("key", [P, EXP])
        count_i = sb("count_i", [P, SORTED], I32)
        count_f = sb("count_f", [P, SORTED])

        xa = sb("xa", [P, 2, DM])
        st_a = sb("st_a", [P, 2, 6])
        mv_a = sb("mv_a", [P, 2, 2])
        var_a = sb("var_a", [P, 2, 2])
        rs_a = sb("rs_a", [P, 2, 2])
        xn = sb("xn", [P, 2, DM])
        xnT = sb("xnT", [P, KC, 2, P])
        cb_new = sb("cb_new", [P, 3, 2, P])
        dt_in = sb("dt_in", [P, 2, NH])
        dt_e = sb("dt_e", [P, 2, NH])
        dt = sb("dt", [P, 2, NH])
        xs = sb("xs", [P, XB, 2, P + TAPS - 1])
        halo = sb("halo", [P, ROWS, XB, TAPS - 1])
        cv = sb("cv", [P, XB, 2, P])
        xhT = sb("xhT", [P, XB, 2, P])
        cb = sb("cb", [P, 3, 2, P])
        mr = sb("mr", [P, 2, 2])
        da = sb("da", [P, 2, NH])
        sm = sb("sm", [P, 3, 2, NH])
        ncum = sb("ncum", [P, 2, NH])
        ex = sb("ex", [P, 3, 2, NH])
        sz = sb("sz", [P, 2, DI])
        em = sb("em", [P, 2, NH, P])
        xh = sb("xh", [P, 2, DI])
        dtx = sb("dtx", [P, 2, DI])
        wdtx = sb("wdtx", [P, 2, DI])
        state = sb("state", [P, ROWS, DI])
        y = sb("y", [P, 2, DI])
        yT = sb("yT", [P, XB, 2, P])
        xr = sb("xr", [P, 2, DM])
        x0 = sb("x0", [P, 2, DM])
        s1 = sb("s1", [P, 2, DM])
        st_c = sb("st_c", [P, 2, 6])
        mv_c = sb("mv_c", [P, 2, 2])
        var_c = sb("var_c", [P, 2])
        rs_c = sb("rs_c", [P, 2])
        x1 = sb("x1", [P, 2, DM])
        st_b = sb("st_b", [P, 2, 6])
        mv_b = sb("mv_b", [P, 2, 2])
        var_b = sb("var_b", [P, 2])
        rs_b = sb("rs_b", [P, 2])
        kept = sb("kept", [P, UNITS, 2, 2])
        xb = sb("xb", [P, 2, DM])
        xbT = sb("xbT", [P, KC, 2, P])
        qkv = sb("qkv", [P, 2 * ROWS, 3 * DM])
        prod = sb("prod", [P, 2, ROWS, DM])
        sc = sb("sc", [P, 2, ROWS, AH])
        mx = sb("mx", [P, 2, AH])
        pr = sb("pr", [P, 2, ROWS, AH])
        den = sb("den", [P, 2, AH])
        rden = sb("rden", [P, 2, AH])
        cx = sb("cx", [P, 2, DM])
        cxT = sb("cxT", [P, KC, 2, P])
        x1r = sb("x1r", [P, 2, DM])
        mrb = sb("mrb", [P, 2, 2])
        x0b = sb("x0b", [P, 2, DM])
        s2 = sb("s2", [P, 2, DM])
        st_f = sb("st_f", [P, 2, 6])
        mv_f = sb("mv_f", [P, 2, 2])
        var_f = sb("var_f", [P, 2])
        rs_f = sb("rs_f", [P, 2])
        h = sb("h", [P, 2, DM])
        hT = sb("hT", [P, KC, 2, P])
        logits = sb("logits", [P, TILES, EXP])

        work = prod[:, :, :, :].rearrange("p a b c -> p (a b c)")
        def part(n, size=TILES * EXP):
            return work[:, n * 512:n * 512 + size]
        dest_i = sb("dest_i", [P, TILES], I32)
        expert_i = sb("expert_i", [P, SORTED], I32)
        rt = sb("rt", [P, 6, TILES])
        re = sb("re", [P, 5, EXP])
        held = qkv[:, :, :].rearrange("p a b -> p (a b)")
        WE = KC * DM * EXP
        w1 = held[:, 0:WE].rearrange("p (e c n) -> p e c n", e=EXP, c=KC)
        w2 = held[:, WE:2 * WE].rearrange("p (e c n) -> p e c n", e=EXP, c=KC)
        b1 = held[:, 2 * WE:2 * WE + EXP * DM].rearrange("p (e n) -> p e n", e=EXP)
        b2 = held[:, 2 * WE + EXP * DM:2 * WE + 2 * EXP * DM].rearrange("p (e n) -> p e n", e=EXP)
        idx = sb("idx", [P, 4], I32)

        pX = ps("pX", [P, 2, 512])
        pY = ps("pY", [P, 2, 512])
        pZ = ps("pZ", [P, 2, 512])
        pW = ps("pW", [P, 512])
        pV = ps("pV", [P, 512])
        xT_v = pX[:, :, :].rearrange("p a (b r t) -> p (a b) r t", b=2, r=2)
        yT_v = pZ[:, :, :].rearrange("p a (b r t) -> p (a b) r t", b=2, r=2)

        small_in, w_in_in, w_in_2, exp_in = (sem(n) for n in ("small_in", "w_in_in", "w_in_2", "exp_in"))
        consts, prep, zeroed = sem("consts"), sem("prep"), sem("zeroed")
        alog_e = sem("alog_e")
        xa_in, xr_in, x1r_in, x1_out, h_out = (sem(n) for n in ("xa_in", "xr_in", "x1r_in", "x1_out", "h_out"))
        LN = 4
        ln_a, xn_ok, xnT_ps, xnT_sb, cbT_ps, cbT_sb = (sem(n) for n in ("ln_a", "xn_ok", "xnT_ps", "xnT_sb", "cbT_ps", "cbT_sb"))
        tok_ps, btok_sb, soft, xs_ps, xs_sb = (sem(n) for n in ("tok_ps", "btok_sb", "soft", "xs_ps", "xs_sb"))
        SOFT = 3
        halo_in, halo_out, conv, cth_ok, xhT_ok = (sem(n) for n in ("halo_in", "halo_out", "conv", "cth_ok", "xhT_ok"))
        mr_ok, shift_ok, da_ok, cum_ps, decay, ex_ok = (sem(n) for n in ("mr_ok", "shift_ok", "da_ok", "cum_ps", "decay", "ex_ok"))
        DECAY = 2
        z_ps, zt_ok, sz_ok, arg_ps, exp_ok = (sem(n) for n in ("z_ps", "zt_ok", "sz_ok", "arg_ps", "exp_ok"))
        xh_ps, xh_sb, dtx_ok, wdtx_ok, dx_ok, m_ok = (sem(n) for n in ("xh_ps", "xh_sb", "dtx_ok", "wdtx_ok", "dx_ok", "m_ok"))
        inter_ps, intra_ps, st_ps, hdec, h_ok = (sem(n) for n in ("inter_ps", "intra_ps", "st_ps", "hdec", "h_ok"))
        yin_ok, ysum_ok, yd_ok, y_ok = (sem(n) for n in ("yin_ok", "ysum_ok", "yd_ok", "y_ok"))
        yT_ps, yT_sb, out_ps, x0_ok, s1_ok, ln_c, s1n_ok, x1_ok = (sem(n) for n in ("yT_ps", "yT_sb", "out_ps", "x0_ok", "s1_ok", "ln_c", "s1n_ok", "x1_ok"))
        ln_b, kept_ok, xb_ok, xbT_ps, xbT_sb, qkv_ps, qkv_sb = (sem(n) for n in ("ln_b", "kept_ok", "xb_ok", "xbT_ps", "xbT_sb", "qkv_ps", "qkv_sb"))
        qk_ok, sc_ok, mx_ok, scm_ok, e_ok, den_ok, rden_ok = (sem(n) for n in ("qk_ok", "sc_ok", "mx_ok", "scm_ok", "e_ok", "den_ok", "rden_ok"))
        pr_ok, pv_ok, cx_ok = (sem(n) for n in ("pr_ok", "pv_ok", "cx_ok"))
        cxT_ps, cxT_sb, ao_ps, mrb_ok, x0b_ok, x0o_ok, s2_ok = (sem(n) for n in ("cxT_ps", "cxT_sb", "ao_ps", "mrb_ok", "x0b_ok", "x0o_ok", "s2_ok"))
        ln_f, s2n_ok, hg_ok, hb_ok = (sem(n) for n in ("ln_f", "s2n_ok", "hg_ok", "hb_ok"))
        hT_ps, hT_sb, lg_ps, lg_sb = (sem(n) for n in ("hT_ps", "hT_sb", "lg_ps", "lg_sb"))
        route, onehot_ok, routed, r_exp, r_ps, idx_ok = (sem(n) for n in ("route", "onehot_ok", "routed", "r_exp", "r_ps", "idx_ok"))
        hs_in = [sem(f"hs_in{j}") for j in range(2)]
        scattered = [sem(f"scattered{j}") for j in range(2)]
        ha_in, h2_in, haT_ps, haT_sb, f1_ps, f1_ok, g_ok, gT_ps, gT_sb, f2_ps = (
            sem(n) for n in ("ha_in", "h2_in", "haT_ps", "haT_sb", "f1_ps", "f1_ok", "g_ok", "gT_ps", "gT_sb", "f2_ps"))
        hb2_ok, s3_ok, ln_g, s3n_ok, l2g_ok, l2b_ok, ln_h, y_fin, ys_out = (
            sem(n) for n in ("hb2_ok", "s3_ok", "ln_g", "s3n_ok", "l2g_ok", "l2b_ok", "ln_h", "y_fin", "ys_out"))
        x1f_in = [sem(f"x1f_in{j}") for j in range(2)]
        gathered = [sem(f"gathered{j}") for j in range(2)]
        fin_ok, idx2_ok, sorted_zero = sem("fin_ok"), sem("idx2_ok"), sem("sorted_zeroed")
        fin_out = [sem(f"fin_out{j}") for j in range(2)]

        x_v = a["x"].rearrange("b (c p) d -> c p b d", p=P)
        out_v = a["out"].rearrange("b (c p) d -> c p b d", p=P)
        x1_v = a["x1_d"].rearrange("(v r p) d -> v p r d", r=2, p=P)
        h_v = a["h_d"].rearrange("(v r p) d -> v p r d", r=2, p=P)
        h_t = a["h_d"].rearrange("(n p) d -> n p d", p=P)
        sorted_t = a["sorted_d"].rearrange("(n p) d -> p n d", p=P)
        sorted_v = a["sorted_d"].rearrange("(v r p) d -> v p r d", r=2, p=P)
        ys_v = a["ys_d"].rearrange("(v r p) d -> v p r d", r=2, p=P)

        def at(view, i):
            if isinstance(i, int):
                return view[i]
            return view[bass.ds(i, 1)].rearrange("o p r d -> (o p) r d")

        def x_unit(view, v):
            if isinstance(v, int):
                return view[v // PAIRS][:, 2 * (v % PAIRS):2 * (v % PAIRS) + 2, :]
            chunk = v >> 2
            chunk.max_val = CHUNKS - 1
            return view[bass.ds(chunk, 1), :, bass.ds((v & 3) * 2, 2), :].rearrange("o p r d -> (o p) r d")

        def rows_of(v):
            return slice(2 * (v % PAIRS), 2 * (v % PAIRS) + 2) if isinstance(v, int) else bass.ds((v & 3) * 2, 2)

        def row_of(v, r):
            return slice(2 * (v % PAIRS) + r, 2 * (v % PAIRS) + r + 1) if isinstance(v, int) else bass.ds((v & 3) * 2 + r, 1)

        def slot_of(v, r):
            return slice(2 * (v % 8) + r, 2 * (v % 8) + r + 1) if isinstance(v, int) else bass.ds((v & 7) * 2 + r, 1)

        def group_of(v):
            return slice(ROWS * (v // 4 % 2), ROWS * (v // 4 % 2) + ROWS) if isinstance(v, int) else bass.ds(((v >> 2) & 1) * ROWS, ROWS)

        def unit_slice(v, n=1):
            return slice(v * n, v * n + n) if isinstance(v, int) else bass.ds(v * n, n)

        def one(i):
            return slice(i, i + 1) if isinstance(i, int) else bass.ds(i, 1)

        held_column = {}

        def waits_apart(eng, *waits):
            for s, c in waits:
                eng.wait_ge(s, c)
            c = held_column.setdefault(waits[0][0].name, len(held_column))
            if eng.engine == mybir.EngineType.Pool:
                nc.gpsimd.tensor_tensor(pool_held[:, c:c + 1], half[:, 0:1], half[:, 0:1], ALU.mult)
            else:
                nc.vector.memset(dve_held[:, c:c + 1], 0.0)

        block = ctx.enter_context(nc.Block())

        @block.sync
        def _(sp):
            small = [(norm_w, "norm_w"), (conv_w, "conv_w"), (conv_b, "conv_b")]
            rows = [(dt_bias, "dt_bias"), (a_log, "a_log"), (d_skip, "d_skip"), (qkv_b, "qkv_b"), (o_b, "o_b"),
                    (ln1_g, "ln1_g"), (ln1_b, "ln1_b"), (r_b, "r_b"), (ln2_g, "ln2_g"), (ln2_b, "ln2_b")]
            for t, n in small:
                sp.dma_start(t[:], a[n]).then_inc(small_in, 16)
            for t, n in rows:
                sp.dma_start(t[:], a[n].partition_broadcast(P)).then_inc(small_in, 16)
            sp.dma_start(w_in[:], a["w_in"]).then_inc(w_in_in, 16)
            for t, n in ((w_out, "w_out"), (w_qkv, "w_qkv"), (w_o, "w_o"), (w_r, "w_r")):
                sp.dma_start(t[:], a[n]).then_inc(w_in_2, 16)

            def body(p):
                if p.runs(A1):
                    sp.wait_ge(xn_ok, p.prev(A1))
                    if p.runs(A1):
                        sp.dma_start(xa[:], x_unit(x_v, p.unit(A1))).then_inc(xa_in, 16)
                if p.runs(A3):
                    sp.wait_ge(x1_ok, p.prev(A3))
                    sp.dma_start(xr[:], x_unit(x_v, p.unit(A3))).then_inc(xr_in, 16)
                if p.runs(B3):
                    sp.wait_ge(x0b_ok, p.prev(B3))
                    sp.wait_ge(x1_out, p.prev(B3, 16, 16))
                    sp.dma_start(x1r[:], at(x1_v, p.unit(B3))).then_inc(x1r_in, 16)
                if p.runs(A3):
                    sp.wait_ge(x1_ok, p.now(A3))
                    sp.dma_start(at(x1_v, p.unit(A3)), x1[:]).then_inc(x1_out, 16)
                if p.runs(B3):
                    sp.wait_ge(hb_ok, p.now(B3))
                    sp.dma_start(at(h_v, p.unit(B3)), h[:]).then_inc(h_out, 16)
            MAIN.run(sp, body)

            sp.wait_ge(pv_ok, 2 * UNITS)
            sp.wait_ge(qk_ok, 2 * UNITS)
            sp.dma_start(w1, a["w1"]).then_inc(exp_in, 16)
            sp.dma_start(w2, a["w2"]).then_inc(exp_in, 16)
            sp.dma_start(b1, a["b1"].partition_broadcast(P)).then_inc(exp_in, 16)
            sp.dma_start(b2, a["b2"].partition_broadcast(P)).then_inc(exp_in, 16)

            sp.wait_ge(h_out, 16 * UNITS)
            sp.wait_ge(x0b_ok, UNITS)
            for j in range(2):
                sp.dma_start(x1r[:, j, :], h_t[j]).then_inc(hs_in[j], 16)
            with sp.Fori(1, TILES // 2) as i:
                for j in range(2):
                    sp.wait_ge(scattered[j], i * 16)
                    sp.dma_start(x1r[:, j, :], h_t[bass.ds(2 * i + j, 1)].rearrange("o p d -> (o p) d")).then_inc(hs_in[j], 16)

            for j in range(2):
                sp.wait_ge(scattered[j], 16 * (TILES // 2))

            def mlp(p):
                if p.runs(C1):
                    sp.wait_ge(haT_ps, p.prev(C1))
                    sp.dma_start(xa[:], at(sorted_v, p.unit(C1))).then_inc(ha_in, 16)
                if p.runs(C2):
                    sp.wait_ge(hb2_ok, p.prev(C2))
                    sp.dma_start(xr[:], at(sorted_v, p.unit(C2))).then_inc(h2_in, 16)
                    sp.wait_ge(y_fin, p.now(C2))
                    sp.dma_start(at(ys_v, p.unit(C2)), x1[:]).then_inc(ys_out, 16)
            MLP.run(sp, mlp)

            for j in range(2):
                sp.dma_start((xn, xb)[j][:], at(x1_v, j)).then_inc(x1f_in[j], 16)
            with sp.Fori(0, UNITS // 2 - 1) as i:
                for j in range(2):
                    sp.wait_ge(fin_ok, 2 * i + j + 1)
                    sp.dma_start(x_unit(out_v, sp.snap(2 * i + j, min_val=0)), (s1, s2)[j][:]).then_inc(fin_out[j], 16)
                    sp.dma_start((xn, xb)[j][:], at(x1_v, sp.snap(2 * i + j + 2, min_val=0))).then_inc(x1f_in[j], 16)
            for j in range(2):
                sp.wait_ge(fin_ok, UNITS - 1 + j)
                sp.dma_start(x_unit(out_v, UNITS - 2 + j), (s1, s2)[j][:]).then_inc(fin_out[j], 16)
            for s, n in ((x1_out, UNITS), (h_out, UNITS), (ys_out, SORTED // 2), (fin_out[0], UNITS // 2), (fin_out[1], UNITS // 2)):
                sp.wait_ge(s, 16 * n)

        @block.tensor
        def _(pe):
            def transposes(out, src, cols):
                for c in range(cols):
                    for r in range(2):
                        mm = nc.tensor.transpose(out[:, c, r, :], src[:, r, c * P:(c + 1) * P], ident[:])
                return mm

            pWt = pW[:, :].rearrange("p (c r t) -> p c r t", c=2, r=2)
            pVt = pV[:, :].rearrange("p (c r t) -> p c r t", c=2, r=2)

            def project(out, lhs, weights, kn, start_col, cols):
                for k in range(kn):
                    mm = nc.tensor.matmul(out, lhs(k), weights[:, k, start_col:start_col + cols],
                                          start=(k == 0), stop=(k == kn - 1))
                return mm

            pe.wait_ge(consts, 1)
            pe.wait_ge(prep, 1)
            pe.wait_ge(w_in_2, 64)

            def body(p):
                if p.runs(B4):
                    pe.wait_ge(hb_ok, p.now(B4))
                    bank_free(pe, p, (yin_ok, p.prev(A2, 2)), (cbT_sb, p.prev(A1)), (lg_sb, p.prev(B4)))
                    transposes(pWt, h, KC).then_inc(hT_ps, 1)
                if p.runs(B3):
                    pe.wait_ge(cx_ok, p.now(B3, 2))
                    bank_free(pe, p, (qkv_sb, p.prev(B1, 2)), (exp_ok, p.prev(A2, 2)), (xnT_sb, p.prev(A1)), (cxT_sb, p.prev(B3)))
                    transposes(pY[:, 0, :].rearrange("p (c r t) -> p c r t", c=2, r=2), cx, KC).then_inc(cxT_ps, 1)
                if p.runs(B1):
                    pe.wait_ge(xb_ok, p.now(B1))
                    bank_free(pe, p, (yin_ok, p.prev(A2, 2)), (xbT_sb, p.prev(B1)))
                    transposes(pVt, xb, KC).then_inc(xbT_ps, 1)
                if p.runs(A1):
                    pe.wait_ge(xn_ok, p.now(A1))
                    bank_free(pe, p, (qkv_sb, p.prev(B1, 2)), (exp_ok, p.prev(A2, 2)), (xnT_sb, p.prev(A1)))
                    transposes(pY[:, 1, :].rearrange("p (c r t) -> p c r t", c=2, r=2), xn, KC).then_inc(xnT_ps, 1)
                if p.runs(A2):
                    bank_free(pe, p, (qkv_sb, p.prev(B1, 2)), (xs_sb, p.prev(A1)), (xh_sb, p.prev(A2)))
                    for r in range(2):
                        mm = project(pX[:, r, :], lambda k: xnT[:, k, r, :], w_in, KC, 0, DI)
                    mm.then_inc(z_ps, 1)
                if p.runs(A3):
                    pe.wait_ge(y_ok, p.now(A3))
                    bank_free(pe, p, (h_ok, p.prev(A2, 2)), (ysum_ok, p.prev(A2, 2)), (s2_ok, p.prev(B3)), (soft, p.prev(A1, SOFT)),
                              (btok_sb, p.prev(A1)), (s1_ok, p.prev(A3)))
                    if p.steady:
                        pe.wait_ge(ysum_ok, p.prev(A2, 2))
                    transposes(yT_v, y, XB).then_inc(yT_ps, 1)
                if p.runs(B4):
                    pe.wait_ge(hT_sb, p.now(B4))
                    for r in range(2):
                        mm = project(pW[:, r * EXP:(r + 1) * EXP], lambda k: hT[:, k, r, :], w_r, KC, 0, EXP)
                    mm.then_inc(lg_ps, 1)
                if p.runs(A2):
                    pe.wait_ge(da_ok, p.now(A2))
                    pe.wait_ge(shift_ok, p.now(A2))
                    bank_free(pe, p, (xbT_sb, p.now(B1)), (yin_ok, p.prev(A2, 2)))
                    rhs = da[:, :, :].rearrange("p r h -> p (r h)")
                    nc.tensor.matmul(pV[:, 256:272], upto[:], rhs, start=True, stop=True)
                    nc.tensor.matmul(pV[:, 272:288], ones[:], rhs, start=True, stop=True)
                    for r in range(2):
                        mm = nc.tensor.matmul(pV[:, r * P:(r + 1) * P], cb[:, 1, r, :], cb[:, 0, r, :], start=True, stop=True)
                    mm.then_inc(cum_ps, 1)
                if p.runs(A3):
                    pe.wait_ge(yT_sb, p.now(A3))
                    for r in range(2):
                        mm = project(pZ[:, 0, r * DM:(r + 1) * DM], lambda k: yT[:, k, r, :], w_out, XB, 0, DM)
                    mm.then_inc(out_ps, 1)

                def args(r):
                    for half_ in range(2):
                        nc.tensor.matmul(pY[:, half_, :], ident_h[:], future[:].unsqueeze(1).to_broadcast([P, 4, P]),
                                         start=True, stop=False, skip_group_check=True)
                        for i in range(4):
                            hd = 4 * half_ + i
                            mm = nc.tensor.matmul(pY[:, half_, i * P:(i + 1) * P], da[:, r, hd:hd + 1].to_broadcast([P, P]),
                                                  upto[:], start=False, stop=(i == 3), skip_group_check=True)
                    return mm

                if p.runs(A2):
                    bank_free(pe, p, (xnT_sb, p.now(A1)), (cxT_sb, p.now(B3)), (qkv_sb, p.prev(B1, 2)), (exp_ok, p.prev(A2, 2)))
                    if p.steady:
                        pe.wait_ge(cxT_sb, p.now(B3))
                    args(0).then_inc(arg_ps, 1)
                if p.runs(B3):
                    pe.wait_ge(cxT_sb, p.now(B3))
                    bank_free(pe, p, (yT_sb, p.now(A3)), (h_ok, p.prev(A2, 2)), (s2_ok, p.prev(B3)))
                    for r in range(2):
                        mm = project(pZ[:, 1, r * DM:(r + 1) * DM], lambda k: cxT[:, k, r, :], w_o, KC, 0, DM)
                    mm.then_inc(ao_ps, 1)
                if p.runs(A1):
                    pe.wait_ge(xnT_sb, p.now(A1))
                    bank_free(pe, p, (lg_sb, p.now(B4)), (yin_ok, p.prev(A2, 2)), (cbT_sb, p.prev(A1)))
                    for m in range(2):
                        for k in range(KC):
                            mm = nc.tensor.matmul(pWt[:, m, :, :], w_in[:, k, COL_C + m * NST:COL_C + (m + 1) * NST],
                                                  xnT[:, k, :, :], start=(k == 0), stop=(k == KC - 1))
                    mm.then_inc(cbT_ps, 1)
                if p.runs(A2):
                    pe.wait_ge(xhT_ok, p.now(A2))
                    pe.wait_ge(sz_ok, p.now(A2))
                    for r in range(2):
                        for b in range(XB):
                            mm = nc.tensor.transpose(pX[:, r, b * P:(b + 1) * P], xhT[:, b, r, :], ident[:])
                    mm.then_inc(xh_ps, 1)
                if p.runs(A1):
                    bank_free(pe, p, (s1_ok, p.now(A3)), (ysum_ok, p.prev(A2, 2)), (soft, p.prev(A1, SOFT)), (btok_sb, p.prev(A1)))
                    for r in range(2):
                        mm = project(pZ[:, 0, r * WTOK:(r + 1) * WTOK], lambda k: xnT[:, k, r, :], w_in, KC, COL_B, WTOK)
                    mm.then_inc(tok_ps, 1)
                if p.runs(A2):
                    pe.wait_ge(exp_ok, p.prev(A2, 2, 1))
                    args(1).then_inc(arg_ps, 1)
                if p.runs(A1):
                    bank_free(pe, p, (xh_sb, p.now(A2)), (qkv_sb, p.prev(B1, 2)), (xs_sb, p.prev(A1)))
                    for b in range(XB):
                        for k in range(KC):
                            mm = nc.tensor.matmul(xT_v[:, b, :, :], w_in[:, k, COL_X + b * P:COL_X + (b + 1) * P],
                                                  xnT[:, k, :, :], start=(k == 0), stop=(k == KC - 1))
                    mm.then_inc(xs_ps, 1)

                def inter(r, out):
                    return nc.tensor.matmul(out, cb[:, 0, r, :], state[:, row_of(p.unit(A2), r), :], start=True, stop=True)

                def intra(r, out):
                    for hd in range(NH):
                        mm = nc.tensor.matmul(out[:, hd * HD:(hd + 1) * HD], em[:, r, hd, :],
                                              dtx[:, r, hd * HD:(hd + 1) * HD], start=True, stop=True)
                    return mm

                def new_state(r, out):
                    return nc.tensor.matmul(out, cb[:, 2, r, :], wdtx[:, r, :], start=True, stop=True)

                if p.runs(A2):
                    pe.wait_ge(h_ok, p.prev(A2, 2))
                    bank_free(pe, p, (cbT_sb, p.now(A1)), (lg_sb, p.now(B4)), (yin_ok, p.prev(A2, 2)))
                    inter(0, pW[:, :]).then_inc(inter_ps, 1)
                    pe.wait_ge(m_ok, p.prev(A2, 2, 1))
                    pe.wait_ge(dtx_ok, p.now(A2))
                    bank_free(pe, p, (soft, p.prev(A1, SOFT, 1)), (s1_ok, p.now(A3)), (ysum_ok, p.prev(A2, 2)))
                    pe.wait_ge(btok_sb, p.now(A1))
                    intra(0, pZ[:, 0, :]).then_inc(intra_ps, 1)
                    pe.wait_ge(wdtx_ok, p.now(A2))
                    bank_free(pe, p, (s2_ok, p.now(B3)), (yT_sb, p.now(A3)), (h_ok, p.prev(A2, 2)))
                    new_state(0, pZ[:, 1, :]).then_inc(st_ps, 1)
                if p.runs(B1):
                    bank_free(pe, p, (exp_ok, p.now(A2, 2)), (xnT_sb, p.now(A1)), (cxT_sb, p.now(B3)), (qkv_sb, p.prev(B1, 2)))
                    pe.wait_ge(xbT_sb, p.now(B1))
                    project(pY[:, 0, :], lambda k: xbT[:, k, 0, :], w_qkv, KC, 0, 2 * DM)
                    project(pY[:, 1, 0:DM], lambda k: xbT[:, k, 0, :], w_qkv, KC, 2 * DM, DM).then_inc(qkv_ps, 1)
                if p.runs(A2):
                    pe.wait_ge(m_ok, p.now(A2, 2))
                    pe.wait_ge(decay, p.now(A2, DECAY))
                    inter(1, pV[:, :]).then_inc(inter_ps, 1)
                if p.runs(B1):
                    bank_free(pe, p, (xs_sb, p.now(A1)), (xh_sb, p.now(A2)), (qkv_sb, p.prev(B1, 2)))
                    project(pX[:, 0, :], lambda k: xbT[:, k, 1, :], w_qkv, KC, 0, 2 * DM)
                    project(pX[:, 1, 0:DM], lambda k: xbT[:, k, 1, :], w_qkv, KC, 2 * DM, DM).then_inc(qkv_ps, 1)
                if p.runs(A2):
                    pe.wait_ge(ysum_ok, p.prev(A2, 2, 1))
                    intra(1, pZ[:, 0, :]).then_inc(intra_ps, 1)
                    pe.wait_ge(h_ok, p.prev(A2, 2, 1))
                    new_state(1, pZ[:, 1, :]).then_inc(st_ps, 1)

            MAIN.run(pe, body)

            pe.wait_ge(onehot_ok, 1)
            pe.wait_ge(qkv_sb, 2 * UNITS)
            onehot = part(5)
            nc.tensor.matmul(pX[:, 0, :], before[:], onehot, start=True, stop=True)
            nc.tensor.matmul(pX[:, 1, :], ones[:], onehot, start=True, stop=True).then_inc(r_ps, 1)

            pe.wait_ge(routed, 1)
            pe.wait_ge(exp_in, 64)

            def mlp(p):
                if p.runs(C2):
                    pe.wait_ge(g_ok, p.now(C2))
                    pe.wait_ge(gT_sb, p.prev(C2))
                    transposes(pVt, cx, KC).then_inc(gT_ps, 1)
                if p.runs(C1):
                    pe.wait_ge(ha_in, p.prev(C1, 16, 16))
                    pe.wait_ge(haT_sb, p.prev(C1))
                    transposes(pWt, xa, KC).then_inc(haT_ps, 1)
                if p.runs(C2):
                    pe.wait_ge(gT_sb, p.now(C2))
                    pe.wait_ge(s3_ok, p.prev(C2))
                    for r in range(2):
                        e = pe.value_load(expert_i[0:1, one(p.unit(C2) * 2 + r)], min_val=0, max_val=EXP - 1)
                        for k in range(KC):
                            mm = nc.tensor.matmul(pY[:, 0, r * DM:(r + 1) * DM], cxT[:, k, r, :],
                                                  w2[:, bass.ds(e, 1), k, :], start=(k == 0), stop=(k == KC - 1))
                    mm.then_inc(f2_ps, 1)
                if p.runs(C1):
                    pe.wait_ge(haT_sb, p.now(C1))
                    pe.wait_ge(f1_ok, p.prev(C1))
                    for r in range(2):
                        e = pe.value_load(expert_i[0:1, one(p.unit(C1) * 2 + r)], min_val=0, max_val=EXP - 1)
                        for k in range(KC):
                            mm = nc.tensor.matmul(pX[:, 0, r * DM:(r + 1) * DM], xnT[:, k, r, :],
                                                  w1[:, bass.ds(e, 1), k, :], start=(k == 0), stop=(k == KC - 1))
                    mm.then_inc(f1_ps, 1)
            MLP.run(pe, mlp)

        @block.scalar
        def _(act):
            copy = nc.scalar.copy
            t4 = "p (c r t) -> p c r t"
            act.wait_ge(small_in, 13 * 16)
            nc.scalar.activation(neg_a[:], a_log[:], ACT.Exp).then_inc(alog_e, 1)

            def decays(p, r):
                act.wait_ge(arg_ps, p.prev(A2, 2, r + 1))
                act.wait_ge(intra_ps, p.prev(A2, 2))
                for hd in range(NH):
                    ins = nc.scalar.activation(em[:, r, hd, :], pY[:, hd // 4, (hd % 4) * P:(hd % 4 + 1) * P], ACT.Exp,
                                               bias=ncum[:, r, hd:hd + 1])
                return ins

            def body(p):
                if p.runs(B4):
                    act.wait_ge(hT_ps, p.now(B4))
                    act.wait_ge(lg_ps, p.prev(B4))
                    copy(hT[:], pW[:, :].rearrange(t4, c=2, r=2)).then_inc(hT_sb, 1)
                if p.runs(B3):
                    act.wait_ge(cxT_ps, p.now(B3))
                    act.wait_ge(ao_ps, p.prev(B3))
                    copy(cxT[:], pY[:, 0, :].rearrange(t4, c=2, r=2)).then_inc(cxT_sb, 1)
                if p.runs(B1):
                    act.wait_ge(xbT_ps, p.now(B1))
                    act.wait_ge(qkv_ps, p.prev(B1, 2))
                    copy(xbT[:], pV[:, :].rearrange(t4, c=2, r=2)).then_inc(xbT_sb, 1)
                if p.runs(A1):
                    act.wait_ge(xnT_ps, p.now(A1))
                    act.wait_ge(xs_ps, p.prev(A1))
                    act.wait_ge(z_ps, p.now(A2))
                    copy(xnT[:], pY[:, 1, :].rearrange(t4, c=2, r=2)).then_inc(xnT_sb, 1)
                if p.runs(A2):
                    act.wait_ge(z_ps, p.now(A2))
                    act.wait_ge(y_ok, p.prev(A2))
                    nc.scalar.activation(sz[:], pX[:], ACT.Tanh).then_inc(zt_ok, 1)
                if p.runs(A3):
                    act.wait_ge(yT_ps, p.now(A3))
                    act.wait_ge(out_ps, p.prev(A3))
                    copy(yT[:], yT_v).then_inc(yT_sb, 1)
                if p.runs(A2):
                    act.wait_ge(decay, p.now(A2, DECAY))
                    act.wait_ge(wdtx_ok, p.prev(A2))
                    act.wait_ge(hdec, p.prev(A2, 2))
                    act.wait_ge(yin_ok, p.prev(A2, 2))
                    nc.scalar.activation(ex[:], sm[:], ACT.Exp).then_inc(ex_ok, 1)
                    decays(p, 0).then_inc(exp_ok, 1)
                if p.runs(B2):
                    act.wait_ge(scm_ok, p.now(B2))
                    act.wait_ge(pv_ok, p.prev(B2, 2))
                    nc.scalar.activation(pr[:], sc[:], ACT.Exp).then_inc(e_ok, 1)
                if p.runs(A1):
                    act.wait_ge(cbT_ps, p.now(A1))
                    act.wait_ge(shift_ok, p.now(A2))
                    copy(cb_new[:, 0:2, :, :], pW[:, :].rearrange(t4, c=2, r=2)).then_inc(cbT_sb, 1)
                if p.runs(A2):
                    act.wait_ge(xh_ps, p.now(A2))
                    act.wait_ge(yd_ok, p.prev(A2))
                    copy(xh[:], pX[:]).then_inc(xh_sb, 1)
                if p.runs(A1):
                    act.wait_ge(tok_ps, p.now(A1))
                    copy(cb_new[:, 2, :, :], pZ[:, 0, 0:2 * WTOK].rearrange("p (r w) -> p r w", r=2)[:, :, 0:NST]).then_inc(btok_sb, 1)
                if p.runs(A2):
                    decays(p, 1).then_inc(exp_ok, 1)
                if p.runs(A1):
                    act.wait_ge(xs_ps, p.now(A1))
                    act.wait_ge(conv, p.prev(A1, TAPS))
                    act.wait_ge(halo_out, p.prev(A1))
                    copy(xs[:, :, :, TAPS - 1:], xT_v).then_inc(xs_sb, 1)
                    act.wait_ge(soft, p.prev(A1, SOFT, 1))
                    nc.scalar.activation(dt_e[:], dt_in[:], ACT.Exp).then_inc(soft, 1)
                    act.wait_ge(conv, p.now(A1, TAPS))
                    act.wait_ge(xh_ps, p.now(A2))
                    nc.scalar.activation(xhT[:], cv[:], ACT.Tanh).then_inc(cth_ok, 1)
                    act.wait_ge(soft, p.prev(A1, SOFT, 2))
                    act.wait_ge(dtx_ok, p.now(A2))
                    act.wait_ge(da_ok, p.now(A2))
                    nc.scalar.activation(dt[:], dt_e[:], ACT.Ln, bias=1.0).then_inc(soft, 1)

            MAIN.run(act, body)

            act.wait_ge(r_exp, 1)
            nc.scalar.activation(part(0), part(0), ACT.Exp).then_inc(r_exp, 1)

            def mlp(p):
                if p.runs(C2):
                    act.wait_ge(gT_ps, p.now(C2))
                    act.wait_ge(f2_ps, p.prev(C2))
                    copy(cxT[:], pV[:, :].rearrange(t4, c=2, r=2)).then_inc(gT_sb, 1)
                if p.runs(C1):
                    act.wait_ge(haT_ps, p.now(C1))
                    act.wait_ge(f1_ps, p.prev(C1))
                    copy(xnT[:], pW[:, :].rearrange(t4, c=2, r=2)).then_inc(haT_sb, 1)
                    act.wait_ge(f1_ok, p.now(C1))
                    act.wait_ge(gT_ps, p.now(C2))
                    nc.scalar.activation(cx[:], x0[:], ACT.Gelu).then_inc(g_ok, 1)
            MLP.run(act, mlp)

        @block.vector
        def _(dve):
            v = nc.vector

            def norm_stats(sem, base, x, st, mv, var, inputs):
                for r in range(2):
                    ins = v.bn_stats(st[:, r, :], x[:, r, :])
                ins.then_inc(sem, 1)
                waits_apart(dve, (sem, base(1)))
                for r in range(2):
                    ins = v.bn_aggr(mv[:, r, :], st[:, r, :])
                ins.then_inc(sem, 1)
                dve.wait_ge(sem, base(2))
                v.tensor_scalar(var[:, 0:2], mv[:, :, 1], EPS, None, ALU.add).then_inc(sem, 1)

            def norm_rows(out, x, mean, factor):
                for r in range(2):
                    ins = v.tensor_scalar(out[:, r, :], x[:, r, :], mean(r), factor(r), ALU.subtract, ALU.mult)
                return ins

            dve.wait_ge(small_in, 13 * 16)
            dve.wait_ge(w_in_in, 16)
            for k in range(KC):
                v.tensor_scalar(w_in[:, k, 0:DI], w_in[:, k, 0:DI], norm_w[:, k:k + 1], 0.5, ALU.mult, ALU.mult)
                v.tensor_scalar(w_in[:, k, DI:PROJ], w_in[:, k, DI:PROJ], norm_w[:, k:k + 1], None, ALU.mult)
            v.tensor_scalar(conv_w[:], conv_w[:], 0.5, None, ALU.mult).then_inc(route, 1)
            v.tensor_scalar(conv_b[:], conv_b[:], 0.5, None, ALU.mult).then_inc(route, 1)
            dve.wait_ge(alog_e, 1)
            v.tensor_scalar(neg_a[:], neg_a[:], -1.0, None, ALU.mult).then_inc(route, 1)
            dve.wait_ge(w_in_2, 64)
            for k in range(KC):
                v.tensor_scalar(w_qkv[:, k, 0:DM], w_qkv[:, k, 0:DM], AD ** -0.5, None, ALU.mult)
            v.tensor_scalar(qkv_b[:, 0:DM], qkv_b[:, 0:DM], AD ** -0.5, None, ALU.mult).then_inc(prep, 1)
            dve.wait_ge(prep, 1)
            dve.wait_ge(route, 3)
            dve.wait_ge(consts, 1)

            def body(p):
                if p.runs(A2):
                    dve.wait_ge(soft, p.now(A2, SOFT))
                    dve.wait_ge(arg_ps, p.prev(A2, 2))
                    v.tensor_tensor(da[:], dt[:], neg_a[:].unsqueeze(1).to_broadcast([P, 2, NH]), ALU.mult).then_inc(da_ok, 1)
                if p.runs(B1):
                    dve.wait_ge(x1_ok, p.now(B1))
                    dve.wait_ge(xb_ok, p.prev(B1))
                    norm_stats(ln_b, lambda n: p.prev(B1, LN, n), x1, st_b, mv_b, var_b, None)
                if p.runs(A3):
                    dve.wait_ge(xr_in, p.prev(A3, 16, 16))
                    dve.wait_ge(s1_ok, p.prev(A3))
                    dve.wait_ge(mr_ok, p.now(A3))
                    norm_rows(x0, xr, lambda r: mr[:, 0, r:r + 1], lambda r: mr[:, 1, r:r + 1]).then_inc(x0_ok, 1)
                if p.runs(A2):
                    dve.wait_ge(ln_a, p.now(A2, LN))
                    dve.wait_ge(x0_ok, p.now(A3))
                    v.tensor_copy(mr[:, 0, :], mv_a[:, :, 0])
                    v.tensor_copy(mr[:, 1, :], rs_a[:, 0, :]).then_inc(mr_ok, 1)
                if p.runs(A1):
                    dve.wait_ge(xa_in, p.prev(A1, 16, 16))
                    dve.wait_ge(mr_ok, p.now(A2))
                    dve.wait_ge(xn_ok, p.prev(A1))
                    for r in range(2):
                        ins = v.bn_stats(st_a[:, r, :], xa[:, r, :])
                    ins.then_inc(ln_a, 1)
                    waits_apart(dve, (ln_a, p.prev(A1, LN, 1)))
                    for r in range(2):
                        ins = v.bn_aggr(mv_a[:, r, :], st_a[:, r, :])
                    ins.then_inc(ln_a, 1)
                    dve.wait_ge(ln_a, p.prev(A1, LN, 2))
                    v.tensor_scalar(var_a[:, 0, :], mv_a[:, :, 1], EPS, None, ALU.add)
                    v.tensor_scalar(var_a[:, 1, :], mv_a[:, :, 1], 1.0 + RMS_EPS, EPS * RMS_EPS, ALU.mult, ALU.add).then_inc(ln_a, 1)

                def scores(r):
                    dve.wait_ge(qkv_sb, p.prev(B1, 2))
                    dve.wait_ge(cx_ok, p.prev(B2, 2))
                    v.tensor_tensor(prod[:, r, :, :], qkv[:, group_of(p.unit(B2)), DM:2 * DM],
                                    qkv[:, slot_of(p.unit(B2), r), 0:DM].to_broadcast([P, ROWS, DM]), ALU.mult).then_inc(qk_ok, 1)
                    dve.wait_ge(qk_ok, p.prev(B2, 2, r + 1))
                    dve.wait_ge(e_ok, p.prev(B2))
                    v.tensor_reduce(sc[:, r, :, :].rearrange("p s h -> p (s h)"), prod[:, r, :, :].rearrange("p s (h d) -> p (s h) d", d=AD),
                                    AX.X, ALU.add).then_inc(sc_ok, 1)

                if p.runs(B2):
                    scores(0)
                if p.runs(B1):
                    dve.wait_ge(ln_b, p.now(B1, LN))
                    dve.wait_ge(xbT_ps, p.prev(B1))
                    norm_rows(xb, x1, lambda r: mv_b[:, r, 0:1], lambda r: rs_b[:, r:r + 1]).then_inc(xb_ok, 1)
                    v.tensor_copy(kept[:, one(p.unit(B1)), 0, :].rearrange("p o r -> p (o r)"), mv_b[:, :, 0])
                    v.tensor_copy(kept[:, one(p.unit(B1)), 1, :].rearrange("p o r -> p (o r)"), rs_b[:]).then_inc(kept_ok, 1)
                if p.runs(A1):
                    dve.wait_ge(ln_a, p.now(A1, LN))
                    dve.wait_ge(xnT_ps, p.prev(A1))
                    norm_rows(xn, xa, lambda r: mv_a[:, r, 0:1], lambda r: rs_a[:, 1, r:r + 1]).then_inc(xn_ok, 1)
                if p.runs(B2):
                    scores(1)
                    dve.wait_ge(sc_ok, p.now(B2, 2))
                    v.tensor_reduce(mx[:], sc[:].rearrange("p r s h -> p r h s"), AX.X, ALU.max).then_inc(mx_ok, 1)
                    dve.wait_ge(mx_ok, p.now(B2))
                    v.tensor_tensor(sc[:], sc[:], mx[:].unsqueeze(2).to_broadcast([P, 2, ROWS, AH]), ALU.subtract).then_inc(scm_ok, 1)
                if p.runs(A2):
                    dve.wait_ge(zt_ok, p.now(A2))
                    v.scalar_tensor_tensor(sz[:], sz[:], 1.0, pX[:], ALU.add, ALU.mult).then_inc(sz_ok, 1)
                    dve.wait_ge(cum_ps, p.now(A2))
                    dve.wait_ge(ex_ok, p.prev(A2))
                    dve.wait_ge(exp_ok, p.prev(A2, 2))
                    v.tensor_copy(sm[:, 1:3, :, :].rearrange("p a r h -> p (a r h)"), pV[:, 256:288]).then_inc(decay, 1)
                    dve.wait_ge(decay, p.prev(A2, DECAY, 1))
                    v.tensor_tensor(sm[:, 0, :, :], sm[:, 2, :, :], sm[:, 1, :, :], ALU.subtract)
                    v.tensor_scalar(ncum[:], sm[:, 1, :, :], -1.0, None, ALU.mult).then_inc(decay, 1)
                if p.runs(B3):
                    dve.wait_ge(kept_ok, p.now(B3))
                    dve.wait_ge(x0b_ok, p.prev(B3))
                    v.tensor_copy(mrb[:], kept[:, one(p.unit(B3)), :, :].rearrange("p o a r -> p (o a) r")).then_inc(mrb_ok, 1)
                if p.runs(A3):
                    dve.wait_ge(out_ps, p.now(A3))
                    dve.wait_ge(s1n_ok, p.prev(A3))
                    dve.wait_ge(x0_ok, p.now(A3))
                    v.tensor_tensor(s1[:].rearrange("p r d -> p (r d)"), pZ[:, 0, :], x0[:].rearrange("p r d -> p (r d)"), ALU.add).then_inc(s1_ok, 1)
                    dve.wait_ge(s1_ok, p.now(A3))
                    norm_stats(ln_c, lambda n: p.prev(A3, LN, n), s1, st_c, mv_c, var_c, None)
                if p.runs(B3):
                    dve.wait_ge(mrb_ok, p.now(B3))
                    dve.wait_ge(x1r_in, p.prev(B3, 16, 16))
                    dve.wait_ge(s2_ok, p.prev(B3))
                    norm_rows(x0b, x1r, lambda r: mrb[:, 0, r:r + 1], lambda r: mrb[:, 1, r:r + 1]).then_inc(x0b_ok, 1)

                def mask(r):
                    dve.wait_ge(exp_ok, p.prev(A2, 2, r + 1))
                    v.tensor_tensor(em[:, r, :, :], em[:, r, :, :], pV[:, r * P:(r + 1) * P].unsqueeze(1).to_broadcast([P, NH, P]),
                                    ALU.mult).then_inc(m_ok, 1)

                if p.runs(A2):
                    mask(0)
                if p.runs(B2):
                    dve.wait_ge(e_ok, p.now(B2))
                    v.tensor_reduce(den[:], pr[:].rearrange("p r s h -> p r h s"), AX.X, ALU.add).then_inc(den_ok, 1)
                    dve.wait_ge(den_ok, p.now(B2))
                    v.reciprocal(rden[:], den[:]).then_inc(rden_ok, 1)
                    dve.wait_ge(rden_ok, p.now(B2))
                    v.tensor_tensor(pr[:], pr[:], rden[:].unsqueeze(2).to_broadcast([P, 2, ROWS, AH]), ALU.mult).then_inc(pr_ok, 1)
                if p.runs(A3):
                    dve.wait_ge(ln_c, p.now(A3, LN))
                    norm_rows(s1, s1, lambda r: mv_c[:, r, 0:1], lambda r: rs_c[:, r:r + 1]).then_inc(s1n_ok, 1)
                    dve.wait_ge(s1n_ok, p.now(A3))
                    dve.wait_ge(x1_out, p.prev(A3, 16))
                    dve.wait_ge(xb_ok, p.now(B1))
                    v.tensor_tensor(x1[:], s1[:], xr[:], ALU.add).then_inc(x1_ok, 1)
                if p.runs(B3):
                    dve.wait_ge(ao_ps, p.now(B3))
                    dve.wait_ge(x0o_ok, p.now(B3))
                    dve.wait_ge(hg_ok, p.prev(B3))
                    v.tensor_tensor(s2[:].rearrange("p r d -> p (r d)"), pZ[:, 1, :], x0b[:].rearrange("p r d -> p (r d)"), ALU.add).then_inc(s2_ok, 1)
                    dve.wait_ge(s2_ok, p.now(B3))
                    norm_stats(ln_f, lambda n: p.prev(B3, LN, n), s2, st_f, mv_f, var_f, None)
                if p.runs(B4):
                    dve.wait_ge(lg_ps, p.now(B4))
                    v.tensor_tensor(logits[:, unit_slice(p.unit(B4), 2), :], pW[:, 0:2 * EXP].rearrange("p (r e) -> p r e", r=2),
                                    r_b[:].unsqueeze(1).to_broadcast([P, 2, EXP]), ALU.add).then_inc(lg_sb, 1)
                if p.runs(A1):
                    dve.wait_ge(btok_sb, p.now(A1))
                    dve.wait_ge(soft, p.prev(A1, SOFT))
                    v.tensor_tensor(dt_in[:], pZ[:, 0, 0:2 * WTOK].rearrange("p (r w) -> p r w", r=2)[:, :, NST:WTOK],
                                    dt_bias[:].unsqueeze(1).to_broadcast([P, 2, NH]), ALU.add).then_inc(soft, 1)
                if p.runs(A2):
                    mask(1)
                if p.runs(B3):
                    dve.wait_ge(ln_f, p.now(B3, LN))
                    norm_rows(s2, s2, lambda r: mv_f[:, r, 0:1], lambda r: rs_f[:, r:r + 1]).then_inc(s2n_ok, 1)
                if p.runs(A1):
                    dve.wait_ge(xs_sb, p.now(A1))
                    dve.wait_ge(halo_in, p.now(A1))
                    dve.wait_ge(cth_ok, p.prev(A1))
                    dve.wait_ge(xhT_ok, p.prev(A1))
                    for b in range(XB):
                        ins = v.tensor_scalar(cv[:, b, :, :], xs[:, b, :, 0:P], conv_w[:, b, 0:1], conv_b[:, b:b + 1], ALU.mult, ALU.add)
                    ins.then_inc(conv, 1)
                    for k in range(1, TAPS):
                        dve.wait_ge(conv, p.prev(A1, TAPS, k))
                        for b in range(XB):
                            ins = v.scalar_tensor_tensor(cv[:, b, :, :], xs[:, b, :, k:k + P], conv_w[:, b, k:k + 1], cv[:, b, :, :],
                                                         ALU.mult, ALU.add)
                        ins.then_inc(conv, 1)

                def inner(r, bank):
                    dve.wait_ge(inter_ps, p.prev(A2, 2, r + 1))
                    dve.wait_ge(ex_ok, p.now(A2))
                    dve.wait_ge(yT_ps, p.now(A3))
                    yr = y[:, r, :].rearrange("p (h d) -> p h d", h=NH)
                    v.tensor_tensor(yr, bank.rearrange("p (h d) -> p h d", h=NH), ex[:, 1, r, :].unsqueeze(2).to_broadcast([P, NH, HD]),
                                    ALU.mult).then_inc(yin_ok, 1)
                    dve.wait_ge(intra_ps, p.prev(A2, 2, r + 1))
                    dve.wait_ge(yin_ok, p.prev(A2, 2, r + 1))
                    v.tensor_tensor(y[:, r, :], pZ[:, 0, :], y[:, r, :], ALU.add).then_inc(ysum_ok, 1)

                def carry(r):
                    dve.wait_ge(st_ps, p.prev(A2, 2, r + 1))
                    dve.wait_ge(hdec, p.prev(A2, 2, r + 1))
                    st = state[:, row_of(p.unit(A2), r), :].rearrange("p o n -> p (o n)")
                    v.tensor_tensor(st, pZ[:, 1, :], st, ALU.add).then_inc(h_ok, 1)

                if p.runs(A2):
                    inner(0, pW[:, :])
                    carry(0)
                if p.runs(B1):
                    for r in range(1):
                        dve.wait_ge(qkv_ps, p.prev(B1, 2, 1))
                        dve.wait_ge(pv_ok, p.prev(B2, 2))
                        v.tensor_tensor(qkv[:, slot_of(p.unit(B1), 0), :].rearrange("p o n -> p (o n)"),
                                        pY[:, :, :].rearrange("p a n -> p (a n)")[:, 0:3 * DM], qkv_b[:], ALU.add).then_inc(qkv_sb, 1)
                if p.runs(A1):
                    dve.wait_ge(cth_ok, p.now(A1))
                    v.scalar_tensor_tensor(xhT[:], xhT[:], 1.0, cv[:], ALU.add, ALU.mult).then_inc(xhT_ok, 1)
                if p.runs(A2):
                    inner(1, pV[:, :])
                    carry(1)
                if p.runs(B1):
                    dve.wait_ge(qkv_ps, p.now(B1, 2))
                    v.tensor_tensor(qkv[:, slot_of(p.unit(B1), 1), :].rearrange("p o n -> p (o n)"),
                                    pX[:, :, :].rearrange("p a n -> p (a n)")[:, 0:3 * DM], qkv_b[:], ALU.add).then_inc(qkv_sb, 1)
                if p.runs(B2):
                    for r in range(2):
                        dve.wait_ge(pv_ok, p.prev(B2, 2, r + 1))
                        dve.wait_ge(cxT_ps, p.now(B3))
                        v.tensor_reduce(cx[:, r, :], prod[:, r, :, :].rearrange("p s c -> p c s"), AX.X, ALU.add).then_inc(cx_ok, 1)

            MAIN.run(dve, body)

            count = [3]

            def then(ins):
                count[0] += 1
                ins.then_inc(route, 1)
                dve.wait_ge(route, count[0])

            TE = TILES * EXP
            te = "p (t e) -> p t e"
            lg = logits[:]
            prob, eq, cand, one1, oneh = part(0), part(1), part(2), part(3), part(5)
            key_b = key[:].unsqueeze(1).to_broadcast([P, TILES, EXP])

            def by_tile(row):
                return row.unsqueeze(2).to_broadcast([P, TILES, EXP])

            dve.wait_ge(lg_sb, UNITS)
            dve.wait_ge(cx_ok, 2 * UNITS)
            P3, EQ3, C3, O3, H3 = (q.rearrange(te, e=EXP) for q in (prob, eq, cand, one1, oneh))
            then(v.tensor_reduce(rt[:, 0, :], lg, AX.X, ALU.max))
            v.tensor_tensor(P3, lg, by_tile(rt[:, 0, :]), ALU.subtract).then_inc(r_exp, 1)
            dve.wait_ge(r_exp, 2)
            then(v.tensor_reduce(rt[:, 0, :], P3, AX.X, ALU.add))
            then(v.reciprocal(rt[:, 1, :], rt[:, 0, :]))
            then(v.tensor_tensor(P3, P3, by_tile(rt[:, 1, :]), ALU.mult))
            then(v.tensor_reduce(rt[:, 2, :], P3, AX.X, ALU.max))
            then(v.tensor_tensor(EQ3, P3, by_tile(rt[:, 2, :]), ALU.is_equal))
            then(v.tensor_tensor(C3, EQ3, key_b, ALU.mult))
            then(v.tensor_reduce(rt[:, 3, :], C3, AX.X, ALU.max))
            then(v.tensor_tensor(O3, key_b, by_tile(rt[:, 3, :]), ALU.is_equal))
            then(v.scalar_tensor_tensor(prob, one1, -2.0, prob, ALU.mult, ALU.add))
            then(v.tensor_reduce(rt[:, 2, :], P3, AX.X, ALU.max))
            then(v.tensor_tensor(EQ3, P3, by_tile(rt[:, 2, :]), ALU.is_equal))
            then(v.tensor_tensor(C3, EQ3, key_b, ALU.mult))
            then(v.tensor_reduce(rt[:, 4, :], C3, AX.X, ALU.max))
            then(v.tensor_tensor(rt[:, 5, :], rt[:, 3, :], rt[:, 4, :], ALU.min))
            v.tensor_tensor(H3, key_b, by_tile(rt[:, 5, :]), ALU.is_equal).then_inc(onehot_ok, 1)
            dve.wait_ge(onehot_ok, 1)
            dve.wait_ge(r_ps, 1)
            tot, incl, rank = part(1), part(2), part(3)
            then(v.tensor_copy(tot, pX[:, 1, :]))
            incl3 = incl.rearrange("p (e t) -> p e t", e=EXP)
            for e in range(EXP):
                ins = v.tensor_tensor_scan(incl3[:, e, :], tot.rearrange(te, e=EXP)[:, :, e], zero[:, 0:TILES], 0.0, ALU.add, ALU.add)
            then(ins)
            then(v.tensor_tensor(rank.rearrange(te, e=EXP), incl.rearrange("p (e t) -> p t e", e=EXP), tot.rearrange(te, e=EXP), ALU.subtract))
            then(v.tensor_tensor(rank, pX[:, 0, :], rank, ALU.add))
            then(v.tensor_copy(re[:, 0, :], incl3[:, :, TILES - 1]))
            cmp3 = part(4).rearrange("p (e t) -> p e t", e=EXP)
            then(v.tensor_tensor(cmp3, re[:, 0, :].unsqueeze(2).to_broadcast([P, EXP, TILES]),
                                 count_f[:, 0:TILES].unsqueeze(1).to_broadcast([P, EXP, TILES]), ALU.is_gt))
            then(v.tensor_reduce(re[:, 1, :], cmp3, AX.X, ALU.add))
            then(v.tensor_tensor_scan(re[:, 2, :], re[:, 1, :], zero[:, 0:EXP], 0.0, ALU.add, ALU.add))
            then(v.tensor_tensor(re[:, 3, :], re[:, 2, :], re[:, 1, :], ALU.subtract))
            then(v.tensor_scalar(re[:, 3, :], re[:, 3, :], float(P), None, ALU.mult))
            then(v.tensor_tensor(rank.rearrange(te, e=EXP), rank.rearrange(te, e=EXP), re[:, 3, :].unsqueeze(1).to_broadcast([P, TILES, EXP]), ALU.add))
            then(v.tensor_tensor(rank, rank, oneh, ALU.mult))
            then(v.tensor_reduce(rt[:, 0, :], rank.rearrange(te, e=EXP), AX.X, ALU.add))
            then(v.tensor_copy(dest_i[:], rt[:, 0, :]))
            then(v.tensor_scalar(re[:, 2, :], re[:, 2, :], float(P), None, ALU.mult))
            cmps = part(6, SORTED * EXP).rearrange(te, e=EXP)
            then(v.tensor_tensor(cmps, count_f[:].unsqueeze(2).to_broadcast([P, SORTED, EXP]),
                                 re[:, 2, :].unsqueeze(1).to_broadcast([P, SORTED, EXP]), ALU.is_ge))
            expert_f = part(4, SORTED)
            then(v.tensor_reduce(expert_f, cmps, AX.X, ALU.add))
            then(v.tensor_scalar(expert_f, expert_f, float(EXP - 1), None, ALU.min))
            v.tensor_copy(expert_i[:], expert_f).then_inc(routed, 1)
            dve.wait_ge(routed, 1)
            dve.wait_ge(exp_in, 64)

            def mlp(p):
                if p.runs(C2):
                    dve.wait_ge(h2_in, p.prev(C2, 16, 16))
                    dve.wait_ge(s3_ok, p.prev(C2))
                    for r in range(2):
                        e = dve.value_load(expert_i[0:1, one(p.unit(C2) * 2 + r)], min_val=0, max_val=EXP - 1)
                        ins = v.tensor_tensor(s1[:, r, :], xr[:, r, :], b2[:, bass.ds(e, 1), :].rearrange("p o n -> p (o n)"), ALU.add)
                    ins.then_inc(hb2_ok, 1)
                if p.runs(C1):
                    dve.wait_ge(f1_ps, p.now(C1))
                    dve.wait_ge(g_ok, p.prev(C1))
                    for r in range(2):
                        e = dve.value_load(expert_i[0:1, one(p.unit(C1) * 2 + r)], min_val=0, max_val=EXP - 1)
                        ins = v.tensor_tensor(x0[:, r, :], pX[:, 0, r * DM:(r + 1) * DM], b1[:, bass.ds(e, 1), :].rearrange("p o n -> p (o n)"), ALU.add)
                    ins.then_inc(f1_ok, 1)
                if p.runs(C2):
                    dve.wait_ge(f2_ps, p.now(C2))
                    dve.wait_ge(hb2_ok, p.now(C2))
                    dve.wait_ge(l2g_ok, p.prev(C2))
                    v.tensor_tensor(s2[:].rearrange("p r d -> p (r d)"), pY[:, 0, :], s1[:].rearrange("p r d -> p (r d)"), ALU.add).then_inc(s3_ok, 1)
                    dve.wait_ge(s3_ok, p.now(C2))
                    norm_stats(ln_g, lambda n: p.prev(C2, LN, n), s2, st_c, mv_c, var_c, None)
                    dve.wait_ge(ln_g, p.now(C2, LN))
                    norm_rows(s2, s2, lambda r: mv_c[:, r, 0:1], lambda r: rs_c[:, r:r + 1]).then_inc(s3n_ok, 1)
                    dve.wait_ge(l2b_ok, p.now(C2))
                    norm_stats(ln_h, lambda n: p.prev(C2, LN, n), h, st_f, mv_f, var_f, None)
                    dve.wait_ge(ln_h, p.now(C2, LN))
                    dve.wait_ge(ys_out, p.prev(C2, 16))
                    norm_rows(x1, h, lambda r: mv_f[:, r, 0:1], lambda r: rs_f[:, r:r + 1]).then_inc(y_fin, 1)
            MLP.run(dve, mlp)

            def finish(i):
                for j in range(2):
                    dve.wait_ge(x1f_in[j], i * 16 + 16)
                    dve.wait_ge(gathered[j], i * 32 + 32)
                    if not isinstance(i, int):
                        dve.wait_ge(fin_out[j], i * 16)
                    v.tensor_tensor((s1, s2)[j][:], (xn, xb)[j][:], (x0, x0b)[j][:], ALU.add).then_inc(fin_ok, 1)

            finish(0)
            with dve.Fori(1, UNITS // 2) as i:
                finish(i)

        @block.gpsimd
        def _(pool):
            g = nc.gpsimd
            steps = [0]

            def const(ins):
                steps[0] += 1
                ins.then_inc(zeroed, 1)
                pool.wait_ge(zeroed, steps[0])

            g.memset(state[:], 0.0)
            g.memset(halo[:], 0.0)
            g.memset(half[:], -0.5)
            const(g.memset(zero[:], 0.0))
            pool.dma_start(sorted_t, zero[:].unsqueeze(1).to_broadcast([P, SORTED, DM])).then_inc(sorted_zero, 16)
            for e in range(EXP):
                g.memset(key[:, e:e + 1], float(EXP - e))
            g.memset(ones[:], 1.0)
            g.memset(ident[:], 0.0)
            g.memset(ident_h[:], 0.0)
            g.memset(upto[:], 1.0)
            g.memset(before[:], 1.0)
            g.memset(future[:], 0.0)
            const(g.iota(count_i[:], pattern=[[P, SORTED]], base=0, channel_multiplier=0))
            for t in (ident, ident_h):
                g.affine_select(out=t[:], in_=t[:], compare_op=ALU.not_equal, fill=1.0, base=0, pattern=[[-1, P]], channel_multiplier=1)
            g.affine_select(out=upto[:], in_=upto[:], compare_op=ALU.is_ge, fill=0.0, base=0, pattern=[[1, P]], channel_multiplier=-1)
            g.affine_select(out=before[:], in_=before[:], compare_op=ALU.is_ge, fill=0.0, base=-1, pattern=[[1, P]], channel_multiplier=-1)
            g.affine_select(out=future[:], in_=future[:], compare_op=ALU.is_ge, fill=NEG, base=0, pattern=[[1, P]], channel_multiplier=-1)
            g.tensor_copy(count_f[:], count_i[:]).then_inc(consts, 1)
            pool.wait_ge(consts, 1)

            def power(sem, count, out, in_):
                pool.wait_ge(sem, count)
                g.tensor_tensor(out, in_, half[:, 0:2] if len(in_.shape) == 2 else half[:].rearrange("p (a r) -> p a r", a=2),
                                ALU.pow).then_inc(sem, 1)

            def body(p):
                if p.runs(A2):
                    waits_apart(pool, (cbT_sb, p.now(A2)), (btok_sb, p.now(A2)), (inter_ps, p.prev(A2, 2)), (st_ps, p.prev(A2, 2)))
                    g.tensor_copy(cb[:], cb_new[:]).then_inc(shift_ok, 1)
                if p.runs(B1):
                    power(ln_b, p.prev(B1, LN, 3), rs_b[:], var_b[:])
                if p.runs(A1):
                    power(ln_a, p.prev(A1, LN, 3), rs_a[:], var_a[:])
                    waits_apart(pool, (conv, p.prev(A1, TAPS)), (halo_out, p.prev(A1)))
                    g.tensor_copy(xs[:, :, :, 0:TAPS - 1].rearrange("p b r k -> p r b k"), halo[:, rows_of(p.unit(A1)), :, :]).then_inc(halo_in, 1)
                if p.runs(A3):
                    power(ln_c, p.prev(A3, LN, 3), rs_c[:], var_c[:])
                if p.runs(B3):
                    pool.wait_ge(x0b_ok, p.now(B3))
                    g.tensor_tensor(x0b[:], x0b[:], o_b[:].unsqueeze(1).to_broadcast([P, 2, DM]), ALU.add).then_inc(x0o_ok, 1)
                by_head = "p r (h d) -> p r h d"
                if p.runs(A2):
                    pool.wait_ge(xh_sb, p.now(A2))
                    pool.wait_ge(intra_ps, p.prev(A2, 2))
                    for r in range(2):
                        ins = g.tensor_tensor(dtx[:, r, :].rearrange("p (h d) -> p h d", h=NH), xh[:, r, :].rearrange("p (h d) -> p h d", h=NH),
                                              dt[:, r, :].unsqueeze(2).to_broadcast([P, NH, HD]), ALU.mult)
                    ins.then_inc(dtx_ok, 1)
                    pool.wait_ge(dtx_ok, p.now(A2))
                    pool.wait_ge(ex_ok, p.now(A2))
                    for r in range(2):
                        ins = g.tensor_tensor(wdtx[:, r, :].rearrange("p (h d) -> p h d", h=NH), dtx[:, r, :].rearrange("p (h d) -> p h d", h=NH),
                                              ex[:, 0, r, :].unsqueeze(2).to_broadcast([P, NH, HD]), ALU.mult)
                    ins.then_inc(wdtx_ok, 1)
                    for r in range(2):
                        ins = g.tensor_tensor(xh[:, r, :].rearrange("p (h d) -> p h d", h=NH), xh[:, r, :].rearrange("p (h d) -> p h d", h=NH),
                                              d_skip[:].unsqueeze(2).to_broadcast([P, NH, HD]), ALU.mult)
                    ins.then_inc(dx_ok, 1)
                if p.runs(B3):
                    power(ln_f, p.prev(B3, LN, 3), rs_f[:], var_f[:])
                if p.runs(A1):
                    waits_apart(pool, (xs_sb, p.now(A1)), (halo_in, p.now(A1)))
                    g.tensor_copy(halo[:, rows_of(p.unit(A1)), :, :], xs[:, :, :, P:P + TAPS - 1].rearrange("p b r k -> p r b k")).then_inc(halo_out, 1)
                if p.runs(B3):
                    pool.wait_ge(s2n_ok, p.now(B3))
                    pool.wait_ge(hT_ps, p.now(B4))
                    pool.wait_ge(h_out, p.prev(B3, 16))
                    g.tensor_tensor(h[:], s2[:], ln1_g[:].unsqueeze(1).to_broadcast([P, 2, DM]), ALU.mult).then_inc(hg_ok, 1)
                    pool.wait_ge(hg_ok, p.now(B3))
                    g.tensor_tensor(h[:], h[:], ln1_b[:].unsqueeze(1).to_broadcast([P, 2, DM]), ALU.add).then_inc(hb_ok, 1)
                if p.runs(A2):
                    for r in range(2):
                        pool.wait_ge(inter_ps, p.prev(A2, 2, r + 1))
                        st = state[:, row_of(p.unit(A2), r), :].rearrange("p o (h d) -> p (o h) d", h=NH)
                        g.tensor_tensor(st, st, ex[:, 2, r, :].unsqueeze(2).to_broadcast([P, NH, HD]), ALU.mult).then_inc(hdec, 1)
                if p.runs(B2):
                    pool.wait_ge(pr_ok, p.now(B2))
                    for r in range(2):
                        g.tensor_tensor(prod[:, r, :, :].rearrange("p s (h d) -> p s h d", d=AD),
                                        qkv[:, group_of(p.unit(B2)), 2 * DM:3 * DM].rearrange("p s (h d) -> p s h d", d=AD),
                                        pr[:, r, :, :].unsqueeze(3).to_broadcast([P, ROWS, AH, AD]), ALU.mult).then_inc(pv_ok, 1)
                if p.runs(A2):
                    pool.wait_ge(ysum_ok, p.now(A2, 2))
                    pool.wait_ge(dx_ok, p.now(A2))
                    pool.wait_ge(sz_ok, p.now(A2))
                    g.tensor_tensor(y[:], y[:], xh[:], ALU.add).then_inc(yd_ok, 1)
                    pool.wait_ge(yd_ok, p.now(A2))
                    g.tensor_tensor(y[:], y[:], sz[:], ALU.mult).then_inc(y_ok, 1)

            MAIN.run(pool, body)

            pool.wait_ge(routed, 1)
            pool.wait_ge(sorted_zero, 16)
            def scatter(i):
                for j in range(2):
                    if not isinstance(i, int):
                        waits_apart(pool, (scattered[j], i * 16))
                    g.tensor_copy(idx[:, j:j + 1], dest_i[:, one(i * 2 + j)]).then_inc(idx_ok, 1)
                    waits_apart(pool, (idx_ok, i * 2 + j + 1), (hs_in[j], i * 16 + 16))
                    g.indirect_dma_start(a["sorted_d"], bass.IndirectOffsetOnAxis(idx[:, j:j + 1], 0), x1r[:, j, :], None).then_inc(scattered[j], 16)

            scatter(0)
            with pool.Fori(1, TILES // 2) as i:
                scatter(i)

            def mlp(p):
                if p.runs(C2):
                    power(ln_g, p.prev(C2, LN, 3), rs_c[:], var_c[:])
                    pool.wait_ge(s3n_ok, p.now(C2))
                    pool.wait_ge(y_fin, p.prev(C2))
                    g.tensor_tensor(h[:], s2[:], ln2_g[:].unsqueeze(1).to_broadcast([P, 2, DM]), ALU.mult).then_inc(l2g_ok, 1)
                    pool.wait_ge(l2g_ok, p.now(C2))
                    g.tensor_tensor(h[:], h[:], ln2_b[:].unsqueeze(1).to_broadcast([P, 2, DM]), ALU.add).then_inc(l2b_ok, 1)
                    power(ln_h, p.prev(C2, LN, 3), rs_f[:], var_f[:])
            MLP.run(pool, mlp)

            pool.wait_ge(ys_out, 16 * (SORTED // 2))
            def gather(i):
                for j in range(2):
                    if not isinstance(i, int):
                        waits_apart(pool, (gathered[j], i * 32))
                    for r in range(2):
                        g.tensor_copy(idx[:, 2 * j + r:2 * j + r + 1], dest_i[:, one(i * 4 + 2 * j + r)]).then_inc(idx2_ok, 1)
                    free = [] if isinstance(i, int) else [(fin_ok, i * 2 + j)]
                    waits_apart(pool, (idx2_ok, i * 4 + 2 * j + 2), *free)
                    for r in range(2):
                        g.indirect_dma_start((x0, x0b)[j][:, r, :], None, a["ys_d"],
                                             bass.IndirectOffsetOnAxis(idx[:, 2 * j + r:2 * j + r + 1], 0)).then_inc(gathered[j], 16)

            gather(0)
            with pool.Fori(1, UNITS // 2) as i:
                gather(i)


def kernel(**inputs):
    import numpy as np
    import concourse.bacc as bacc
    from concourse.bass_utils import run_bass_kernel_spmd

    g = {k.replace("L0_attn_", "a_").replace("L0_ffn_", "f_"): np.asarray(v) for k, v in inputs.items()}

    def blocks(m):
        m = m.reshape(m.shape[:-2] + (m.shape[-2] // P, P, m.shape[-1]))
        return np.ascontiguousarray(np.moveaxis(m, -2, 0))

    wt = g["a_in_proj_w"].T
    state_b, state_c = wt[:, 2 * DI:2 * DI + NST], wt[:, 2 * DI + NST:2 * DI + 2 * NST]
    arrays = {
        "x": g["a_x"],
        "w_in": blocks(np.concatenate([wt[:, :2 * DI], state_c, state_b, wt[:, 2 * DI + 2 * NST:]], axis=1)),
        "w_out": blocks(g["a_out_proj_w"].T),
        "w_qkv": blocks(g["f_in_proj_w"].T),
        "w_o": blocks(g["f_out_w"].T),
        "w_r": blocks(g["f_router_w"].T),
        "w1": blocks(np.swapaxes(g["f_w1"], 1, 2)),
        "w2": blocks(np.swapaxes(g["f_w2"], 1, 2)),
        "b1": g["f_b1"].reshape(-1), "b2": g["f_b2"].reshape(-1),
        "norm_w": g["a_norm_w"].reshape(KC, P).T, "conv_w": np.moveaxis(g["a_conv_w"].reshape(XB, P, TAPS), 1, 0),
        "conv_b": g["a_conv_b"].reshape(XB, P).T, "dt_bias": g["a_dt_bias"], "a_log": g["a_A_log"], "d_skip": g["a_D"],
        "qkv_b": g["f_in_proj_b"], "o_b": g["f_out_b"], "ln1_g": g["f_ln1_g"], "ln1_b": g["f_ln1_b"], "r_b": g["f_router_b"],
        "ln2_g": g["f_ln2_g"], "ln2_b": g["f_ln2_b"],
    }
    arrays = {k: np.ascontiguousarray(v) for k, v in arrays.items()}
    nc = bacc.Bacc("TRN2", target_bir_lowering=False, num_devices=1)
    a = {k: nc.dram_tensor(f"in_{k}", v.shape, mybir.dt.from_np(v.dtype), kind="ExternalInput").ap() for k, v in arrays.items()}
    a["b1"] = a["b1"].rearrange("(e n) -> e n", e=EXP)
    a["b2"] = a["b2"].rearrange("(e n) -> e n", e=EXP)
    a["out"] = nc.dram_tensor("out", (ROWS, SEQ, DM), F32, kind="ExternalOutput").ap()
    for name, rows in (("x1_d", ROWS * SEQ), ("h_d", ROWS * SEQ), ("sorted_d", SORTED * P), ("ys_d", SORTED * P)):
        a[name] = nc.dram_tensor(name, (rows, DM), F32, kind="Internal").ap()
    program(nc, a)
    r = run_bass_kernel_spmd(nc, [{f"in_{k}": v for k, v in arrays.items()}], core_ids=[0])
    return r.results[0]["out"]
```

```python
from contextlib import ExitStack

import concourse.bass as bass
from concourse import mybir

F32 = mybir.dt.float32
BF16 = mybir.dt.bfloat16
I32 = mybir.dt.int32
ALU = mybir.AluOpType
ACT = mybir.ActivationFunctionType
AX = mybir.AxisListType

P = 128
ROWS, SEQ, DM = 8, 1024, 256
KC = DM // P
DI = 512
XB = DI // P
NST = 128
HD = 64
NH = DI // HD
TAPS = 4
CHUNKS = SEQ // P
PAIRS = ROWS // 2
UNITS = CHUNKS * PAIRS
TILES = 2 * UNITS
AH, AD = 16, DM // 16
EXP = 8
EPS = 1e-5
RMS_EPS = 1e-6
PROJ = 2 * DI + 2 * NST + NH
COL_X, COL_C, COL_B = DI, 2 * DI, 2 * DI + NST
WTOK = NST + NH
SORTED = TILES + EXP
NEG = -1.0e30


class Schedule:

    def __init__(self, lags, units):
        self.lags, self.units = lags, units
        top = max(lags)
        edges = sorted({x for lag in lags for x in (lag, lag + 1, lag + units)} | {top + 1})
        self.segments = list(zip(edges[:-1], edges[1:]))

    def run(self, eng, body):
        for lo, hi in self.segments:
            if hi - lo == 1:
                body(Pass(self, eng, lo, lo, lo))
            else:
                with eng.Fori(lo, hi) as u:
                    body(Pass(self, eng, lo, hi - 1, u))


class Pass:

    def __init__(self, schedule, eng, first, last, u):
        self.schedule, self.eng, self.first, self.last, self.u = schedule, eng, first, last, u
        self.held = {}
        self.steady = all(self.runs(lag) for lag in schedule.lags) and first > max(schedule.lags)

    def runs(self, lag):
        return lag <= self.first and self.last < lag + self.schedule.units

    def _hold(self, key, make, top):
        if isinstance(self.u, int):
            return make(self.u)
        if key not in self.held:
            self.held[key] = self.eng.snap(make(self.u), min_val=0, max_val=top)
        return self.held[key]

    def unit(self, lag):
        return self._hold(("unit", lag), lambda u: u - lag, self.schedule.units - 1)

    def now(self, lag, per=1, n=0):
        if self.last < lag:
            return 0
        if self.first >= lag + self.schedule.units:
            return per * self.schedule.units
        return self._hold((lag, per, per + n), lambda u: (u - lag + 1) * per + n, per * self.schedule.units)

    def prev(self, lag, per=1, n=0):
        if self.last < lag:
            return 0
        if self.first >= lag + self.schedule.units:
            return per * self.schedule.units
        return self._hold((lag, per, n), lambda u: (u - lag) * per + n, per * self.schedule.units)


MAIN = Schedule([0, 1, 2, 3, 7, 8, 9], UNITS)
A1, A2, A3, B1, B2, B3, B4 = MAIN.lags
MLP = Schedule([0, 1, 2, 3, 4, 5], SORTED // 2)
C1, C2, C3, C4, C5, C6 = MLP.lags


def bank_free(pe, p, latest, *earlier):
    for sem, count in (latest,) if p.steady else (latest,) + earlier:
        pe.wait_ge(sem, count)


def program(nc, a):
    with ExitStack() as ctx:
        def sb(name, shape, dt=F32):
            return ctx.enter_context(nc.sbuf_tensor(name, shape, dt))

        def ps(name, shape):
            return ctx.enter_context(nc.psum_tensor(name, shape, F32))

        def sem(name):
            return ctx.enter_context(nc.semaphore(name))

        w_in = sb("w_in", [P, KC, PROJ])
        w_out = sb("w_out", [P, XB, DM])
        w_qkv = sb("w_qkv", [P, KC, 3 * DM])
        w_o = sb("w_o", [P, KC, DM])
        w_r = sb("w_r", [P, KC, EXP])
        norm_w = sb("norm_w", [P, KC])
        conv_w = sb("conv_w", [P, XB, TAPS])
        conv_b = sb("conv_b", [P, XB])
        dt_bias = sb("dt_bias", [P, NH])
        a_log = sb("a_log", [P, NH])
        neg_a = sb("neg_a", [P, NH])
        d_skip = sb("d_skip", [P, NH])
        qkv_b = sb("qkv_b", [P, 3 * DM])
        o_b = sb("o_b", [P, DM])
        ln1_g = sb("ln1_g", [P, DM])
        ln1_b = sb("ln1_b", [P, DM])
        r_b = sb("r_b", [P, EXP])
        ln2_g = sb("ln2_g", [P, DM])
        ln2_b = sb("ln2_b", [P, DM])
        ident = sb("ident", [P, P])
        upto = sb("upto", [P, P])
        before = sb("before", [P, P])
        ones = sb("ones", [P, P])
        ident_h = sb("ident_h", [P, P], BF16)
        future = sb("future", [P, P], BF16)
        half = sb("half", [P, 4])
        pool_held, dve_held = sb("pool_held", [P, 16]), sb("dve_held", [P, 16])
        zero = sb("zero", [P, DM])
        key = sb("key", [P, EXP])
        count_i = sb("count_i", [P, SORTED], I32)
        count_f = sb("count_f", [P, SORTED])

        xa = sb("xa", [P, 2, DM])
        st_a = sb("st_a", [P, 2, 6])
        mv_a = sb("mv_a", [P, 2, 2])
        var_a = sb("var_a", [P, 2, 2])
        nr_a = sb("nr_a", [P, 2, 2, 2])
        nm_a, rs_a = nr_a[:, 0, :, :], nr_a[:, 1, :, :]
        kept_a = sb("kept_a", [P, UNITS, 2, 2])
        xn = sb("xn", [P, 2, DM])
        xnT = sb("xnT", [P, KC, 2, P])
        cb_new = sb("cb_new", [P, 3, 2, P])
        dt_in = sb("dt_in", [P, 2, NH])
        dt_e = sb("dt_e", [P, 2, NH])
        dt = sb("dt", [P, 2, NH])
        xs = sb("xs", [P, XB, 2, P + TAPS - 1])
        halo = sb("halo", [P, ROWS, XB, TAPS - 1])
        cv = sb("cv", [P, XB, 2, P])
        xhT = sb("xhT", [P, XB, 2, P])
        cb = sb("cb", [P, 2, 2, P])
        bc = sb("bc", [P, 2, P])
        mr = sb("mr", [P, 2, 2])
        da = sb("da", [P, 2, NH])
        sm = sb("sm", [P, 3, 2, NH])
        ncum = sb("ncum", [P, 2, NH])
        ex = sb("ex", [P, 3, 2, NH])
        sz = sb("sz", [P, 2, DI])
        em = sb("em", [P, 2, NH, P])
        xh = sb("xh", [P, 2, DI])
        dtx = sb("dtx", [P, 2, DI])
        wdtx = sb("wdtx", [P, 2, DI])
        state = sb("state", [P, ROWS, DI])
        y = sb("y", [P, 2, DI])
        yT = sb("yT", [P, XB, 2, P])
        xr = sb("xr", [P, 2, DM])
        x0 = sb("x0", [P, 2, DM])
        s1 = sb("s1", [P, 2, DM])
        st_c = sb("st_c", [P, 2, 6])
        mv_c = sb("mv_c", [P, 2, 2])
        var_c = sb("var_c", [P, 2])
        rs_c = sb("rs_c", [P, 2])
        x1 = sb("x1", [P, 2, DM])
        st_b = sb("st_b", [P, 2, 6])
        mv_b = sb("mv_b", [P, 2, 2])
        var_b = sb("var_b", [P, 2])
        nr_b = sb("nr_b", [P, 2, 2])
        nm_b, rs_b = nr_b[:, 0, :], nr_b[:, 1, :]
        kept = sb("kept", [P, UNITS, 2, 2])
        nm_c, nm_f = sb("nm_c", [P, 2]), sb("nm_f", [P, 2])
        xb = sb("xb", [P, 2, DM])
        xbT = sb("xbT", [P, KC, 2, P])
        qkv = sb("qkv", [P, 2 * ROWS, 3 * DM])
        prod = sb("prod", [P, 2, ROWS, DM])
        sc = sb("sc", [P, 2, ROWS, AH])
        mx = sb("mx", [P, 2, AH])
        pr = sb("pr", [P, 2, ROWS, AH])
        den = sb("den", [P, 2, AH])
        rden = sb("rden", [P, 2, AH])
        cx = sb("cx", [P, 2, DM])
        cxT = sb("cxT", [P, KC, 2, P])
        x1r = sb("x1r", [P, 2, DM])
        mrb = sb("mrb", [P, 2, 2])
        x0b = sb("x0b", [P, 2, DM])
        s2 = sb("s2", [P, 2, DM])
        st_f = sb("st_f", [P, 2, 6])
        mv_f = sb("mv_f", [P, 2, 2])
        var_f = sb("var_f", [P, 2])
        rs_f = sb("rs_f", [P, 2])
        h = sb("h", [P, 2, DM])
        hT = sb("hT", [P, KC, 2, P])
        logits = sb("logits", [P, TILES, EXP])

        work = prod[:, :, :, :].rearrange("p a b c -> p (a b c)")
        def part(n, size=TILES * EXP):
            return work[:, n * 512:n * 512 + size]
        dest_i = sb("dest_i", [P, TILES], I32)
        expert_i = sb("expert_i", [P, SORTED], I32)
        rt = sb("rt", [P, 6, TILES])
        re = sb("re", [P, 5, EXP])
        held = qkv[:, :, :].rearrange("p a b -> p (a b)")
        WE = KC * DM * EXP
        w1 = held[:, 0:WE].rearrange("p (e c n) -> p e c n", e=EXP, c=KC)
        w2 = held[:, WE:2 * WE].rearrange("p (e c n) -> p e c n", e=EXP, c=KC)
        b1 = held[:, 2 * WE:2 * WE + EXP * DM].rearrange("p (e n) -> p e n", e=EXP)
        b2 = held[:, 2 * WE + EXP * DM:2 * WE + 2 * EXP * DM].rearrange("p (e n) -> p e n", e=EXP)
        idx = sb("idx", [P, 4], I32)

        pX = ps("pX", [P, 2, 512])
        pY = ps("pY", [P, 2, 512])
        pZ = ps("pZ", [P, 2, 512])
        pW = ps("pW", [P, 512])
        pV = ps("pV", [P, 512])
        xT_v = pX[:, :, :].rearrange("p a (b r t) -> p (a b) r t", b=2, r=2)
        yT_v = pZ[:, :, :].rearrange("p a (b r t) -> p (a b) r t", b=2, r=2)

        small_in, w_in_in, w_in_2, exp_in = (sem(n) for n in ("small_in", "w_in_in", "w_in_2", "exp_in"))
        consts, prep, zeroed = sem("consts"), sem("prep"), sem("zeroed")
        alog_e = sem("alog_e")
        xa_in, xr_in, x1r_in, x1_out, h_out = (sem(n) for n in ("xa_in", "xr_in", "x1r_in", "x1_out", "h_out"))
        LN = 5
        ln_a, xn_ok, xnT_ps, xnT_sb, cbT_ps, cbT_sb = (sem(n) for n in ("ln_a", "xn_ok", "xnT_ps", "xnT_sb", "cbT_ps", "cbT_sb"))
        tok_ps, btok_sb, soft, xs_ps, xs_sb = (sem(n) for n in ("tok_ps", "btok_sb", "soft", "xs_ps", "xs_sb"))
        SOFT = 3
        halo_in, halo_out, conv, xhT_ok = (sem(n) for n in ("halo_in", "halo_out", "conv", "xhT_ok"))
        mr_ok, shift_ok, da_ok, cum_ps, decay, ex_ok = (sem(n) for n in ("mr_ok", "shift_ok", "da_ok", "cum_ps", "decay", "ex_ok"))
        kept_a_ok = sem("kept_a_ok")
        bc_ps, bc_sb = sem("bc_ps"), sem("bc_sb")
        DECAY = 2
        z_ps, sz_ok, arg_ps, exp_ok = (sem(n) for n in ("z_ps", "sz_ok", "arg_ps", "exp_ok"))
        xh_ps, xh_sb, dtx_ok, wdtx_ok, dx_ok, m_ok = (sem(n) for n in ("xh_ps", "xh_sb", "dtx_ok", "wdtx_ok", "dx_ok", "m_ok"))
        inter_ps, intra_ps, st_ps, hdec, h_ok = (sem(n) for n in ("inter_ps", "intra_ps", "st_ps", "hdec", "h_ok"))
        yin_ok, ysum_ok, yd_ok, y_ok = (sem(n) for n in ("yin_ok", "ysum_ok", "yd_ok", "y_ok"))
        yT_ps, yT_sb, out_ps, x0_ok, s1_ok, ln_c, s1n_ok, x1_ok = (sem(n) for n in ("yT_ps", "yT_sb", "out_ps", "x0_ok", "s1_ok", "ln_c", "s1n_ok", "x1_ok"))
        ln_b, kept_ok, xb_ok, xbT_ps, xbT_sb, qkv_ps, qkv_sb = (sem(n) for n in ("ln_b", "kept_ok", "xb_ok", "xbT_ps", "xbT_sb", "qkv_ps", "qkv_sb"))
        qk_ok, sc_ok, mx_ok, scm_ok, e_ok, den_ok, rden_ok = (sem(n) for n in ("qk_ok", "sc_ok", "mx_ok", "scm_ok", "e_ok", "den_ok", "rden_ok"))
        pr_ok, pv_ok, cx_ok = (sem(n) for n in ("pr_ok", "pv_ok", "cx_ok"))
        cxT_ps, cxT_sb, ao_ps, mrb_ok, x0b_ok, x0o_ok, s2_ok = (sem(n) for n in ("cxT_ps", "cxT_sb", "ao_ps", "mrb_ok", "x0b_ok", "x0o_ok", "s2_ok"))
        ln_f, s2n_ok, hg_ok, hb_ok = (sem(n) for n in ("ln_f", "s2n_ok", "hg_ok", "hb_ok"))
        hT_ps, hT_sb, lg_ps, lg_sb = (sem(n) for n in ("hT_ps", "hT_sb", "lg_ps", "lg_sb"))
        route, onehot_ok, routed, r_exp, r_ps, idx_ok = (sem(n) for n in ("route", "onehot_ok", "routed", "r_exp", "r_ps", "idx_ok"))
        hs_in = [sem(f"hs_in{j}") for j in range(2)]
        scattered = [sem(f"scattered{j}") for j in range(2)]
        ha_in, h2_in, haT_ps, haT_sb, f1_ps, f1_ok, g_ok, gT_ps, gT_sb, f2_ps = (
            sem(n) for n in ("ha_in", "h2_in", "haT_ps", "haT_sb", "f1_ps", "f1_ok", "g_ok", "gT_ps", "gT_sb", "f2_ps"))
        hb2_ok, s3_ok, ln_g, s3n_ok, l2g_ok, l2b_ok, ln_h, y_fin, ys_out = (
            sem(n) for n in ("hb2_ok", "s3_ok", "ln_g", "s3n_ok", "l2g_ok", "l2b_ok", "ln_h", "y_fin", "ys_out"))
        x1f_in = [sem(f"x1f_in{j}") for j in range(2)]
        gathered = [sem(f"gathered{j}") for j in range(2)]
        fin_ok, idx2_ok, sorted_zero = sem("fin_ok"), sem("idx2_ok"), sem("sorted_zeroed")
        fin_out = [sem(f"fin_out{j}") for j in range(2)]

        x_v = a["x"].rearrange("b (c p) d -> c p b d", p=P)
        out_v = a["out"].rearrange("b (c p) d -> c p b d", p=P)
        x1_v = a["x1_d"].rearrange("(v r p) d -> v p r d", r=2, p=P)
        h_v = a["h_d"].rearrange("(v r p) d -> v p r d", r=2, p=P)
        h_t = a["h_d"].rearrange("(n p) d -> n p d", p=P)
        sorted_t = a["sorted_d"].rearrange("(n p) d -> p n d", p=P)
        sorted_v = a["sorted_d"].rearrange("(v r p) d -> v p r d", r=2, p=P)
        ys_v = a["ys_d"].rearrange("(v r p) d -> v p r d", r=2, p=P)

        def at(view, i):
            if isinstance(i, int):
                return view[i]
            return view[bass.ds(i, 1)].rearrange("o p r d -> (o p) r d")

        def x_unit(view, v):
            if isinstance(v, int):
                return view[v // PAIRS][:, 2 * (v % PAIRS):2 * (v % PAIRS) + 2, :]
            chunk = v >> 2
            chunk.max_val = CHUNKS - 1
            return view[bass.ds(chunk, 1), :, bass.ds((v & 3) * 2, 2), :].rearrange("o p r d -> (o p) r d")

        def rows_of(v):
            return slice(2 * (v % PAIRS), 2 * (v % PAIRS) + 2) if isinstance(v, int) else bass.ds((v & 3) * 2, 2)

        def row_of(v, r):
            return slice(2 * (v % PAIRS) + r, 2 * (v % PAIRS) + r + 1) if isinstance(v, int) else bass.ds((v & 3) * 2 + r, 1)

        def slot_of(v, r):
            return slice(2 * (v % 8) + r, 2 * (v % 8) + r + 1) if isinstance(v, int) else bass.ds((v & 7) * 2 + r, 1)

        def group_of(v):
            return slice(ROWS * (v // 4 % 2), ROWS * (v // 4 % 2) + ROWS) if isinstance(v, int) else bass.ds(((v >> 2) & 1) * ROWS, ROWS)

        def unit_slice(v, n=1):
            return slice(v * n, v * n + n) if isinstance(v, int) else bass.ds(v * n, n)

        def one(i):
            return slice(i, i + 1) if isinstance(i, int) else bass.ds(i, 1)

        held_column = {}

        def waits_apart(eng, *waits):
            for s, c in waits:
                eng.wait_ge(s, c)
            c = held_column.setdefault(waits[0][0].name, len(held_column))
            if eng.engine == mybir.EngineType.Pool:
                nc.gpsimd.tensor_tensor(pool_held[:, c:c + 1], half[:, 0:1], half[:, 0:1], ALU.mult)
            else:
                nc.vector.memset(dve_held[:, c:c + 1], 0.0)

        block = ctx.enter_context(nc.Block())

        @block.sync
        def _(sp):
            small = [(norm_w, "norm_w"), (conv_w, "conv_w"), (conv_b, "conv_b")]
            rows = [(dt_bias, "dt_bias"), (a_log, "a_log"), (d_skip, "d_skip"), (qkv_b, "qkv_b"), (o_b, "o_b"),
                    (ln1_g, "ln1_g"), (ln1_b, "ln1_b"), (r_b, "r_b"), (ln2_g, "ln2_g"), (ln2_b, "ln2_b")]
            for t, n in small:
                sp.dma_start(t[:], a[n]).then_inc(small_in, 16)
            for t, n in rows:
                sp.dma_start(t[:], a[n].partition_broadcast(P)).then_inc(small_in, 16)
            sp.dma_start(w_in[:], a["w_in"]).then_inc(w_in_in, 16)
            for t, n in ((w_out, "w_out"), (w_qkv, "w_qkv"), (w_o, "w_o"), (w_r, "w_r")):
                sp.dma_start(t[:], a[n]).then_inc(w_in_2, 16)

            def body(p):
                if p.runs(A1):
                    sp.wait_ge(xn_ok, p.prev(A1))
                    if p.runs(A1):
                        sp.dma_start(xa[:], x_unit(x_v, p.unit(A1))).then_inc(xa_in, 16)
                if p.runs(A3):
                    sp.wait_ge(x1_ok, p.prev(A3))
                    sp.dma_start(xr[:], x_unit(x_v, p.unit(A3))).then_inc(xr_in, 16)
                if p.runs(B3):
                    sp.wait_ge(x0b_ok, p.prev(B3))
                    sp.wait_ge(x1_out, p.prev(B3, 16, 16))
                    sp.dma_start(x1r[:], at(x1_v, p.unit(B3))).then_inc(x1r_in, 16)
                if p.runs(A3):
                    sp.wait_ge(x1_ok, p.now(A3))
                    sp.dma_start(at(x1_v, p.unit(A3)), x1[:]).then_inc(x1_out, 16)
                if p.runs(B3):
                    sp.wait_ge(hb_ok, p.now(B3))
                    sp.dma_start(at(h_v, p.unit(B3)), h[:]).then_inc(h_out, 16)
            MAIN.run(sp, body)

            sp.wait_ge(pv_ok, 2 * UNITS)
            sp.wait_ge(qk_ok, 2 * UNITS)
            sp.dma_start(w1, a["w1"]).then_inc(exp_in, 16)
            sp.dma_start(w2, a["w2"]).then_inc(exp_in, 16)
            sp.dma_start(b1, a["b1"].partition_broadcast(P)).then_inc(exp_in, 16)
            sp.dma_start(b2, a["b2"].partition_broadcast(P)).then_inc(exp_in, 16)

            sp.wait_ge(h_out, 16 * UNITS)
            sp.wait_ge(x0b_ok, UNITS)
            for j in range(2):
                sp.dma_start(x1r[:, j, :], h_t[j]).then_inc(hs_in[j], 16)
            with sp.Fori(1, TILES // 2) as i:
                for j in range(2):
                    sp.wait_ge(scattered[j], i * 16)
                    sp.dma_start(x1r[:, j, :], h_t[bass.ds(2 * i + j, 1)].rearrange("o p d -> (o p) d")).then_inc(hs_in[j], 16)

            for j in range(2):
                sp.wait_ge(scattered[j], 16 * (TILES // 2))

            def mlp(p):
                if p.runs(C1):
                    sp.wait_ge(haT_ps, p.prev(C1))
                    sp.dma_start(xa[:], at(sorted_v, p.unit(C1))).then_inc(ha_in, 16)
                if p.runs(C4):
                    sp.wait_ge(hb2_ok, p.prev(C4))
                    sp.dma_start(xr[:], at(sorted_v, p.unit(C4))).then_inc(h2_in, 16)
                if p.runs(C6):
                    sp.wait_ge(y_fin, p.now(C6))
                    sp.dma_start(at(ys_v, p.unit(C6)), x1[:]).then_inc(ys_out, 16)
            MLP.run(sp, mlp)

            for j in range(2):
                sp.dma_start((xn, xb)[j][:], at(x1_v, j)).then_inc(x1f_in[j], 16)
            with sp.Fori(0, UNITS // 2 - 1) as i:
                for j in range(2):
                    sp.wait_ge(fin_ok, 2 * i + j + 1)
                    sp.dma_start(x_unit(out_v, sp.snap(2 * i + j, min_val=0)), (s1, s2)[j][:]).then_inc(fin_out[j], 16)
                    sp.dma_start((xn, xb)[j][:], at(x1_v, sp.snap(2 * i + j + 2, min_val=0))).then_inc(x1f_in[j], 16)
            for j in range(2):
                sp.wait_ge(fin_ok, UNITS - 1 + j)
                sp.dma_start(x_unit(out_v, UNITS - 2 + j), (s1, s2)[j][:]).then_inc(fin_out[j], 16)
            for s, n in ((x1_out, UNITS), (h_out, UNITS), (ys_out, SORTED // 2), (fin_out[0], UNITS // 2), (fin_out[1], UNITS // 2)):
                sp.wait_ge(s, 16 * n)

        @block.tensor
        def _(pe):
            def transposes(out, src, cols):
                for c in range(cols):
                    for r in range(2):
                        mm = nc.tensor.transpose(out[:, c, r, :], src[:, r, c * P:(c + 1) * P], ident[:])
                return mm

            pWt = pW[:, :].rearrange("p (c r t) -> p c r t", c=2, r=2)
            pVt = pV[:, :].rearrange("p (c r t) -> p c r t", c=2, r=2)

            def project(out, lhs, weights, kn, start_col, cols):
                for k in range(kn):
                    mm = nc.tensor.matmul(out, lhs(k), weights[:, k, start_col:start_col + cols],
                                          start=(k == 0), stop=(k == kn - 1))
                return mm

            pe.wait_ge(consts, 1)
            pe.wait_ge(prep, 1)
            pe.wait_ge(w_in_2, 64)

            def args(p, r):
                for half_ in range(2):
                    nc.tensor.matmul(pY[:, half_, :], ident_h[:], future[:].unsqueeze(1).to_broadcast([P, 4, P]),
                                     start=True, stop=False, skip_group_check=True)
                    for i in range(4):
                        hd = 4 * half_ + i
                        mm = nc.tensor.matmul(pY[:, half_, i * P:(i + 1) * P], da[:, r, hd:hd + 1].to_broadcast([P, P]),
                                              upto[:], start=False, stop=(i == 3), skip_group_check=True)
                return mm

            def inter(p, r, out):
                return nc.tensor.matmul(out, cb[:, 0, r, :], state[:, row_of(p.unit(A2), r), :], start=True, stop=True)

            def intra(r, out):
                for hd in range(NH):
                    mm = nc.tensor.matmul(out[:, hd * HD:(hd + 1) * HD], em[:, r, hd, :],
                                          dtx[:, r, hd * HD:(hd + 1) * HD], start=True, stop=True)
                return mm

            def new_state(r, out):
                return nc.tensor.matmul(out, cb[:, 1, r, :], wdtx[:, r, :], start=True, stop=True)

            def body(p):
                if p.runs(A2):
                    pe.wait_ge(da_ok, p.now(A2))
                    bank_free(pe, p, (yin_ok, p.prev(A2, 2)), (bc_sb, p.prev(A1)))
                    rhs = da[:, :, :].rearrange("p r h -> p (r h)")
                    nc.tensor.matmul(pV[:, 0:16], upto[:], rhs, start=True, stop=True)
                    nc.tensor.matmul(pV[:, 16:32], ones[:], rhs, start=True, stop=True).then_inc(cum_ps, 1)
                    bank_free(pe, p, (qkv_sb, p.prev(B1, 2)), (xs_sb, p.prev(A1)), (xh_sb, p.prev(A2)))
                    for r in range(2):
                        mm = project(pX[:, r, :], lambda k: xnT[:, k, r, :], w_in, KC, 0, DI)
                    mm.then_inc(z_ps, 1)
                if p.runs(B3):
                    pe.wait_ge(cx_ok, p.now(B3, 2))
                    bank_free(pe, p, (qkv_sb, p.prev(B1, 2)), (exp_ok, p.prev(A2, 2)), (xbT_sb, p.prev(B1)), (cxT_sb, p.prev(B3)))
                    transposes(pY[:, 0, :].rearrange("p (c r t) -> p c r t", c=2, r=2), cx, KC).then_inc(cxT_ps, 1)
                if p.runs(B4):
                    pe.wait_ge(hb_ok, p.now(B4))
                    bank_free(pe, p, (yin_ok, p.prev(A2, 2)), (cbT_sb, p.prev(A1)), (lg_sb, p.prev(B4)))
                    transposes(pWt, h, KC).then_inc(hT_ps, 1)
                if p.runs(A2):
                    bank_free(pe, p, (cxT_sb, p.now(B3)), (xnT_sb, p.prev(A1)), (xbT_sb, p.prev(B1)), (qkv_sb, p.prev(B1, 2)),
                              (exp_ok, p.prev(A2, 2)))
                    args(p, 0).then_inc(arg_ps, 1)
                if p.runs(A3):
                    pe.wait_ge(y_ok, p.now(A3))
                    bank_free(pe, p, (h_ok, p.prev(A2, 2)), (ysum_ok, p.prev(A2, 2)), (s2_ok, p.prev(B3)), (soft, p.prev(A1, SOFT)),
                              (btok_sb, p.prev(A1)), (s1_ok, p.prev(A3)))
                    if p.steady:
                        pe.wait_ge(ysum_ok, p.prev(A2, 2))
                    transposes(yT_v, y, XB).then_inc(yT_ps, 1)
                if p.runs(B4):
                    pe.wait_ge(hT_sb, p.now(B4))
                    for r in range(2):
                        mm = project(pW[:, r * EXP:(r + 1) * EXP], lambda k: hT[:, k, r, :], w_r, KC, 0, EXP)
                    mm.then_inc(lg_ps, 1)
                if p.runs(A3):
                    pe.wait_ge(yT_sb, p.now(A3))
                    for r in range(2):
                        mm = project(pZ[:, 0, r * DM:(r + 1) * DM], lambda k: yT[:, k, r, :], w_out, XB, 0, DM)
                    mm.then_inc(out_ps, 1)
                if p.runs(B3):
                    pe.wait_ge(cxT_sb, p.now(B3))
                    bank_free(pe, p, (yT_sb, p.now(A3)), (h_ok, p.prev(A2, 2)), (s2_ok, p.prev(B3)))
                    for r in range(2):
                        mm = project(pZ[:, 1, r * DM:(r + 1) * DM], lambda k: cxT[:, k, r, :], w_o, KC, 0, DM)
                    mm.then_inc(ao_ps, 1)
                if p.runs(A2):
                    pe.wait_ge(xhT_ok, p.now(A2))
                    pe.wait_ge(sz_ok, p.now(A2))
                    for r in range(2):
                        for b in range(XB):
                            mm = nc.tensor.transpose(pX[:, r, b * P:(b + 1) * P], xhT[:, b, r, :], ident[:])
                    mm.then_inc(xh_ps, 1)
                if p.runs(A1):
                    pe.wait_ge(xn_ok, p.now(A1))
                    bank_free(pe, p, (exp_ok, p.prev(A2, 2, 1)), (qkv_sb, p.prev(B1, 2)), (xnT_sb, p.prev(A1)))
                    transposes(pY[:, 1, :].rearrange("p (c r t) -> p c r t", c=2, r=2), xn, KC).then_inc(xnT_ps, 1)
                if p.runs(B1):
                    pe.wait_ge(xb_ok, p.now(B1))
                    bank_free(pe, p, (exp_ok, p.prev(A2, 2, 1)), (cxT_sb, p.now(B3)), (qkv_sb, p.prev(B1, 2)), (xbT_sb, p.prev(B1)))
                    transposes(pY[:, 0, :].rearrange("p (c r t) -> p c r t", c=2, r=2), xb, KC).then_inc(xbT_ps, 1)
                if p.runs(A1):
                    pe.wait_ge(xnT_sb, p.now(A1))
                    bank_free(pe, p, (s1_ok, p.now(A3)), (ysum_ok, p.prev(A2, 2)), (soft, p.prev(A1, SOFT)), (btok_sb, p.prev(A1)))
                    for r in range(2):
                        mm = project(pZ[:, 0, r * WTOK:(r + 1) * WTOK], lambda k: xnT[:, k, r, :], w_in, KC, COL_B, WTOK)
                    mm.then_inc(tok_ps, 1)
                if p.runs(A2):
                    bank_free(pe, p, (xbT_sb, p.now(B1)), (xnT_sb, p.now(A1)), (exp_ok, p.prev(A2, 2, 1)))
                    args(p, 1).then_inc(arg_ps, 1)
                if p.runs(A1):
                    bank_free(pe, p, (lg_sb, p.now(B4)), (yin_ok, p.prev(A2, 2)), (cbT_sb, p.prev(A1)))
                    for m in range(2):
                        for k in range(KC):
                            mm = nc.tensor.matmul(pWt[:, m, :, :], w_in[:, k, COL_C + m * NST:COL_C + (m + 1) * NST],
                                                  xnT[:, k, :, :], start=(k == 0), stop=(k == KC - 1))
                    mm.then_inc(cbT_ps, 1)
                    bank_free(pe, p, (xh_sb, p.now(A2)), (qkv_sb, p.prev(B1, 2)), (xs_sb, p.prev(A1)))
                    for b in range(XB):
                        for k in range(KC):
                            mm = nc.tensor.matmul(xT_v[:, b, :, :], w_in[:, k, COL_X + b * P:COL_X + (b + 1) * P],
                                                  xnT[:, k, :, :], start=(k == 0), stop=(k == KC - 1))
                    mm.then_inc(xs_ps, 1)
                if p.runs(A1):
                    pe.wait_ge(cbT_sb, p.now(A1))
                    bank_free(pe, p, (decay, p.now(A2, DECAY)), (yin_ok, p.prev(A2, 2)), (bc_sb, p.prev(A1)))
                    for r in range(2):
                        mm = nc.tensor.matmul(pV[:, r * P:(r + 1) * P], cb_new[:, 1, r, :], cb_new[:, 0, r, :], start=True, stop=True)
                    mm.then_inc(bc_ps, 1)
                if p.runs(A2):
                    pe.wait_ge(h_ok, p.prev(A2, 2))
                    pe.wait_ge(shift_ok, p.now(A2))
                    bank_free(pe, p, (cbT_sb, p.now(A1)), (lg_sb, p.now(B4)), (yin_ok, p.prev(A2, 2)))
                    inter(p, 0, pW[:, :]).then_inc(inter_ps, 1)
                    pe.wait_ge(m_ok, p.prev(A2, 2, 1))
                    pe.wait_ge(dtx_ok, p.now(A2))
                    bank_free(pe, p, (soft, p.prev(A1, SOFT, 1)), (s1_ok, p.now(A3)), (ysum_ok, p.prev(A2, 2)))
                    pe.wait_ge(btok_sb, p.now(A1))
                    intra(0, pZ[:, 0, :]).then_inc(intra_ps, 1)
                if p.runs(B1):
                    bank_free(pe, p, (exp_ok, p.now(A2, 2)), (xnT_sb, p.now(A1)), (cxT_sb, p.now(B3)), (qkv_sb, p.prev(B1, 2)))
                    pe.wait_ge(xbT_sb, p.now(B1))
                    project(pY[:, 0, :], lambda k: xbT[:, k, 0, :], w_qkv, KC, 0, 2 * DM)
                    project(pY[:, 1, 0:DM], lambda k: xbT[:, k, 0, :], w_qkv, KC, 2 * DM, DM).then_inc(qkv_ps, 1)
                if p.runs(A2):
                    pe.wait_ge(wdtx_ok, p.now(A2))
                    bank_free(pe, p, (s2_ok, p.now(B3)), (yT_sb, p.now(A3)), (h_ok, p.prev(A2, 2)))
                    new_state(0, pZ[:, 1, :]).then_inc(st_ps, 1)
                    bank_free(pe, p, (bc_sb, p.now(A1)), (decay, p.now(A2, DECAY)))
                    inter(p, 1, pV[:, :]).then_inc(inter_ps, 1)
                    pe.wait_ge(m_ok, p.now(A2, 2))
                    pe.wait_ge(ysum_ok, p.prev(A2, 2, 1))
                    intra(1, pZ[:, 0, :]).then_inc(intra_ps, 1)
                    pe.wait_ge(h_ok, p.prev(A2, 2, 1))
                    new_state(1, pZ[:, 1, :]).then_inc(st_ps, 1)
                if p.runs(B1):
                    bank_free(pe, p, (xs_sb, p.now(A1)), (xh_sb, p.now(A2)), (qkv_sb, p.prev(B1, 2)))
                    project(pX[:, 0, :], lambda k: xbT[:, k, 1, :], w_qkv, KC, 0, 2 * DM)
                    project(pX[:, 1, 0:DM], lambda k: xbT[:, k, 1, :], w_qkv, KC, 2 * DM, DM).then_inc(qkv_ps, 1)

            MAIN.run(pe, body)

            pe.wait_ge(onehot_ok, 1)
            pe.wait_ge(qkv_sb, 2 * UNITS)
            onehot = part(5)
            nc.tensor.matmul(pX[:, 0, :], before[:], onehot, start=True, stop=True)
            nc.tensor.matmul(pX[:, 1, :], ones[:], onehot, start=True, stop=True).then_inc(r_ps, 1)

            pe.wait_ge(routed, 1)
            pe.wait_ge(exp_in, 64)

            def expert_of(p, stage, r):
                return pe.value_load(expert_i[0:1, one(p.unit(stage) * 2 + r)], min_val=0, max_val=EXP - 1)

            def mlp(p):
                if p.runs(C4):
                    pe.wait_ge(gT_sb, p.now(C4))
                    pe.wait_ge(s3_ok, p.prev(C4))
                    for r in range(2):
                        e = expert_of(p, C4, r)
                        for k in range(KC):
                            mm = nc.tensor.matmul(pY[:, 0, r * DM:(r + 1) * DM], cxT[:, k, r, :],
                                                  w2[:, bass.ds(e, 1), k, :], start=(k == 0), stop=(k == KC - 1))
                    mm.then_inc(f2_ps, 1)
                if p.runs(C2):
                    pe.wait_ge(haT_sb, p.now(C2))
                    pe.wait_ge(f1_ok, p.prev(C2))
                    for r in range(2):
                        e = expert_of(p, C2, r)
                        for k in range(KC):
                            mm = nc.tensor.matmul(pX[:, 0, r * DM:(r + 1) * DM], xnT[:, k, r, :],
                                                  w1[:, bass.ds(e, 1), k, :], start=(k == 0), stop=(k == KC - 1))
                    mm.then_inc(f1_ps, 1)
                if p.runs(C1):
                    pe.wait_ge(ha_in, p.prev(C1, 16, 16))
                    pe.wait_ge(haT_sb, p.prev(C1))
                    transposes(pWt, xa, KC).then_inc(haT_ps, 1)
                if p.runs(C3):
                    pe.wait_ge(g_ok, p.now(C3))
                    pe.wait_ge(gT_sb, p.prev(C3))
                    transposes(pVt, cx, KC).then_inc(gT_ps, 1)
            MLP.run(pe, mlp)

        @block.scalar
        def _(act):
            copy = nc.scalar.copy
            t4 = "p (c r t) -> p c r t"
            act.wait_ge(small_in, 13 * 16)
            nc.scalar.activation(neg_a[:], a_log[:], ACT.Exp).then_inc(alog_e, 1)

            def decays(p, r):
                act.wait_ge(arg_ps, p.prev(A2, 2, r + 1))
                act.wait_ge(intra_ps, p.prev(A2, 2))
                for hd in range(NH):
                    ins = nc.scalar.activation(em[:, r, hd, :], pY[:, hd // 4, (hd % 4) * P:(hd % 4 + 1) * P], ACT.Exp,
                                               bias=ncum[:, r, hd:hd + 1])
                return ins

            def norm_rows(out, x, shift, factor):
                for r in range(2):
                    ins = nc.scalar.activation(out[:, r, :], x[:, r, :], ACT.Identity, bias=shift[:, r:r + 1], scale=factor[:, r:r + 1])
                return ins

            def body(p):
                if p.runs(A3):
                    act.wait_ge(xr_in, p.prev(A3, 16, 16))
                    act.wait_ge(s1_ok, p.prev(A3))
                    act.wait_ge(mr_ok, p.now(A3))
                    norm_rows(x0, xr, mr[:, 0, :], mr[:, 1, :]).then_inc(x0_ok, 1)
                if p.runs(A2):
                    act.wait_ge(z_ps, p.now(A2))
                    act.wait_ge(y_ok, p.prev(A2))
                    nc.scalar.activation(sz[:], pX[:], ACT.Silu).then_inc(sz_ok, 1)
                if p.runs(B3):
                    act.wait_ge(cxT_ps, p.now(B3))
                    act.wait_ge(ao_ps, p.prev(B3))
                    copy(cxT[:], pY[:, 0, :].rearrange(t4, c=2, r=2)).then_inc(cxT_sb, 1)
                if p.runs(B4):
                    act.wait_ge(hT_ps, p.now(B4))
                    act.wait_ge(lg_ps, p.prev(B4))
                    copy(hT[:], pW[:, :].rearrange(t4, c=2, r=2)).then_inc(hT_sb, 1)
                if p.runs(A2):
                    act.wait_ge(decay, p.now(A2, DECAY))
                    act.wait_ge(wdtx_ok, p.prev(A2))
                    act.wait_ge(hdec, p.prev(A2, 2))
                    act.wait_ge(yin_ok, p.prev(A2, 2))
                    nc.scalar.activation(ex[:], sm[:], ACT.Exp).then_inc(ex_ok, 1)
                if p.runs(B3):
                    act.wait_ge(mrb_ok, p.now(B3))
                    act.wait_ge(x1r_in, p.prev(B3, 16, 16))
                    act.wait_ge(s2_ok, p.prev(B3))
                    norm_rows(x0b, x1r, mrb[:, 0, :], mrb[:, 1, :]).then_inc(x0b_ok, 1)
                if p.runs(A2):
                    decays(p, 0).then_inc(exp_ok, 1)
                if p.runs(A3):
                    act.wait_ge(yT_ps, p.now(A3))
                    act.wait_ge(out_ps, p.prev(A3))
                    copy(yT[:], yT_v).then_inc(yT_sb, 1)
                if p.runs(A1):
                    act.wait_ge(ln_a, p.now(A1, LN))
                    act.wait_ge(xnT_ps, p.prev(A1))
                    norm_rows(xn, xa, nm_a[:, 1, :], rs_a[:, 1, :]).then_inc(xn_ok, 1)
                if p.runs(B1):
                    act.wait_ge(ln_b, p.now(B1, LN))
                    act.wait_ge(xbT_ps, p.prev(B1))
                    norm_rows(xb, x1, nm_b, rs_b).then_inc(xb_ok, 1)
                if p.runs(B2):
                    act.wait_ge(scm_ok, p.now(B2))
                    act.wait_ge(pv_ok, p.prev(B2, 2))
                    nc.scalar.activation(pr[:], sc[:], ACT.Exp).then_inc(e_ok, 1)
                if p.runs(A2):
                    act.wait_ge(xh_ps, p.now(A2))
                    act.wait_ge(yd_ok, p.prev(A2))
                    copy(xh[:], pX[:]).then_inc(xh_sb, 1)
                if p.runs(A1):
                    act.wait_ge(xnT_ps, p.now(A1))
                    act.wait_ge(xs_ps, p.prev(A1))
                    act.wait_ge(z_ps, p.now(A2))
                    copy(xnT[:], pY[:, 1, :].rearrange(t4, c=2, r=2)).then_inc(xnT_sb, 1)
                if p.runs(B1):
                    act.wait_ge(xbT_ps, p.now(B1))
                    act.wait_ge(qkv_ps, p.prev(B1, 2))
                    copy(xbT[:], pY[:, 0, :].rearrange(t4, c=2, r=2)).then_inc(xbT_sb, 1)
                if p.runs(A1):
                    act.wait_ge(tok_ps, p.now(A1))
                    act.wait_ge(shift_ok, p.now(A2))
                    copy(cb_new[:, 2, :, :], pZ[:, 0, 0:2 * WTOK].rearrange("p (r w) -> p r w", r=2)[:, :, 0:NST]).then_inc(btok_sb, 1)
                if p.runs(A2):
                    decays(p, 1).then_inc(exp_ok, 1)
                if p.runs(A1):
                    act.wait_ge(cbT_ps, p.now(A1))
                    copy(cb_new[:, 0:2, :, :], pW[:, :].rearrange(t4, c=2, r=2)).then_inc(cbT_sb, 1)
                    act.wait_ge(soft, p.prev(A1, SOFT, 1))
                    nc.scalar.activation(dt_e[:], dt_in[:], ACT.Exp).then_inc(soft, 1)
                if p.runs(A3):
                    act.wait_ge(ln_c, p.now(A3, LN))
                    norm_rows(s1, s1, nm_c, rs_c).then_inc(s1n_ok, 1)
                if p.runs(A1):
                    act.wait_ge(bc_ps, p.now(A1))
                    act.wait_ge(m_ok, p.now(A2, 2))
                    copy(bc[:], pV[:, 0:2 * P].rearrange("p (r t) -> p r t", r=2)).then_inc(bc_sb, 1)
                    act.wait_ge(xs_ps, p.now(A1))
                    act.wait_ge(conv, p.prev(A1, TAPS))
                    act.wait_ge(halo_out, p.prev(A1))
                    act.wait_ge(xhT_ok, p.prev(A1))
                    for b in range(XB):
                        ins = nc.scalar.activation(cv[:, b, :, :], xT_v[:, b, :, :], ACT.Identity,
                                                   bias=conv_b[:, b:b + 1], scale=conv_w[:, b, TAPS - 1:TAPS])
                    ins.then_inc(conv, 1)
                    copy(xs[:, :, :, TAPS - 1:], xT_v).then_inc(xs_sb, 1)
                if p.runs(B3):
                    act.wait_ge(ln_f, p.now(B3, LN))
                    norm_rows(s2, s2, nm_f, rs_f).then_inc(s2n_ok, 1)
                if p.runs(A1):
                    act.wait_ge(soft, p.prev(A1, SOFT, 2))
                    act.wait_ge(dtx_ok, p.now(A2))
                    act.wait_ge(da_ok, p.prev(A1))
                    nc.scalar.activation(dt[:], dt_e[:], ACT.Ln, bias=1.0).then_inc(soft, 1)
                    act.wait_ge(conv, p.now(A1, TAPS))
                    act.wait_ge(xh_ps, p.now(A2))
                    nc.scalar.activation(xhT[:], cv[:], ACT.Silu).then_inc(xhT_ok, 1)

            MAIN.run(act, body)

            act.wait_ge(r_exp, 1)
            nc.scalar.activation(part(0), part(0), ACT.Exp).then_inc(r_exp, 1)

            def mlp(p):
                if p.runs(C5):
                    act.wait_ge(ln_g, p.now(C5, LN))
                    norm_rows(s2, s2, nm_c, rs_c).then_inc(s3n_ok, 1)
                if p.runs(C6):
                    act.wait_ge(ln_h, p.now(C6, LN))
                    act.wait_ge(ys_out, p.prev(C6, 16))
                    norm_rows(x1, h, nm_f, rs_f).then_inc(y_fin, 1)
                if p.runs(C1):
                    act.wait_ge(haT_ps, p.now(C1))
                    act.wait_ge(f1_ps, p.now(C2))
                    copy(xnT[:], pW[:, :].rearrange(t4, c=2, r=2)).then_inc(haT_sb, 1)
                if p.runs(C3):
                    act.wait_ge(gT_ps, p.now(C3))
                    act.wait_ge(f2_ps, p.now(C4))
                    copy(cxT[:], pV[:, :].rearrange(t4, c=2, r=2)).then_inc(gT_sb, 1)
                if p.runs(C2):
                    act.wait_ge(f1_ok, p.now(C2))
                    act.wait_ge(gT_ps, p.now(C3))
                    nc.scalar.activation(cx[:], x0[:], ACT.Gelu).then_inc(g_ok, 1)
            MLP.run(act, mlp)

        @block.vector
        def _(dve):
            v = nc.vector

            def norm_stats(sem, base, x, st, mv, var):
                for r in range(2):
                    ins = v.bn_stats(st[:, r, :], x[:, r, :])
                ins.then_inc(sem, 1)
                waits_apart(dve, (sem, base(1)))
                for r in range(2):
                    ins = v.bn_aggr(mv[:, r, :], st[:, r, :])
                ins.then_inc(sem, 1)
                dve.wait_ge(sem, base(2))
                if var is not None:
                    v.tensor_scalar(var[:, 0:2], mv[:, :, 1], EPS, None, ALU.add).then_inc(sem, 1)
                else:
                    v.tensor_scalar(var_a[:, 0, :], mv[:, :, 1], EPS, None, ALU.add)
                    v.tensor_scalar(var_a[:, 1, :], mv[:, :, 1], 1.0 + RMS_EPS, EPS * RMS_EPS, ALU.mult, ALU.add).then_inc(sem, 1)

            def norm_shift(sem, count, out, mean, factor):
                dve.wait_ge(sem, count)
                v.scalar_tensor_tensor(out, mean, -1.0, factor, ALU.mult, ALU.mult).then_inc(sem, 1)

            dve.wait_ge(small_in, 13 * 16)
            dve.wait_ge(w_in_in, 16)
            for k in range(KC):
                v.tensor_scalar(w_in[:, k, :], w_in[:, k, :], norm_w[:, k:k + 1], None, ALU.mult)
            dve.wait_ge(alog_e, 1)
            v.tensor_scalar(neg_a[:], neg_a[:], -1.0, None, ALU.mult).then_inc(route, 1)
            dve.wait_ge(w_in_2, 64)
            for k in range(KC):
                v.tensor_scalar(w_qkv[:, k, 0:DM], w_qkv[:, k, 0:DM], AD ** -0.5, None, ALU.mult)
            v.tensor_scalar(qkv_b[:, 0:DM], qkv_b[:, 0:DM], AD ** -0.5, None, ALU.mult).then_inc(prep, 1)
            dve.wait_ge(prep, 1)
            dve.wait_ge(route, 1)
            dve.wait_ge(consts, 1)

            def scores(p, r):
                products(p, r)
                sums(p, r)

            def products(p, r):
                dve.wait_ge(qkv_sb, p.prev(B1, 2))
                dve.wait_ge(cx_ok, p.prev(B2, 2))
                v.tensor_tensor(prod[:, r, :, :], qkv[:, group_of(p.unit(B2)), DM:2 * DM],
                                qkv[:, slot_of(p.unit(B2), r), 0:DM].to_broadcast([P, ROWS, DM]), ALU.mult).then_inc(qk_ok, 1)

            def sums(p, r):
                dve.wait_ge(qk_ok, p.prev(B2, 2, r + 1))
                dve.wait_ge(e_ok, p.prev(B2))
                v.tensor_reduce(sc[:, r, :, :].rearrange("p s h -> p (s h)"), prod[:, r, :, :].rearrange("p s (h d) -> p (s h) d", d=AD),
                                AX.X, ALU.add).then_inc(sc_ok, 1)

            def context(p, r):
                dve.wait_ge(pv_ok, p.prev(B2, 2, r + 1))
                dve.wait_ge(cxT_ps, p.now(B3))
                v.tensor_reduce(cx[:, r, :], prod[:, r, :, :].rearrange("p s c -> p c s"), AX.X, ALU.add).then_inc(cx_ok, 1)

            def mask(p, r):
                dve.wait_ge(exp_ok, p.prev(A2, 2, r + 1))
                dve.wait_ge(bc_sb, p.now(A2))
                v.tensor_tensor(em[:, r, :, :], em[:, r, :, :], bc[:, r, :].unsqueeze(1).to_broadcast([P, NH, P]),
                                ALU.mult).then_inc(m_ok, 1)

            def inner(p, r, bank):
                dve.wait_ge(inter_ps, p.prev(A2, 2, r + 1))
                dve.wait_ge(ex_ok, p.now(A2))
                dve.wait_ge(yT_ps, p.now(A3))
                yr = y[:, r, :].rearrange("p (h d) -> p h d", h=NH)
                v.tensor_tensor(yr, bank.rearrange("p (h d) -> p h d", h=NH), ex[:, 1, r, :].unsqueeze(2).to_broadcast([P, NH, HD]),
                                ALU.mult).then_inc(yin_ok, 1)
                dve.wait_ge(intra_ps, p.prev(A2, 2, r + 1))
                dve.wait_ge(yin_ok, p.prev(A2, 2, r + 1))
                v.tensor_tensor(y[:, r, :], pZ[:, 0, :], y[:, r, :], ALU.add).then_inc(ysum_ok, 1)

            def carry(p, r):
                dve.wait_ge(st_ps, p.prev(A2, 2, r + 1))
                dve.wait_ge(hdec, p.prev(A2, 2, r + 1))
                st = state[:, row_of(p.unit(A2), r), :].rearrange("p o n -> p (o n)")
                v.tensor_tensor(st, pZ[:, 1, :], st, ALU.add).then_inc(h_ok, 1)

            def biased(p, r, bank):
                dve.wait_ge(qkv_ps, p.prev(B1, 2, r + 1))
                dve.wait_ge(pv_ok, p.prev(B2, 2))
                v.tensor_tensor(qkv[:, slot_of(p.unit(B1), r), :].rearrange("p o n -> p (o n)"),
                                bank.rearrange("p a n -> p (a n)")[:, 0:3 * DM], qkv_b[:], ALU.add).then_inc(qkv_sb, 1)

            def body(p):
                if p.runs(B1):
                    dve.wait_ge(x1_ok, p.now(B1))
                    dve.wait_ge(xb_ok, p.prev(B1))
                    norm_stats(ln_b, lambda n: p.prev(B1, LN, n), x1, st_b, mv_b, var_b)
                if p.runs(A3):
                    dve.wait_ge(kept_a_ok, p.now(A3))
                    dve.wait_ge(x0_ok, p.prev(A3))
                    v.tensor_copy(mr[:], kept_a[:, one(p.unit(A3)), :, :].rearrange("p o a r -> p (o a) r")).then_inc(mr_ok, 1)
                if p.runs(B3):
                    dve.wait_ge(kept_ok, p.now(B3))
                    dve.wait_ge(x0b_ok, p.prev(B3))
                    v.tensor_copy(mrb[:], kept[:, one(p.unit(B3)), :, :].rearrange("p o a r -> p (o a) r")).then_inc(mrb_ok, 1)
                if p.runs(A2):
                    dve.wait_ge(cum_ps, p.now(A2))
                    dve.wait_ge(ex_ok, p.prev(A2))
                    dve.wait_ge(exp_ok, p.prev(A2, 2))
                    v.tensor_copy(sm[:, 1:3, :, :].rearrange("p a r h -> p (a r h)"), pV[:, 0:32]).then_inc(decay, 1)
                if p.runs(A1):
                    dve.wait_ge(xa_in, p.prev(A1, 16, 16))
                    dve.wait_ge(xn_ok, p.prev(A1))
                    norm_stats(ln_a, lambda n: p.prev(A1, LN, n), xa, st_a, mv_a, None)
                if p.runs(A2):
                    dve.wait_ge(decay, p.prev(A2, DECAY, 1))
                    v.tensor_tensor(sm[:, 0, :, :], sm[:, 2, :, :], sm[:, 1, :, :], ALU.subtract)
                    v.tensor_scalar(ncum[:], sm[:, 1, :, :], -1.0, None, ALU.mult).then_inc(decay, 1)
                if p.runs(B2):
                    products(p, 0)
                if p.runs(A1):
                    norm_shift(ln_a, p.prev(A1, LN, 4), nm_a, mv_a[:, :, 0].unsqueeze(1).to_broadcast([P, 2, 2]), rs_a)
                    dve.wait_ge(ln_a, p.now(A1, LN))
                    v.tensor_copy(kept_a[:, one(p.unit(A1)), :, :].rearrange("p o a r -> p (o a) r"), nr_a[:, :, 0, :]).then_inc(kept_a_ok, 1)
                if p.runs(B1):
                    norm_shift(ln_b, p.prev(B1, LN, 4), nm_b, mv_b[:, :, 0], rs_b)
                    dve.wait_ge(ln_b, p.now(B1, LN))
                    v.tensor_copy(kept[:, one(p.unit(B1)), :, :].rearrange("p o a r -> p (o a) r"), nr_b[:]).then_inc(kept_ok, 1)
                if p.runs(B2):
                    sums(p, 0)
                if p.runs(B2):
                    scores(p, 1)
                    dve.wait_ge(sc_ok, p.now(B2, 2))
                    v.tensor_reduce(mx[:], sc[:].rearrange("p r s h -> p r h s"), AX.X, ALU.max).then_inc(mx_ok, 1)
                    dve.wait_ge(mx_ok, p.now(B2))
                    v.tensor_tensor(sc[:], sc[:], mx[:].unsqueeze(2).to_broadcast([P, 2, ROWS, AH]), ALU.subtract).then_inc(scm_ok, 1)
                if p.runs(B4):
                    dve.wait_ge(lg_ps, p.now(B4))
                    v.tensor_tensor(logits[:, unit_slice(p.unit(B4), 2), :], pW[:, 0:2 * EXP].rearrange("p (r e) -> p r e", r=2),
                                    r_b[:].unsqueeze(1).to_broadcast([P, 2, EXP]), ALU.add).then_inc(lg_sb, 1)
                if p.runs(A3):
                    dve.wait_ge(out_ps, p.now(A3))
                    dve.wait_ge(s1n_ok, p.prev(A3))
                    dve.wait_ge(x0_ok, p.now(A3))
                    v.tensor_tensor(s1[:].rearrange("p r d -> p (r d)"), pZ[:, 0, :], x0[:].rearrange("p r d -> p (r d)"), ALU.add).then_inc(s1_ok, 1)
                    dve.wait_ge(s1_ok, p.now(A3))
                    norm_stats(ln_c, lambda n: p.prev(A3, LN, n), s1, st_c, mv_c, var_c)
                if p.runs(B2):
                    dve.wait_ge(e_ok, p.now(B2))
                    v.tensor_reduce(den[:], pr[:].rearrange("p r s h -> p r h s"), AX.X, ALU.add).then_inc(den_ok, 1)
                    dve.wait_ge(den_ok, p.now(B2))
                    v.reciprocal(rden[:], den[:]).then_inc(rden_ok, 1)
                    dve.wait_ge(rden_ok, p.now(B2))
                    v.tensor_tensor(pr[:], pr[:], rden[:].unsqueeze(2).to_broadcast([P, 2, ROWS, AH]), ALU.mult).then_inc(pr_ok, 1)
                if p.runs(A2):
                    mask(p, 0)
                if p.runs(B3):
                    dve.wait_ge(ao_ps, p.now(B3))
                    dve.wait_ge(x0o_ok, p.now(B3))
                    dve.wait_ge(hg_ok, p.prev(B3))
                    v.tensor_tensor(s2[:].rearrange("p r d -> p (r d)"), pZ[:, 1, :], x0b[:].rearrange("p r d -> p (r d)"), ALU.add).then_inc(s2_ok, 1)
                    dve.wait_ge(s2_ok, p.now(B3))
                    norm_stats(ln_f, lambda n: p.prev(B3, LN, n), s2, st_f, mv_f, var_f)
                if p.runs(A3):
                    norm_shift(ln_c, p.prev(A3, LN, 4), nm_c[:], mv_c[:, :, 0], rs_c[:])
                if p.runs(A1):
                    dve.wait_ge(btok_sb, p.now(A1))
                    dve.wait_ge(soft, p.prev(A1, SOFT))
                    v.tensor_tensor(dt_in[:], pZ[:, 0, 0:2 * WTOK].rearrange("p (r w) -> p r w", r=2)[:, :, NST:WTOK],
                                    dt_bias[:].unsqueeze(1).to_broadcast([P, 2, NH]), ALU.add).then_inc(soft, 1)
                if p.runs(B2):
                    context(p, 0)
                if p.runs(A2):
                    mask(p, 1)
                if p.runs(B3):
                    norm_shift(ln_f, p.prev(B3, LN, 4), nm_f[:], mv_f[:, :, 0], rs_f[:])
                if p.runs(B2):
                    context(p, 1)
                if p.runs(A3):
                    dve.wait_ge(s1n_ok, p.now(A3))
                    dve.wait_ge(x1_out, p.prev(A3, 16))
                    dve.wait_ge(xb_ok, p.now(B1))
                    v.tensor_tensor(x1[:], s1[:], xr[:], ALU.add).then_inc(x1_ok, 1)
                if p.runs(A2):
                    inner(p, 0, pW[:, :])

                def taps(k):
                    dve.wait_ge(conv, p.prev(A1, TAPS, k + 1))
                    for b in range(XB):
                        ins = v.scalar_tensor_tensor(cv[:, b, :, :], xs[:, b, :, k:k + P], conv_w[:, b, k:k + 1], cv[:, b, :, :],
                                                     ALU.mult, ALU.add)
                    ins.then_inc(conv, 1)

                if p.runs(A1):
                    dve.wait_ge(xs_sb, p.now(A1))
                    dve.wait_ge(halo_in, p.now(A1))
                    taps(0)
                if p.runs(A2):
                    carry(p, 0)
                if p.runs(B1):
                    biased(p, 0, pY[:, :, :])
                if p.runs(A2):
                    inner(p, 1, pV[:, :])
                    carry(p, 1)
                if p.runs(A1):
                    dve.wait_ge(soft, p.now(A1, SOFT))
                    dve.wait_ge(arg_ps, p.now(A2, 2))
                    v.tensor_tensor(da[:], dt[:], neg_a[:].unsqueeze(1).to_broadcast([P, 2, NH]), ALU.mult).then_inc(da_ok, 1)
                    taps(1)
                if p.runs(B1):
                    biased(p, 1, pX[:, :, :])
                if p.runs(A1):
                    taps(2)

            MAIN.run(dve, body)

            count = [1]

            def then(ins):
                count[0] += 1
                ins.then_inc(route, 1)
                dve.wait_ge(route, count[0])

            TE = TILES * EXP
            te = "p (t e) -> p t e"
            lg = logits[:]
            prob, eq, cand, one1, oneh = part(0), part(1), part(2), part(3), part(5)
            key_b = key[:].unsqueeze(1).to_broadcast([P, TILES, EXP])

            def by_tile(row):
                return row.unsqueeze(2).to_broadcast([P, TILES, EXP])

            dve.wait_ge(lg_sb, UNITS)
            dve.wait_ge(cx_ok, 2 * UNITS)
            P3, EQ3, C3, O3, H3 = (q.rearrange(te, e=EXP) for q in (prob, eq, cand, one1, oneh))
            then(v.tensor_reduce(rt[:, 0, :], lg, AX.X, ALU.max))
            v.tensor_tensor(P3, lg, by_tile(rt[:, 0, :]), ALU.subtract).then_inc(r_exp, 1)
            dve.wait_ge(r_exp, 2)
            then(v.tensor_reduce(rt[:, 0, :], P3, AX.X, ALU.add))
            then(v.reciprocal(rt[:, 1, :], rt[:, 0, :]))
            then(v.tensor_tensor(P3, P3, by_tile(rt[:, 1, :]), ALU.mult))
            then(v.tensor_reduce(rt[:, 2, :], P3, AX.X, ALU.max))
            then(v.tensor_tensor(EQ3, P3, by_tile(rt[:, 2, :]), ALU.is_equal))
            then(v.tensor_tensor(C3, EQ3, key_b, ALU.mult))
            then(v.tensor_reduce(rt[:, 3, :], C3, AX.X, ALU.max))
            then(v.tensor_tensor(O3, key_b, by_tile(rt[:, 3, :]), ALU.is_equal))
            then(v.scalar_tensor_tensor(prob, one1, -2.0, prob, ALU.mult, ALU.add))
            then(v.tensor_reduce(rt[:, 2, :], P3, AX.X, ALU.max))
            then(v.tensor_tensor(EQ3, P3, by_tile(rt[:, 2, :]), ALU.is_equal))
            then(v.tensor_tensor(C3, EQ3, key_b, ALU.mult))
            then(v.tensor_reduce(rt[:, 4, :], C3, AX.X, ALU.max))
            then(v.tensor_tensor(rt[:, 5, :], rt[:, 3, :], rt[:, 4, :], ALU.min))
            v.tensor_tensor(H3, key_b, by_tile(rt[:, 5, :]), ALU.is_equal).then_inc(onehot_ok, 1)
            dve.wait_ge(onehot_ok, 1)
            dve.wait_ge(r_ps, 1)
            tot, incl, rank = part(1), part(2), part(3)
            then(v.tensor_copy(tot, pX[:, 1, :]))
            incl3 = incl.rearrange("p (e t) -> p e t", e=EXP)
            for e in range(EXP):
                ins = v.tensor_tensor_scan(incl3[:, e, :], tot.rearrange(te, e=EXP)[:, :, e], zero[:, 0:TILES], 0.0, ALU.add, ALU.add)
            then(ins)
            then(v.tensor_tensor(rank.rearrange(te, e=EXP), incl.rearrange("p (e t) -> p t e", e=EXP), tot.rearrange(te, e=EXP), ALU.subtract))
            then(v.tensor_tensor(rank, pX[:, 0, :], rank, ALU.add))
            then(v.tensor_copy(re[:, 0, :], incl3[:, :, TILES - 1]))
            cmp3 = part(4).rearrange("p (e t) -> p e t", e=EXP)
            then(v.tensor_tensor(cmp3, re[:, 0, :].unsqueeze(2).to_broadcast([P, EXP, TILES]),
                                 count_f[:, 0:TILES].unsqueeze(1).to_broadcast([P, EXP, TILES]), ALU.is_gt))
            then(v.tensor_reduce(re[:, 1, :], cmp3, AX.X, ALU.add))
            then(v.tensor_tensor_scan(re[:, 2, :], re[:, 1, :], zero[:, 0:EXP], 0.0, ALU.add, ALU.add))
            then(v.tensor_tensor(re[:, 3, :], re[:, 2, :], re[:, 1, :], ALU.subtract))
            then(v.tensor_scalar(re[:, 3, :], re[:, 3, :], float(P), None, ALU.mult))
            then(v.tensor_tensor(rank.rearrange(te, e=EXP), rank.rearrange(te, e=EXP), re[:, 3, :].unsqueeze(1).to_broadcast([P, TILES, EXP]), ALU.add))
            then(v.tensor_tensor(rank, rank, oneh, ALU.mult))
            then(v.tensor_reduce(rt[:, 0, :], rank.rearrange(te, e=EXP), AX.X, ALU.add))
            then(v.tensor_copy(dest_i[:], rt[:, 0, :]))
            then(v.tensor_scalar(re[:, 2, :], re[:, 2, :], float(P), None, ALU.mult))
            cmps = part(6, SORTED * EXP).rearrange(te, e=EXP)
            then(v.tensor_tensor(cmps, count_f[:].unsqueeze(2).to_broadcast([P, SORTED, EXP]),
                                 re[:, 2, :].unsqueeze(1).to_broadcast([P, SORTED, EXP]), ALU.is_ge))
            expert_f = part(4, SORTED)
            then(v.tensor_reduce(expert_f, cmps, AX.X, ALU.add))
            then(v.tensor_scalar(expert_f, expert_f, float(EXP - 1), None, ALU.min))
            v.tensor_copy(expert_i[:], expert_f).then_inc(routed, 1)
            dve.wait_ge(routed, 1)
            dve.wait_ge(exp_in, 64)

            def mlp(p):
                if p.runs(C5):
                    norm_shift(ln_g, p.now(C5, LN, -1), nm_c[:], mv_c[:, :, 0], rs_c[:])
                if p.runs(C6):
                    norm_shift(ln_h, p.now(C6, LN, -1), nm_f[:], mv_f[:, :, 0], rs_f[:])
                if p.runs(C4):
                    dve.wait_ge(h2_in, p.prev(C4, 16, 16))
                    dve.wait_ge(s3_ok, p.prev(C4))
                    for r in range(2):
                        e = dve.value_load(expert_i[0:1, one(p.unit(C4) * 2 + r)], min_val=0, max_val=EXP - 1)
                        ins = v.tensor_tensor(s1[:, r, :], xr[:, r, :], b2[:, bass.ds(e, 1), :].rearrange("p o n -> p (o n)"), ALU.add)
                    ins.then_inc(hb2_ok, 1)
                if p.runs(C2):
                    dve.wait_ge(f1_ps, p.now(C2))
                    dve.wait_ge(g_ok, p.prev(C2))
                    for r in range(2):
                        e = dve.value_load(expert_i[0:1, one(p.unit(C2) * 2 + r)], min_val=0, max_val=EXP - 1)
                        ins = v.tensor_tensor(x0[:, r, :], pX[:, 0, r * DM:(r + 1) * DM], b1[:, bass.ds(e, 1), :].rearrange("p o n -> p (o n)"), ALU.add)
                    ins.then_inc(f1_ok, 1)
                if p.runs(C4):
                    dve.wait_ge(f2_ps, p.now(C4))
                    dve.wait_ge(hb2_ok, p.now(C4))
                    dve.wait_ge(l2g_ok, p.now(C5))
                    v.tensor_tensor(s2[:].rearrange("p r d -> p (r d)"), pY[:, 0, :], s1[:].rearrange("p r d -> p (r d)"), ALU.add).then_inc(s3_ok, 1)
                    dve.wait_ge(s3_ok, p.now(C4))
                    norm_stats(ln_g, lambda n: p.prev(C4, LN, n), s2, st_c, mv_c, var_c)
                if p.runs(C5):
                    dve.wait_ge(l2b_ok, p.now(C5))
                    norm_stats(ln_h, lambda n: p.prev(C5, LN, n), h, st_f, mv_f, var_f)
            MLP.run(dve, mlp)

            def finish(i):
                for j in range(2):
                    dve.wait_ge(x1f_in[j], i * 16 + 16)
                    dve.wait_ge(gathered[j], i * 32 + 32)
                    if not isinstance(i, int):
                        dve.wait_ge(fin_out[j], i * 16)
                    v.tensor_tensor((s1, s2)[j][:], (xn, xb)[j][:], (x0, x0b)[j][:], ALU.add).then_inc(fin_ok, 1)

            finish(0)
            with dve.Fori(1, UNITS // 2) as i:
                finish(i)

        @block.gpsimd
        def _(pool):
            g = nc.gpsimd
            steps = [0]

            def const(ins):
                steps[0] += 1
                ins.then_inc(zeroed, 1)
                pool.wait_ge(zeroed, steps[0])

            g.memset(state[:], 0.0)
            g.memset(halo[:], 0.0)
            g.memset(half[:], -0.5)
            const(g.memset(zero[:], 0.0))
            pool.dma_start(sorted_t, zero[:].unsqueeze(1).to_broadcast([P, SORTED, DM])).then_inc(sorted_zero, 16)
            for e in range(EXP):
                g.memset(key[:, e:e + 1], float(EXP - e))
            g.memset(ones[:], 1.0)
            g.memset(ident[:], 0.0)
            g.memset(ident_h[:], 0.0)
            g.memset(upto[:], 1.0)
            g.memset(before[:], 1.0)
            g.memset(future[:], 0.0)
            const(g.iota(count_i[:], pattern=[[P, SORTED]], base=0, channel_multiplier=0))
            for t in (ident, ident_h):
                g.affine_select(out=t[:], in_=t[:], compare_op=ALU.not_equal, fill=1.0, base=0, pattern=[[-1, P]], channel_multiplier=1)
            g.affine_select(out=upto[:], in_=upto[:], compare_op=ALU.is_ge, fill=0.0, base=0, pattern=[[1, P]], channel_multiplier=-1)
            g.affine_select(out=before[:], in_=before[:], compare_op=ALU.is_ge, fill=0.0, base=-1, pattern=[[1, P]], channel_multiplier=-1)
            g.affine_select(out=future[:], in_=future[:], compare_op=ALU.is_ge, fill=NEG, base=0, pattern=[[1, P]], channel_multiplier=-1)
            g.tensor_copy(count_f[:], count_i[:]).then_inc(consts, 1)
            pool.wait_ge(consts, 1)

            def power(sem, count, out, in_):
                pool.wait_ge(sem, count)
                g.tensor_tensor(out, in_, half[:, 0:2] if len(in_.shape) == 2 else half[:].rearrange("p (a r) -> p a r", a=2),
                                ALU.pow).then_inc(sem, 1)

            def by_heads(t, r):
                return t[:, r, :].rearrange("p (h d) -> p h d", h=NH)

            def body(p):
                if p.runs(A2):
                    waits_apart(pool, (cbT_sb, p.now(A2)), (btok_sb, p.now(A2)), (inter_ps, p.prev(A2, 2)), (st_ps, p.prev(A2, 2)))
                    g.tensor_copy(cb[:], cb_new[:, 0:3:2, :, :]).then_inc(shift_ok, 1)
                if p.runs(B1):
                    power(ln_b, p.prev(B1, LN, 3), rs_b, var_b[:])
                if p.runs(A1):
                    power(ln_a, p.prev(A1, LN, 3), rs_a, var_a[:])
                    waits_apart(pool, (conv, p.prev(A1, TAPS)), (halo_out, p.prev(A1)))
                    g.tensor_copy(xs[:, :, :, 0:TAPS - 1].rearrange("p b r k -> p r b k"), halo[:, rows_of(p.unit(A1)), :, :]).then_inc(halo_in, 1)
                if p.runs(B3):
                    pool.wait_ge(x0b_ok, p.now(B3))
                    g.tensor_tensor(x0b[:], x0b[:], o_b[:].unsqueeze(1).to_broadcast([P, 2, DM]), ALU.add).then_inc(x0o_ok, 1)
                if p.runs(A3):
                    power(ln_c, p.prev(A3, LN, 3), rs_c[:], var_c[:])
                if p.runs(A2):
                    pool.wait_ge(xh_sb, p.now(A2))
                    pool.wait_ge(intra_ps, p.prev(A2, 2))
                    for r in range(2):
                        ins = g.tensor_tensor(by_heads(dtx, r), by_heads(xh, r), dt[:, r, :].unsqueeze(2).to_broadcast([P, NH, HD]), ALU.mult)
                    ins.then_inc(dtx_ok, 1)

                def weighted(r):
                    g.tensor_tensor(prod[:, r, :, :].rearrange("p s (h d) -> p s h d", d=AD),
                                    qkv[:, group_of(p.unit(B2)), 2 * DM:3 * DM].rearrange("p s (h d) -> p s h d", d=AD),
                                    pr[:, r, :, :].unsqueeze(3).to_broadcast([P, ROWS, AH, AD]), ALU.mult).then_inc(pv_ok, 1)

                if p.runs(B2):
                    pool.wait_ge(pr_ok, p.now(B2))
                    weighted(0)
                if p.runs(B3):
                    power(ln_f, p.prev(B3, LN, 3), rs_f[:], var_f[:])
                if p.runs(B2):
                    weighted(1)
                if p.runs(A2):
                    pool.wait_ge(dtx_ok, p.now(A2))
                    pool.wait_ge(ex_ok, p.now(A2))
                    pool.wait_ge(st_ps, p.prev(A2, 2))
                    for r in range(2):
                        ins = g.tensor_tensor(by_heads(wdtx, r), by_heads(dtx, r), ex[:, 0, r, :].unsqueeze(2).to_broadcast([P, NH, HD]), ALU.mult)
                    ins.then_inc(wdtx_ok, 1)
                    for r in range(2):
                        pool.wait_ge(inter_ps, p.prev(A2, 2, r + 1))
                        st = state[:, row_of(p.unit(A2), r), :].rearrange("p o (h d) -> p (o h) d", h=NH)
                        g.tensor_tensor(st, st, ex[:, 2, r, :].unsqueeze(2).to_broadcast([P, NH, HD]), ALU.mult).then_inc(hdec, 1)
                        if r == 0:
                            for q in range(2):
                                ins = g.tensor_tensor(by_heads(xh, q), by_heads(xh, q), d_skip[:].unsqueeze(2).to_broadcast([P, NH, HD]), ALU.mult)
                            ins.then_inc(dx_ok, 1)
                if p.runs(A1):
                    waits_apart(pool, (xs_sb, p.now(A1)), (halo_in, p.now(A1)))
                    g.tensor_copy(halo[:, rows_of(p.unit(A1)), :, :], xs[:, :, :, P:P + TAPS - 1].rearrange("p b r k -> p r b k")).then_inc(halo_out, 1)
                if p.runs(B3):
                    pool.wait_ge(s2n_ok, p.now(B3))
                    pool.wait_ge(hT_ps, p.now(B4))
                    pool.wait_ge(h_out, p.prev(B3, 16))
                    g.tensor_tensor(h[:], s2[:], ln1_g[:].unsqueeze(1).to_broadcast([P, 2, DM]), ALU.mult).then_inc(hg_ok, 1)
                    pool.wait_ge(hg_ok, p.now(B3))
                    g.tensor_tensor(h[:], h[:], ln1_b[:].unsqueeze(1).to_broadcast([P, 2, DM]), ALU.add).then_inc(hb_ok, 1)
                if p.runs(A2):
                    pool.wait_ge(ysum_ok, p.now(A2, 2))
                    pool.wait_ge(dx_ok, p.now(A2))
                    pool.wait_ge(sz_ok, p.now(A2))
                    g.tensor_tensor(y[:], y[:], xh[:], ALU.add).then_inc(yd_ok, 1)
                    pool.wait_ge(yd_ok, p.now(A2))
                    g.tensor_tensor(y[:], y[:], sz[:], ALU.mult).then_inc(y_ok, 1)

            MAIN.run(pool, body)

            pool.wait_ge(routed, 1)
            pool.wait_ge(sorted_zero, 16)
            def scatter(i):
                for j in range(2):
                    if not isinstance(i, int):
                        waits_apart(pool, (scattered[j], i * 16))
                    g.tensor_copy(idx[:, j:j + 1], dest_i[:, one(i * 2 + j)]).then_inc(idx_ok, 1)
                    waits_apart(pool, (idx_ok, i * 2 + j + 1), (hs_in[j], i * 16 + 16))
                    g.indirect_dma_start(a["sorted_d"], bass.IndirectOffsetOnAxis(idx[:, j:j + 1], 0), x1r[:, j, :], None).then_inc(scattered[j], 16)

            scatter(0)
            with pool.Fori(1, TILES // 2) as i:
                scatter(i)

            def mlp(p):
                if p.runs(C5):
                    pool.wait_ge(s3n_ok, p.now(C5))
                    pool.wait_ge(y_fin, p.now(C6))
                    g.tensor_tensor(h[:], s2[:], ln2_g[:].unsqueeze(1).to_broadcast([P, 2, DM]), ALU.mult).then_inc(l2g_ok, 1)
                    pool.wait_ge(l2g_ok, p.now(C5))
                    g.tensor_tensor(h[:], h[:], ln2_b[:].unsqueeze(1).to_broadcast([P, 2, DM]), ALU.add).then_inc(l2b_ok, 1)
                if p.runs(C4):
                    power(ln_g, p.prev(C4, LN, 3), rs_c[:], var_c[:])
                if p.runs(C5):
                    power(ln_h, p.prev(C5, LN, 3), rs_f[:], var_f[:])
            MLP.run(pool, mlp)

            pool.wait_ge(ys_out, 16 * (SORTED // 2))
            def gather(i):
                for j in range(2):
                    if not isinstance(i, int):
                        waits_apart(pool, (gathered[j], i * 32))
                    for r in range(2):
                        g.tensor_copy(idx[:, 2 * j + r:2 * j + r + 1], dest_i[:, one(i * 4 + 2 * j + r)]).then_inc(idx2_ok, 1)
                    free = [] if isinstance(i, int) else [(fin_ok, i * 2 + j)]
                    waits_apart(pool, (idx2_ok, i * 4 + 2 * j + 2), *free)
                    for r in range(2):
                        g.indirect_dma_start((x0, x0b)[j][:, r, :], None, a["ys_d"],
                                             bass.IndirectOffsetOnAxis(idx[:, 2 * j + r:2 * j + r + 1], 0)).then_inc(gathered[j], 16)

            gather(0)
            with pool.Fori(1, UNITS // 2) as i:
                gather(i)


def kernel(**inputs):
    import numpy as np
    import concourse.bacc as bacc
    from concourse.bass_utils import run_bass_kernel_spmd

    g = {k.replace("L0_attn_", "a_").replace("L0_ffn_", "f_"): np.asarray(v) for k, v in inputs.items()}

    def blocks(m):
        m = m.reshape(m.shape[:-2] + (m.shape[-2] // P, P, m.shape[-1]))
        return np.ascontiguousarray(np.moveaxis(m, -2, 0))

    wt = g["a_in_proj_w"].T
    state_b, state_c = wt[:, 2 * DI:2 * DI + NST], wt[:, 2 * DI + NST:2 * DI + 2 * NST]
    arrays = {
        "x": g["a_x"],
        "w_in": blocks(np.concatenate([wt[:, :2 * DI], state_c, state_b, wt[:, 2 * DI + 2 * NST:]], axis=1)),
        "w_out": blocks(g["a_out_proj_w"].T),
        "w_qkv": blocks(g["f_in_proj_w"].T),
        "w_o": blocks(g["f_out_w"].T),
        "w_r": blocks(g["f_router_w"].T),
        "w1": blocks(np.swapaxes(g["f_w1"], 1, 2)),
        "w2": blocks(np.swapaxes(g["f_w2"], 1, 2)),
        "b1": g["f_b1"].reshape(-1), "b2": g["f_b2"].reshape(-1),
        "norm_w": g["a_norm_w"].reshape(KC, P).T, "conv_w": np.moveaxis(g["a_conv_w"].reshape(XB, P, TAPS), 1, 0),
        "conv_b": g["a_conv_b"].reshape(XB, P).T, "dt_bias": g["a_dt_bias"], "a_log": g["a_A_log"], "d_skip": g["a_D"],
        "qkv_b": g["f_in_proj_b"], "o_b": g["f_out_b"], "ln1_g": g["f_ln1_g"], "ln1_b": g["f_ln1_b"], "r_b": g["f_router_b"],
        "ln2_g": g["f_ln2_g"], "ln2_b": g["f_ln2_b"],
    }
    arrays = {k: np.ascontiguousarray(v) for k, v in arrays.items()}
    nc = bacc.Bacc("TRN2", target_bir_lowering=False, num_devices=1)
    a = {k: nc.dram_tensor(f"in_{k}", v.shape, mybir.dt.from_np(v.dtype), kind="ExternalInput").ap() for k, v in arrays.items()}
    a["b1"] = a["b1"].rearrange("(e n) -> e n", e=EXP)
    a["b2"] = a["b2"].rearrange("(e n) -> e n", e=EXP)
    a["out"] = nc.dram_tensor("out", (ROWS, SEQ, DM), F32, kind="ExternalOutput").ap()
    for name, rows in (("x1_d", ROWS * SEQ), ("h_d", ROWS * SEQ), ("sorted_d", SORTED * P), ("ys_d", SORTED * P)):
        a[name] = nc.dram_tensor(name, (rows, DM), F32, kind="Internal").ap()
    program(nc, a)
    r = run_bass_kernel_spmd(nc, [{f"in_{k}": v for k, v in arrays.items()}], core_ids=[0])
    return r.results[0]["out"]
```

```python
from contextlib import ExitStack

import concourse.bass as bass
from concourse import mybir

F32 = mybir.dt.float32
BF16 = mybir.dt.bfloat16
I32 = mybir.dt.int32
ALU = mybir.AluOpType
ACT = mybir.ActivationFunctionType
AX = mybir.AxisListType

P = 128
ROWS, SEQ, DM = 8, 1024, 256
KC = DM // P
DI = 512
XB = DI // P
NST = 128
HD = 64
NH = DI // HD
TAPS = 4
CHUNKS = SEQ // P
PAIRS = ROWS // 2
UNITS = CHUNKS * PAIRS
TILES = 2 * UNITS
AH, AD = 16, DM // 16
EXP = 8
EPS = 1e-5
RMS_EPS = 1e-6
PROJ = 2 * DI + 2 * NST + NH
COL_X, COL_C, COL_B = DI, 2 * DI, 2 * DI + NST
WTOK = NST + NH
SORTED = TILES + EXP
NEG = -1.0e30


class Schedule:

    def __init__(self, lags, units):
        self.lags, self.units = lags, units
        top = max(lags)
        edges = sorted({x for lag in lags for x in (lag, lag + 1, lag + units)} | {top + 1})
        self.segments = list(zip(edges[:-1], edges[1:]))

    def run(self, eng, body):
        for lo, hi in self.segments:
            if hi - lo == 1:
                body(Pass(self, eng, lo, lo, lo))
            else:
                with eng.Fori(lo, hi) as u:
                    body(Pass(self, eng, lo, hi - 1, u))


class Pass:

    def __init__(self, schedule, eng, first, last, u):
        self.schedule, self.eng, self.first, self.last, self.u = schedule, eng, first, last, u
        self.held = {}
        self.steady = all(self.runs(lag) for lag in schedule.lags) and first > max(schedule.lags)

    def runs(self, lag):
        return lag <= self.first and self.last < lag + self.schedule.units

    def _hold(self, key, make, top):
        if isinstance(self.u, int):
            return make(self.u)
        if key not in self.held:
            self.held[key] = self.eng.snap(make(self.u), min_val=0, max_val=top)
        return self.held[key]

    def unit(self, lag):
        return self._hold(("unit", lag), lambda u: u - lag, self.schedule.units - 1)

    def now(self, lag, per=1, n=0):
        if self.last < lag:
            return 0
        if self.first >= lag + self.schedule.units:
            return per * self.schedule.units
        return self._hold((lag, per, per + n), lambda u: (u - lag + 1) * per + n, per * self.schedule.units)

    def prev(self, lag, per=1, n=0):
        if self.last < lag:
            return 0
        if self.first >= lag + self.schedule.units:
            return per * self.schedule.units
        return self._hold((lag, per, n), lambda u: (u - lag) * per + n, per * self.schedule.units)


MAIN = Schedule([0, 1, 2, 3, 7, 8, 9], UNITS)
A1, A2, A3, B1, B2, B3, B4 = MAIN.lags
MLP = Schedule([0, 1, 2, 3, 4, 5, 6], SORTED // 2)
C1, C2, C3, C4, C5, C6, C7 = MLP.lags
RING = 8
ROW = DM + 1
TOKENS = ROWS * SEQ


def bank_free(pe, p, latest, *earlier):
    for sem, count in (latest,) if p.steady else (latest,) + earlier:
        pe.wait_ge(sem, count)


def program(nc, a):
    with ExitStack() as ctx:
        def sb(name, shape, dt=F32):
            return ctx.enter_context(nc.sbuf_tensor(name, shape, dt))

        def ps(name, shape):
            return ctx.enter_context(nc.psum_tensor(name, shape, F32))

        def sem(name):
            return ctx.enter_context(nc.semaphore(name))

        w_in = sb("w_in", [P, KC, PROJ])
        w_out = sb("w_out", [P, XB, DM])
        w_qkv = sb("w_qkv", [P, KC, 3 * DM])
        w_o = sb("w_o", [P, KC, DM])
        w_r = sb("w_r", [P, KC, EXP])
        norm_w = sb("norm_w", [P, KC])
        conv_w = sb("conv_w", [P, XB, TAPS])
        conv_b = sb("conv_b", [P, XB])
        dt_bias = sb("dt_bias", [P, NH])
        a_log = sb("a_log", [P, NH])
        neg_a = sb("neg_a", [P, NH])
        d_skip = sb("d_skip", [P, NH])
        qkv_b = sb("qkv_b", [P, 3 * DM])
        o_b = sb("o_b", [P, DM])
        ln1_g = sb("ln1_g", [P, DM])
        ln1_b = sb("ln1_b", [P, DM])
        r_b = sb("r_b", [P, EXP])
        ln2_g = sb("ln2_g", [P, DM])
        ln2_b = sb("ln2_b", [P, DM])
        ident = sb("ident", [P, P])
        upto = sb("upto", [P, P])
        before = sb("before", [P, P])
        ones = sb("ones", [P, P])
        ident_h = sb("ident_h", [P, P], BF16)
        future = sb("future", [P, P], BF16)
        half = sb("half", [P, 4])
        pool_held, dve_held = sb("pool_held", [P, 24]), sb("dve_held", [P, 24])
        zero = sb("zero", [P, ROW])
        key = sb("key", [P, EXP])
        count_i = sb("count_i", [P, SORTED], I32)
        count_f = sb("count_f", [P, SORTED])

        xa = sb("xa", [P, 2, DM])
        st_a = sb("st_a", [P, 2, 6])
        mv_a = sb("mv_a", [P, 2, 2])
        var_a = sb("var_a", [P, 2, 2])
        nr_a = sb("nr_a", [P, 2, 2, 2])
        nm_a, rs_a = nr_a[:, 0, :, :], nr_a[:, 1, :, :]
        kept_a = sb("kept_a", [P, UNITS, 2, 2])
        xn = sb("xn", [P, 2, DM])
        xnT = sb("xnT", [P, KC, 2, P])
        cb_new = sb("cb_new", [P, 3, 2, P])
        dt_in = sb("dt_in", [P, 2, NH])
        dt_e = sb("dt_e", [P, 2, NH])
        dt = sb("dt", [P, 2, NH])
        xs = sb("xs", [P, XB, 2, P + TAPS - 1])
        halo = sb("halo", [P, ROWS, XB, TAPS - 1])
        cv = sb("cv", [P, XB, 2, P])
        xhT = sb("xhT", [P, XB, 2, P])
        cb = sb("cb", [P, 2, 2, P])
        bc = sb("bc", [P, 2, P])
        mr = sb("mr", [P, 2, 2])
        da = sb("da", [P, 2, NH])
        sm = sb("sm", [P, 3, 2, NH])
        ncum = sb("ncum", [P, 2, NH])
        ex = sb("ex", [P, 3, 2, NH])
        sz = sb("sz", [P, 2, DI])
        em = sb("em", [P, 2, NH, P])
        xh = sb("xh", [P, 2, DI])
        dtx = sb("dtx", [P, 2, DI])
        wdtx = sb("wdtx", [P, 2, DI])
        state = sb("state", [P, ROWS, DI])
        y = sb("y", [P, 2, DI])
        yT = sb("yT", [P, XB, 2, P])
        xr_row = sb("xr_row", [P, 2, ROW])
        xr = xr_row[:, :, 0:DM]
        x0 = sb("x0", [P, 2, DM])
        s1 = sb("s1", [P, 2, DM])
        st_c = sb("st_c", [P, 2, 6])
        mv_c = sb("mv_c", [P, 2, 2])
        var_c = sb("var_c", [P, 2])
        rs_c = sb("rs_c", [P, 2])
        x1 = sb("x1", [P, 2, DM])
        st_b = sb("st_b", [P, 2, 6])
        mv_b = sb("mv_b", [P, 2, 2])
        var_b = sb("var_b", [P, 2])
        nr_b = sb("nr_b", [P, 2, 2])
        nm_b, rs_b = nr_b[:, 0, :], nr_b[:, 1, :]
        kept = sb("kept", [P, UNITS, 2, 2])
        nm_c, nm_f = sb("nm_c", [P, 2]), sb("nm_f", [P, 2])
        xb = sb("xb", [P, 2, DM])
        xbT = sb("xbT", [P, KC, 2, P])
        qkv = sb("qkv", [P, 2 * ROWS, 3 * DM])
        spread = sb("spread", [P, 2 * RING * ROW])
        prod = spread[:, 0:2 * ROWS * DM].rearrange("p (r s d) -> p r s d", r=2, s=ROWS)
        ring = spread[:, :].rearrange("p (n d) -> p n d", d=ROW)
        sc = sb("sc", [P, 2, ROWS, AH])
        mx = sb("mx", [P, 2, AH])
        pr = sb("pr", [P, 2, ROWS, AH])
        den = sb("den", [P, 2, AH])
        rden = sb("rden", [P, 2, AH])
        cx = sb("cx", [P, 2, DM])
        cxT = sb("cxT", [P, KC, 2, P])
        x1r = sb("x1r", [P, 2, DM])
        mrb = sb("mrb", [P, 2, 2])
        x0b = sb("x0b", [P, 2, DM])
        s2 = sb("s2", [P, 2, DM])
        st_f = sb("st_f", [P, 2, 6])
        mv_f = sb("mv_f", [P, 2, 2])
        var_f = sb("var_f", [P, 2])
        rs_f = sb("rs_f", [P, 2])
        h = sb("h", [P, 2, DM])
        hT = sb("hT", [P, KC, 2, P])
        logits = sb("logits", [P, TILES, EXP])

        def part(n, size=TILES * EXP):
            if n < 4:
                return em[:, :, :, :].rearrange("p r h t -> p (r h t)")[:, n * TILES * EXP:n * TILES * EXP + size]
            start = RING * ROW + (n - 4) * TILES * EXP
            return spread[:, start:start + size]

        dest_i = sb("dest_i", [P, TILES], I32)
        expert_i = sb("expert_i", [P, SORTED], I32)
        rt = sb("rt", [P, 6, TILES])
        re = sb("re", [P, 5, EXP])
        held = qkv[:, :, :].rearrange("p a b -> p (a b)")
        WE = KC * DM * EXP
        w1 = held[:, 0:WE].rearrange("p (e c n) -> p e c n", e=EXP, c=KC)
        w2 = held[:, WE:2 * WE].rearrange("p (e c n) -> p e c n", e=EXP, c=KC)
        b1 = held[:, 2 * WE:2 * WE + EXP * DM].rearrange("p (e n) -> p e n", e=EXP)
        b2 = held[:, 2 * WE + EXP * DM:2 * WE + 2 * EXP * DM].rearrange("p (e n) -> p e n", e=EXP)
        idx = sb("idx", [P, 2 * RING], I32)
        token_i, token_f = sb("token_i", [P, TILES], I32), sb("token_f", [P, TILES])
        pad_i = sb("pad_i", [P, 1], I32)
        whose = sb("whose", [P, SORTED], I32)
        first_row = sb("first_row", [P, P])

        pX = ps("pX", [P, 2, 512])
        pY = ps("pY", [P, 2, 512])
        pZ = ps("pZ", [P, 2, 512])
        pW = ps("pW", [P, 512])
        pV = ps("pV", [P, 512])
        xT_v = pX[:, :, :].rearrange("p a (b r t) -> p (a b) r t", b=2, r=2)
        yT_v = pZ[:, :, :].rearrange("p a (b r t) -> p (a b) r t", b=2, r=2)

        small_in, w_in_in, weights_in, exp_in = (sem(n) for n in ("small_in", "w_in_in", "weights_in", "exp_in"))
        consts, prep, zeroed = sem("consts"), sem("prep"), sem("zeroed")
        alog_e = sem("alog_e")
        xa_in, xr_in, x1r_in, x1_out, h_out = (sem(n) for n in ("xa_in", "xr_in", "x1r_in", "x1_out", "h_out"))
        LN = 5
        ln_a, xn_ok, xnT_ps, xnT_sb, cbT_ps, cbT_sb = (sem(n) for n in ("ln_a", "xn_ok", "xnT_ps", "xnT_sb", "cbT_ps", "cbT_sb"))
        tok_ps, btok_sb, soft, xs_ps, xs_sb = (sem(n) for n in ("tok_ps", "btok_sb", "soft", "xs_ps", "xs_sb"))
        SOFT = 3
        halo_in, halo_out, conv, xhT_ok = (sem(n) for n in ("halo_in", "halo_out", "conv", "xhT_ok"))
        mr_ok, shift_ok, da_ok, cum_ps, decay, ex_ok = (sem(n) for n in ("mr_ok", "shift_ok", "da_ok", "cum_ps", "decay", "ex_ok"))
        kept_a_ok = sem("kept_a_ok")
        bc_ps, bc_sb = sem("bc_ps"), sem("bc_sb")
        DECAY = 2
        z_ps, sz_ok, arg_ps, exp_ok = (sem(n) for n in ("z_ps", "sz_ok", "arg_ps", "exp_ok"))
        xh_ps, xh_sb, dtx_ok, wdtx_ok, dx_ok = (sem(n) for n in ("xh_ps", "xh_sb", "dtx_ok", "wdtx_ok", "dx_ok"))
        m_ok = [sem(f"m_ok{r}") for r in range(2)]
        inter_ps, intra_ps, st_ps, hdec, h_ok = (sem(n) for n in ("inter_ps", "intra_ps", "st_ps", "hdec", "h_ok"))
        yin_ok, ysum_ok, yd_ok, y_ok = (sem(n) for n in ("yin_ok", "ysum_ok", "yd_ok", "y_ok"))
        yT_ps, yT_sb, out_ps, x0_ok, s1_ok, ln_c, s1n_ok, x1_ok = (sem(n) for n in ("yT_ps", "yT_sb", "out_ps", "x0_ok", "s1_ok", "ln_c", "s1n_ok", "x1_ok"))
        ln_b, kept_ok, xb_ok, xbT_ps, xbT_sb, qkv_ps, qkv_sb = (sem(n) for n in ("ln_b", "kept_ok", "xb_ok", "xbT_ps", "xbT_sb", "qkv_ps", "qkv_sb"))
        qk_ok, sc_ok, mx_ok, scm_ok, e_ok, den_ok, rden_ok = (sem(n) for n in ("qk_ok", "sc_ok", "mx_ok", "scm_ok", "e_ok", "den_ok", "rden_ok"))
        pr_ok, cx_ok = sem("pr_ok"), sem("cx_ok")
        pv_ok = [sem(f"pv_ok{r}") for r in range(2)]
        cxT_ps, cxT_sb, ao_ps, mrb_ok, x0b_ok, x0o_ok, s2_ok = (sem(n) for n in ("cxT_ps", "cxT_sb", "ao_ps", "mrb_ok", "x0b_ok", "x0o_ok", "s2_ok"))
        ln_f, s2n_ok, hg_ok, hb_ok = (sem(n) for n in ("ln_f", "s2n_ok", "hg_ok", "hb_ok"))
        hT_ps, hT_sb, lg_ps, lg_sb = (sem(n) for n in ("hT_ps", "hT_sb", "lg_ps", "lg_sb"))
        dest_ok = sem("dest_ok")
        route, onehot_ok, routed, r_exp, r_ps, idx_ok = (sem(n) for n in ("route", "onehot_ok", "routed", "r_exp", "r_ps", "idx_ok"))
        hs_in = [sem(f"hs_in{j}") for j in range(2)]
        scattered = [sem(f"scattered{j}") for j in range(2)]
        ha_in, h2_in, haT_ps, haT_sb, f1_ps, g_ok, gT_ps, gT_sb, f2_ps = (
            sem(n) for n in ("ha_in", "h2_in", "haT_ps", "haT_sb", "f1_ps", "g_ok", "gT_ps", "gT_sb", "f2_ps"))
        s3_ok, ln_g, s3n_ok, l2g_ok, l2b_ok, ln_h, y_fin = (
            sem(n) for n in ("s3_ok", "ln_g", "s3n_ok", "l2g_ok", "l2b_ok", "ln_h", "y_fin"))
        gathered = [sem(f"gathered{r}") for r in range(2)]
        whose_ok, sum_ok, idx2_ok, idx3_ok, filled, out_sent = (
            sem(n) for n in ("whose_ok", "sum_ok", "idx2_ok", "idx3_ok", "filled", "out_sent"))

        x_v = a["x"].rearrange("b (c p) d -> c p b d", p=P)
        x1_v = a["x1_d"][0:TOKENS, :].rearrange("(b c p) d -> c p b d", b=ROWS, p=P)
        h_v = a["h_d"].rearrange("(v r p) d -> v p r d", r=2, p=P)
        h_n = a["h_d"].rearrange("(n p) d -> p n d", p=P)
        sorted_n = a["sorted_d"].rearrange("(n p) d -> p n d", p=P)
        sorted_rows = a["sorted_d"].rearrange("(v r p) d -> v p r d", r=2, p=P)
        sorted_v = a["sorted_d"][:, 0:DM].rearrange("(v r p) d -> v p r d", r=2, p=P)

        def at(view, i):
            if isinstance(i, int):
                return view[i]
            return view[bass.ds(i, 1)].rearrange("o p r d -> (o p) r d")

        def x_unit(view, v):
            if isinstance(v, int):
                return view[v // PAIRS][:, 2 * (v % PAIRS):2 * (v % PAIRS) + 2, :]
            chunk = v >> 2
            chunk.max_val = CHUNKS - 1
            return view[bass.ds(chunk, 1), :, bass.ds((v & 3) * 2, 2), :].rearrange("o p r d -> (o p) r d")

        def rows_of(v):
            return slice(2 * (v % PAIRS), 2 * (v % PAIRS) + 2) if isinstance(v, int) else bass.ds((v & 3) * 2, 2)

        def row_of(v, r):
            return slice(2 * (v % PAIRS) + r, 2 * (v % PAIRS) + r + 1) if isinstance(v, int) else bass.ds((v & 3) * 2 + r, 1)

        def slot_of(v, r):
            return slice(2 * (v % 8) + r, 2 * (v % 8) + r + 1) if isinstance(v, int) else bass.ds((v & 7) * 2 + r, 1)

        def group_of(v):
            return slice(ROWS * (v // 4 % 2), ROWS * (v // 4 % 2) + ROWS) if isinstance(v, int) else bass.ds(((v >> 2) & 1) * ROWS, ROWS)

        def unit_slice(v, n=1):
            return slice(v * n, v * n + n) if isinstance(v, int) else bass.ds(v * n, n)

        def one(i):
            return slice(i, i + 1) if isinstance(i, int) else bass.ds(i, 1)

        held_column = {}

        def waits_apart(eng, *waits):
            for s, c in waits:
                eng.wait_ge(s, c)
            c = held_column.setdefault(tuple(w[0].name for w in waits), len(held_column))
            if eng.engine == mybir.EngineType.Pool:
                nc.gpsimd.tensor_tensor(pool_held[:, c:c + 1], half[:, 0:1], half[:, 0:1], ALU.mult)
            else:
                nc.vector.memset(dve_held[:, c:c + 1], 0.0)

        def weighted(engine, p, r):
            engine.tensor_tensor(prod[:, r, :, :].rearrange("p s (h d) -> p s h d", d=AD),
                                 qkv[:, group_of(p.unit(B2)), 2 * DM:3 * DM].rearrange("p s (h d) -> p s h d", d=AD),
                                 pr[:, r, :, :].unsqueeze(3).to_broadcast([P, ROWS, AH, AD]), ALU.mult).then_inc(pv_ok[r], 1)

        def mask(queue, engine, p, r):
            queue.wait_ge(exp_ok, p.prev(A2, 2, r + 1))
            queue.wait_ge(bc_sb, p.now(A2))
            engine.tensor_tensor(em[:, r, :, :], em[:, r, :, :], bc[:, r, :].unsqueeze(1).to_broadcast([P, NH, P]),
                                 ALU.mult).then_inc(m_ok[r], 1)

        block = ctx.enter_context(nc.Block())

        @block.sync
        def _(sp):
            small = [(norm_w, "norm_w"), (conv_w, "conv_w"), (conv_b, "conv_b")]
            rows = [(dt_bias, "dt_bias"), (a_log, "a_log"), (d_skip, "d_skip"), (qkv_b, "qkv_b"), (o_b, "o_b"),
                    (ln1_g, "ln1_g"), (ln1_b, "ln1_b"), (r_b, "r_b"), (ln2_g, "ln2_g"), (ln2_b, "ln2_b")]
            sp.dma_start(w_in[:], a["w_in"]).then_inc(w_in_in, 16)
            sp.dma_start(xa[:], x_unit(x_v, 0)).then_inc(xa_in, 16)
            for t, n in small:
                sp.dma_start(t[:], a[n]).then_inc(small_in, 16)
            for t, n in rows:
                sp.dma_start(t[:], a[n].partition_broadcast(P)).then_inc(small_in, 16)
            for t, n in ((w_out, "w_out"), (w_qkv, "w_qkv"), (w_o, "w_o"), (w_r, "w_r")):
                sp.dma_start(t[:], a[n]).then_inc(weights_in, 16)

            def body(p):
                if p.runs(A1) and p.first > A1:
                    sp.wait_ge(xn_ok, p.prev(A1))
                    sp.dma_start(xa[:], x_unit(x_v, p.unit(A1))).then_inc(xa_in, 16)
                if p.runs(A3):
                    sp.wait_ge(x1_ok, p.prev(A3))
                    sp.dma_start(xr[:], x_unit(x_v, p.unit(A3))).then_inc(xr_in, 16)
                if p.runs(B3):
                    sp.wait_ge(x0b_ok, p.prev(B3))
                    sp.wait_ge(x1_out, p.prev(B3, 16, 16))
                    sp.dma_start(x1r[:], x_unit(x1_v, p.unit(B3))).then_inc(x1r_in, 16)
                if p.runs(A3):
                    sp.wait_ge(x1_ok, p.now(A3))
                    sp.dma_start(x_unit(x1_v, p.unit(A3)), x1[:]).then_inc(x1_out, 16)
                if p.runs(B3):
                    sp.wait_ge(hb_ok, p.now(B3))
                    sp.dma_start(at(h_v, p.unit(B3)), h[:]).then_inc(h_out, 16)
            MAIN.run(sp, body)

            for r in range(2):
                sp.wait_ge(pv_ok[r], UNITS)
            sp.wait_ge(qk_ok, 2 * UNITS)
            sp.dma_start(w1, a["w1"]).then_inc(exp_in, 16)
            sp.dma_start(w2, a["w2"]).then_inc(exp_in, 16)
            sp.dma_start(b1, a["b1"].partition_broadcast(P)).then_inc(exp_in, 16)
            sp.dma_start(b2, a["b2"].partition_broadcast(P)).then_inc(exp_in, 16)

            sp.wait_ge(h_out, 16 * UNITS)
            sp.wait_ge(cx_ok, 2 * UNITS)
            for j in range(2):
                if j == 1:
                    sp.wait_ge(routed, 1)
                sp.dma_start(ring[:, RING * j:RING * (j + 1), 0:DM], h_n[:, RING * j:RING * (j + 1), :]).then_inc(hs_in[j], 16)
            with sp.Fori(1, TILES // (2 * RING)) as i:
                for j in range(2):
                    sp.wait_ge(scattered[j], i * (16 * RING))
                    sp.dma_start(ring[:, RING * j:RING * (j + 1), 0:DM], h_n[:, bass.ds((2 * i + j) * RING, RING), :]).then_inc(hs_in[j], 16)

            for j in range(2):
                sp.wait_ge(scattered[j], 16 * (TILES // 2))

            def mlp(p):
                if p.runs(C1):
                    sp.wait_ge(haT_ps, p.prev(C1))
                    sp.dma_start(xa[:], at(sorted_v, p.unit(C1))).then_inc(ha_in, 16)
                if p.runs(C4):
                    sp.wait_ge(s3_ok, p.prev(C4))
                    sp.wait_ge(whose_ok, p.prev(C4))
                    sp.dma_start(xr_row[:], at(sorted_rows, p.unit(C4))).then_inc(h2_in, 16)
            MLP.run(sp, mlp)
            sp.wait_ge(x1_out, 16 * UNITS)

        @block.tensor
        def _(pe):
            def transposes(out, src, cols):
                for c in range(cols):
                    for r in range(2):
                        mm = nc.tensor.transpose(out[:, c, r, :], src[:, r, c * P:(c + 1) * P], ident[:])
                return mm

            pWt = pW[:, :].rearrange("p (c r t) -> p c r t", c=2, r=2)
            pVt = pV[:, :].rearrange("p (c r t) -> p c r t", c=2, r=2)

            def project(out, lhs, weights, kn, start_col, cols):
                for k in range(kn):
                    mm = nc.tensor.matmul(out, lhs(k), weights[:, k, start_col:start_col + cols],
                                          start=(k == 0), stop=(k == kn - 1))
                return mm

            pe.wait_ge(consts, 1)
            pe.wait_ge(prep, 1)

            def args(p, r):
                for half_ in range(2):
                    nc.tensor.matmul(pY[:, half_, :], ident_h[:], future[:].unsqueeze(1).to_broadcast([P, 4, P]),
                                     start=True, stop=False, skip_group_check=True)
                    for i in range(4):
                        hd = 4 * half_ + i
                        mm = nc.tensor.matmul(pY[:, half_, i * P:(i + 1) * P], da[:, r, hd:hd + 1].to_broadcast([P, P]),
                                              upto[:], start=False, stop=(i == 3), skip_group_check=True)
                return mm

            def inter(p, r, out):
                return nc.tensor.matmul(out, cb[:, 0, r, :], state[:, row_of(p.unit(A2), r), :], start=True, stop=True)

            def intra(r, out):
                for hd in range(NH):
                    mm = nc.tensor.matmul(out[:, hd * HD:(hd + 1) * HD], em[:, r, hd, :],
                                          dtx[:, r, hd * HD:(hd + 1) * HD], start=True, stop=True)
                return mm

            def new_state(r, out):
                return nc.tensor.matmul(out, cb[:, 1, r, :], wdtx[:, r, :], start=True, stop=True)

            def body(p):
                if p.first == A3:
                    pe.wait_ge(weights_in, 64)
                    pe.wait_ge(prep, 2)
                if p.runs(A2):
                    pe.wait_ge(da_ok, p.now(A2))
                    bank_free(pe, p, (yin_ok, p.prev(A2, 2)), (bc_sb, p.prev(A1)))
                    rhs = da[:, :, :].rearrange("p r h -> p (r h)")
                    nc.tensor.matmul(pV[:, 0:16], upto[:], rhs, start=True, stop=True)
                    nc.tensor.matmul(pV[:, 16:32], ones[:], rhs, start=True, stop=True).then_inc(cum_ps, 1)
                if p.runs(B3):
                    pe.wait_ge(cx_ok, p.now(B3, 2))
                    bank_free(pe, p, (qkv_sb, p.prev(B1, 2, -1)), (exp_ok, p.prev(A2, 2)), (xbT_sb, p.prev(B1)), (cxT_sb, p.prev(B3)))
                    transposes(pY[:, 0, :].rearrange("p (c r t) -> p c r t", c=2, r=2), cx, KC).then_inc(cxT_ps, 1)
                if p.runs(B4):
                    pe.wait_ge(hb_ok, p.now(B4))
                    bank_free(pe, p, (yin_ok, p.prev(A2, 2)), (cbT_sb, p.prev(A1)), (lg_sb, p.prev(B4)))
                    transposes(pWt, h, KC).then_inc(hT_ps, 1)
                if p.runs(A2):
                    bank_free(pe, p, (qkv_sb, p.prev(B1, 2)), (xs_sb, p.prev(A1)), (xh_sb, p.prev(A2)))
                    for r in range(2):
                        mm = project(pX[:, r, :], lambda k: xnT[:, k, r, :], w_in, KC, 0, DI)
                    mm.then_inc(z_ps, 1)
                    bank_free(pe, p, (cxT_sb, p.now(B3)), (xnT_sb, p.prev(A1)), (xbT_sb, p.prev(B1)), (qkv_sb, p.prev(B1, 2)),
                              (exp_ok, p.prev(A2, 2)))
                    args(p, 0).then_inc(arg_ps, 1)
                if p.runs(A3):
                    pe.wait_ge(y_ok, p.now(A3))
                    bank_free(pe, p, (h_ok, p.prev(A2, 2)), (ysum_ok, p.prev(A2, 2)), (s2_ok, p.prev(B3)), (soft, p.prev(A1, SOFT)),
                              (btok_sb, p.prev(A1)), (s1_ok, p.prev(A3)))
                    if p.steady:
                        pe.wait_ge(ysum_ok, p.prev(A2, 2))
                    transposes(yT_v, y, XB).then_inc(yT_ps, 1)
                if p.runs(B4):
                    pe.wait_ge(hT_sb, p.now(B4))
                    for r in range(2):
                        mm = project(pW[:, r * EXP:(r + 1) * EXP], lambda k: hT[:, k, r, :], w_r, KC, 0, EXP)
                    mm.then_inc(lg_ps, 1)
                if p.runs(A2):
                    pe.wait_ge(xhT_ok, p.now(A2))
                    pe.wait_ge(sz_ok, p.now(A2))
                    for r in range(2):
                        for b in range(XB):
                            mm = nc.tensor.transpose(pX[:, r, b * P:(b + 1) * P], xhT[:, b, r, :], ident[:])
                    mm.then_inc(xh_ps, 1)
                if p.runs(A3):
                    pe.wait_ge(yT_sb, p.now(A3))
                    for r in range(2):
                        mm = project(pZ[:, 0, r * DM:(r + 1) * DM], lambda k: yT[:, k, r, :], w_out, XB, 0, DM)
                    mm.then_inc(out_ps, 1)
                if p.runs(A1):
                    pe.wait_ge(xn_ok, p.now(A1))
                    bank_free(pe, p, (exp_ok, p.prev(A2, 2, 1)), (qkv_sb, p.prev(B1, 2)), (xnT_sb, p.prev(A1)))
                    transposes(pY[:, 1, :].rearrange("p (c r t) -> p c r t", c=2, r=2), xn, KC).then_inc(xnT_ps, 1)
                if p.runs(B3):
                    pe.wait_ge(cxT_sb, p.now(B3))
                    bank_free(pe, p, (yT_sb, p.now(A3)), (h_ok, p.prev(A2, 2)), (s2_ok, p.prev(B3)))
                    for r in range(2):
                        mm = project(pZ[:, 1, r * DM:(r + 1) * DM], lambda k: cxT[:, k, r, :], w_o, KC, 0, DM)
                    mm.then_inc(ao_ps, 1)
                if p.runs(B1):
                    pe.wait_ge(xb_ok, p.now(B1))
                    bank_free(pe, p, (exp_ok, p.prev(A2, 2, 1)), (cxT_sb, p.now(B3)), (qkv_sb, p.prev(B1, 2)), (xbT_sb, p.prev(B1)))
                    transposes(pY[:, 0, :].rearrange("p (c r t) -> p c r t", c=2, r=2), xb, KC).then_inc(xbT_ps, 1)
                if p.runs(A1):
                    pe.wait_ge(xnT_sb, p.now(A1))
                    bank_free(pe, p, (s1_ok, p.now(A3)), (ysum_ok, p.prev(A2, 2)), (soft, p.prev(A1, SOFT)), (btok_sb, p.prev(A1)))
                    for r in range(2):
                        mm = project(pZ[:, 0, r * WTOK:(r + 1) * WTOK], lambda k: xnT[:, k, r, :], w_in, KC, COL_B, WTOK)
                    mm.then_inc(tok_ps, 1)
                if p.runs(A2):
                    bank_free(pe, p, (xbT_sb, p.now(B1)), (xnT_sb, p.now(A1)), (exp_ok, p.prev(A2, 2, 1)))
                    args(p, 1).then_inc(arg_ps, 1)
                if p.runs(A1):
                    bank_free(pe, p, (lg_sb, p.now(B4)), (yin_ok, p.prev(A2, 2)), (cbT_sb, p.prev(A1)))
                    for m in range(2):
                        for k in range(KC):
                            mm = nc.tensor.matmul(pWt[:, m, :, :], w_in[:, k, COL_C + m * NST:COL_C + (m + 1) * NST],
                                                  xnT[:, k, :, :], start=(k == 0), stop=(k == KC - 1))
                    mm.then_inc(cbT_ps, 1)
                    bank_free(pe, p, (xh_sb, p.now(A2)), (qkv_sb, p.prev(B1, 2)), (xs_sb, p.prev(A1)))
                    for b in range(XB):
                        for k in range(KC):
                            mm = nc.tensor.matmul(xT_v[:, b, :, :], w_in[:, k, COL_X + b * P:COL_X + (b + 1) * P],
                                                  xnT[:, k, :, :], start=(k == 0), stop=(k == KC - 1))
                    mm.then_inc(xs_ps, 1)
                if p.runs(A1):
                    pe.wait_ge(cbT_sb, p.now(A1))
                    bank_free(pe, p, (decay, p.now(A2, DECAY)), (yin_ok, p.prev(A2, 2)), (bc_sb, p.prev(A1)))
                    for r in range(2):
                        mm = nc.tensor.matmul(pV[:, r * P:(r + 1) * P], cb_new[:, 1, r, :], cb_new[:, 0, r, :], start=True, stop=True)
                    mm.then_inc(bc_ps, 1)
                if p.runs(A2):
                    pe.wait_ge(h_ok, p.prev(A2, 2))
                    pe.wait_ge(shift_ok, p.now(A2))
                    bank_free(pe, p, (cbT_sb, p.now(A1)), (lg_sb, p.now(B4)), (yin_ok, p.prev(A2, 2)))
                    inter(p, 0, pW[:, :]).then_inc(inter_ps, 1)
                    pe.wait_ge(m_ok[0], p.now(A2))
                    pe.wait_ge(dtx_ok, p.now(A2))
                    bank_free(pe, p, (soft, p.prev(A1, SOFT, 1)), (s1_ok, p.now(A3)), (ysum_ok, p.prev(A2, 2)))
                    pe.wait_ge(btok_sb, p.now(A1))
                    intra(0, pZ[:, 0, :]).then_inc(intra_ps, 1)
                if p.runs(B1):
                    bank_free(pe, p, (exp_ok, p.now(A2, 2)), (xnT_sb, p.now(A1)), (cxT_sb, p.now(B3)), (qkv_sb, p.prev(B1, 2)))
                    pe.wait_ge(xbT_sb, p.now(B1))
                    project(pY[:, 0, :], lambda k: xbT[:, k, 0, :], w_qkv, KC, 0, 2 * DM)
                    project(pY[:, 1, 0:DM], lambda k: xbT[:, k, 0, :], w_qkv, KC, 2 * DM, DM).then_inc(qkv_ps, 1)
                if p.runs(A2):
                    pe.wait_ge(wdtx_ok, p.now(A2))
                    bank_free(pe, p, (s2_ok, p.now(B3)), (yT_sb, p.now(A3)), (h_ok, p.prev(A2, 2)))
                    new_state(0, pZ[:, 1, :]).then_inc(st_ps, 1)
                    bank_free(pe, p, (bc_sb, p.now(A1)), (decay, p.now(A2, DECAY)))
                    inter(p, 1, pV[:, :]).then_inc(inter_ps, 1)
                    pe.wait_ge(m_ok[1], p.now(A2))
                    pe.wait_ge(ysum_ok, p.prev(A2, 2, 1))
                    intra(1, pZ[:, 0, :]).then_inc(intra_ps, 1)
                    pe.wait_ge(h_ok, p.prev(A2, 2, 1))
                    new_state(1, pZ[:, 1, :]).then_inc(st_ps, 1)
                if p.runs(B1):
                    bank_free(pe, p, (xs_sb, p.now(A1)), (xh_sb, p.now(A2)), (qkv_sb, p.prev(B1, 2)))
                    project(pX[:, 0, :], lambda k: xbT[:, k, 1, :], w_qkv, KC, 0, 2 * DM)
                    project(pX[:, 1, 0:DM], lambda k: xbT[:, k, 1, :], w_qkv, KC, 2 * DM, DM).then_inc(qkv_ps, 1)

            MAIN.run(pe, body)

            pe.wait_ge(onehot_ok, 1)
            pe.wait_ge(qkv_sb, 2 * UNITS)
            onehot = part(5)
            nc.tensor.matmul(pX[:, 0, :], before[:], onehot, start=True, stop=True)
            nc.tensor.matmul(pX[:, 1, :], ones[:], onehot, start=True, stop=True).then_inc(r_ps, 1)

            pe.wait_ge(routed, 1)
            pe.wait_ge(exp_in, 64)

            def expert_of(p, stage, r):
                return pe.value_load(expert_i[0:1, one(p.unit(stage) * 2 + r)], min_val=0, max_val=EXP - 1)

            def layer(out, rowsT, r, weights, bias, e):
                for k in range(KC):
                    nc.tensor.matmul(out, rowsT[:, k, r, :], weights[:, bass.ds(e, 1), k, :], start=(k == 0), stop=False)
                return nc.tensor.matmul(out, first_row[:], bias[:, bass.ds(e, 1), :], start=False, stop=True)

            def mlp(p):
                if p.runs(C1):
                    pe.wait_ge(ha_in, p.prev(C1, 16, 16))
                    pe.wait_ge(haT_sb, p.prev(C1))
                    transposes(pWt, xa, KC).then_inc(haT_ps, 1)
                if p.runs(C3):
                    pe.wait_ge(g_ok, p.now(C3))
                    pe.wait_ge(gT_sb, p.prev(C3))
                    transposes(pVt, cx, KC).then_inc(gT_ps, 1)
                if p.runs(C2):
                    pe.wait_ge(haT_sb, p.now(C2))
                    pe.wait_ge(g_ok, p.prev(C2))
                    for r in range(2):
                        mm = layer(pX[:, 0, r * DM:(r + 1) * DM], xnT, r, w1, b1, expert_of(p, C2, r))
                    mm.then_inc(f1_ps, 1)
                if p.runs(C4):
                    pe.wait_ge(gT_sb, p.now(C4))
                    pe.wait_ge(s3_ok, p.prev(C4))
                    for r in range(2):
                        mm = layer(pY[:, 0, r * DM:(r + 1) * DM], cxT, r, w2, b2, expert_of(p, C4, r))
                    mm.then_inc(f2_ps, 1)
            MLP.run(pe, mlp)

        @block.scalar
        def _(act):
            copy = nc.scalar.copy
            t4 = "p (c r t) -> p c r t"
            act.wait_ge(small_in, 13 * 16)
            nc.scalar.activation(neg_a[:], a_log[:], ACT.Exp).then_inc(alog_e, 1)

            def decays(p, r):
                act.wait_ge(arg_ps, p.prev(A2, 2, r + 1))
                act.wait_ge(intra_ps, p.prev(A2, 2))
                for hd in range(NH):
                    ins = nc.scalar.activation(em[:, r, hd, :], pY[:, hd // 4, (hd % 4) * P:(hd % 4 + 1) * P], ACT.Exp,
                                               bias=ncum[:, r, hd:hd + 1])
                return ins

            def norm_rows(out, x, shift, factor):
                for r in range(2):
                    ins = nc.scalar.activation(out[:, r, :], x[:, r, :], ACT.Identity, bias=shift[:, r:r + 1], scale=factor[:, r:r + 1])
                return ins

            def body(p):
                if p.runs(A3):
                    act.wait_ge(kept_a_ok, p.now(A3))
                    act.wait_ge(x0_ok, p.prev(A3))
                    copy(mr[:], kept_a[:, one(p.unit(A3)), :, :].rearrange("p o a r -> p (o a) r")).then_inc(mr_ok, 1)
                if p.runs(B3):
                    act.wait_ge(kept_ok, p.now(B3))
                    act.wait_ge(x0b_ok, p.prev(B3))
                    copy(mrb[:], kept[:, one(p.unit(B3)), :, :].rearrange("p o a r -> p (o a) r")).then_inc(mrb_ok, 1)
                if p.runs(B3):
                    act.wait_ge(cxT_ps, p.now(B3))
                    act.wait_ge(ao_ps, p.prev(B3))
                    copy(cxT[:], pY[:, 0, :].rearrange(t4, c=2, r=2)).then_inc(cxT_sb, 1)
                if p.runs(B4):
                    act.wait_ge(hT_ps, p.now(B4))
                    act.wait_ge(lg_ps, p.prev(B4))
                    copy(hT[:], pW[:, :].rearrange(t4, c=2, r=2)).then_inc(hT_sb, 1)
                if p.runs(A2):
                    act.wait_ge(xh_ps, p.prev(A2))
                    act.wait_ge(conv, p.now(A2, TAPS))
                    nc.scalar.activation(xhT[:], cv[:], ACT.Silu).then_inc(xhT_ok, 1)
                    act.wait_ge(z_ps, p.now(A2))
                    act.wait_ge(y_ok, p.prev(A2))
                    nc.scalar.activation(sz[:], pX[:], ACT.Silu).then_inc(sz_ok, 1)
                if p.runs(A3):
                    act.wait_ge(xr_in, p.prev(A3, 16, 16))
                    act.wait_ge(s1_ok, p.prev(A3))
                    act.wait_ge(mr_ok, p.now(A3))
                    norm_rows(x0, xr, mr[:, 0, :], mr[:, 1, :]).then_inc(x0_ok, 1)
                if p.runs(A2):
                    act.wait_ge(wdtx_ok, p.prev(A2))
                    act.wait_ge(hdec, p.prev(A2, 2))
                    act.wait_ge(yin_ok, p.prev(A2, 2))
                    act.wait_ge(decay, p.now(A2, DECAY))
                    nc.scalar.activation(ex[:], sm[:], ACT.Exp).then_inc(ex_ok, 1)
                if p.runs(A3):
                    act.wait_ge(yT_ps, p.now(A3))
                    act.wait_ge(out_ps, p.prev(A3))
                    copy(yT[:], yT_v).then_inc(yT_sb, 1)
                if p.runs(A2):
                    act.wait_ge(xh_ps, p.now(A2))
                    act.wait_ge(yd_ok, p.prev(A2))
                    copy(xh[:], pX[:]).then_inc(xh_sb, 1)
                if p.runs(A1):
                    act.wait_ge(ln_a, p.now(A1, LN))
                    act.wait_ge(xnT_ps, p.prev(A1))
                    norm_rows(xn, xa, nm_a[:, 1, :], rs_a[:, 1, :]).then_inc(xn_ok, 1)
                if p.runs(A2):
                    decays(p, 0).then_inc(exp_ok, 1)
                if p.runs(B1):
                    act.wait_ge(ln_b, p.now(B1, LN))
                    act.wait_ge(xbT_ps, p.prev(B1))
                    norm_rows(xb, x1, nm_b, rs_b).then_inc(xb_ok, 1)
                if p.runs(A1):
                    act.wait_ge(xnT_ps, p.now(A1))
                    act.wait_ge(xs_ps, p.prev(A1))
                    act.wait_ge(z_ps, p.now(A2))
                    copy(xnT[:], pY[:, 1, :].rearrange(t4, c=2, r=2)).then_inc(xnT_sb, 1)
                if p.runs(B3):
                    act.wait_ge(mrb_ok, p.now(B3))
                    act.wait_ge(x1r_in, p.prev(B3, 16, 16))
                    act.wait_ge(s2_ok, p.prev(B3))
                    norm_rows(x0b, x1r, mrb[:, 0, :], mrb[:, 1, :]).then_inc(x0b_ok, 1)
                if p.runs(B1):
                    act.wait_ge(xbT_ps, p.now(B1))
                    act.wait_ge(qkv_ps, p.prev(B1, 2))
                    copy(xbT[:], pY[:, 0, :].rearrange(t4, c=2, r=2)).then_inc(xbT_sb, 1)
                if p.runs(A1):
                    act.wait_ge(ln_a, p.now(A1, LN))
                    copy(kept_a[:, one(p.unit(A1)), :, :].rearrange("p o a r -> p (o a) r"), nr_a[:, :, 0, :]).then_inc(kept_a_ok, 1)
                if p.runs(B1):
                    act.wait_ge(ln_b, p.now(B1, LN))
                    copy(kept[:, one(p.unit(B1)), :, :].rearrange("p o a r -> p (o a) r"), nr_b[:]).then_inc(kept_ok, 1)
                if p.runs(A1):
                    act.wait_ge(tok_ps, p.now(A1))
                    act.wait_ge(shift_ok, p.now(A2))
                    copy(cb_new[:, 2, :, :], pZ[:, 0, 0:2 * WTOK].rearrange("p (r w) -> p r w", r=2)[:, :, 0:NST]).then_inc(btok_sb, 1)
                if p.runs(B2):
                    act.wait_ge(scm_ok, p.now(B2))
                    for r in range(2):
                        act.wait_ge(pv_ok[r], p.prev(B2))
                    nc.scalar.activation(pr[:], sc[:], ACT.Exp).then_inc(e_ok, 1)
                if p.runs(A2):
                    decays(p, 1).then_inc(exp_ok, 1)
                if p.runs(A1):
                    act.wait_ge(cbT_ps, p.now(A1))
                    copy(cb_new[:, 0:2, :, :], pW[:, :].rearrange(t4, c=2, r=2)).then_inc(cbT_sb, 1)
                    act.wait_ge(soft, p.prev(A1, SOFT, 1))
                    nc.scalar.activation(dt_e[:], dt_in[:], ACT.Exp).then_inc(soft, 1)
                if p.runs(A3):
                    act.wait_ge(ln_c, p.now(A3, LN))
                    norm_rows(s1, s1, nm_c, rs_c).then_inc(s1n_ok, 1)
                if p.runs(A1):
                    act.wait_ge(bc_ps, p.now(A1))
                    act.wait_ge(m_ok[0], p.now(A2))
                    act.wait_ge(m_ok[1], p.now(A2))
                    copy(bc[:], pV[:, 0:2 * P].rearrange("p (r t) -> p r t", r=2)).then_inc(bc_sb, 1)
                    act.wait_ge(xs_ps, p.now(A1))
                    act.wait_ge(conv, p.prev(A1, TAPS))
                    act.wait_ge(halo_out, p.prev(A1))
                    act.wait_ge(xhT_ok, p.now(A2))
                    for b in range(XB):
                        ins = nc.scalar.activation(cv[:, b, :, :], xT_v[:, b, :, :], ACT.Identity,
                                                   bias=conv_b[:, b:b + 1], scale=conv_w[:, b, TAPS - 1:TAPS])
                    ins.then_inc(conv, 1)
                    copy(xs[:, :, :, TAPS - 1:], xT_v).then_inc(xs_sb, 1)
                if p.runs(B3):
                    act.wait_ge(ln_f, p.now(B3, LN))
                    norm_rows(s2, s2, nm_f, rs_f).then_inc(s2n_ok, 1)
                if p.runs(A1):
                    act.wait_ge(soft, p.prev(A1, SOFT, 2))
                    act.wait_ge(dtx_ok, p.now(A2))
                    act.wait_ge(da_ok, p.prev(A1))
                    nc.scalar.activation(dt[:], dt_e[:], ACT.Ln, bias=1.0).then_inc(soft, 1)

            MAIN.run(act, body)

            act.wait_ge(r_exp, 1)
            nc.scalar.activation(part(0), part(0), ACT.Exp).then_inc(r_exp, 1)

            def mlp(p):
                if p.runs(C2):
                    act.wait_ge(f1_ps, p.now(C2))
                    act.wait_ge(gT_ps, p.now(C3))
                    nc.scalar.activation(cx[:].rearrange("p r d -> p (r d)"), pX[:, 0, :], ACT.Gelu).then_inc(g_ok, 1)
                if p.runs(C1):
                    act.wait_ge(haT_ps, p.now(C1))
                    act.wait_ge(f1_ps, p.now(C2))
                    copy(xnT[:], pW[:, :].rearrange(t4, c=2, r=2)).then_inc(haT_sb, 1)
                if p.runs(C5):
                    act.wait_ge(ln_g, p.now(C5, LN))
                    act.wait_ge(l2g_ok, p.prev(C5))
                    norm_rows(s1, s2, nm_c, rs_c).then_inc(s3n_ok, 1)
                if p.runs(C3):
                    act.wait_ge(gT_ps, p.now(C3))
                    act.wait_ge(f2_ps, p.now(C4))
                    copy(cxT[:], pV[:, :].rearrange(t4, c=2, r=2)).then_inc(gT_sb, 1)
                if p.runs(C6):
                    act.wait_ge(ln_h, p.now(C6, LN))
                    act.wait_ge(sum_ok, p.now(C7, 2))
                    norm_rows(x1, h, nm_f, rs_f).then_inc(y_fin, 1)
            MLP.run(act, mlp)

        @block.vector
        def _(dve):
            v = nc.vector

            def norm_stats(sem, base, x, st, mv, var):
                for r in range(2):
                    ins = v.bn_stats(st[:, r, :], x[:, r, :])
                ins.then_inc(sem, 1)
                waits_apart(dve, (sem, base(1)))
                for r in range(2):
                    ins = v.bn_aggr(mv[:, r, :], st[:, r, :])
                ins.then_inc(sem, 1)
                dve.wait_ge(sem, base(2))
                if var is not None:
                    v.tensor_scalar(var[:, 0:2], mv[:, :, 1], EPS, None, ALU.add).then_inc(sem, 1)
                else:
                    v.tensor_scalar(var_a[:, 0, :], mv[:, :, 1], EPS, None, ALU.add)
                    v.tensor_scalar(var_a[:, 1, :], mv[:, :, 1], 1.0 + RMS_EPS, EPS * RMS_EPS, ALU.mult, ALU.add).then_inc(sem, 1)

            def norm_shift(sem, count, out, mean, factor):
                dve.wait_ge(sem, count)
                v.scalar_tensor_tensor(out, mean, -1.0, factor, ALU.mult, ALU.mult).then_inc(sem, 1)

            dve.wait_ge(small_in, 13 * 16)
            dve.wait_ge(w_in_in, 16)
            for k in range(KC):
                ins = v.tensor_scalar(w_in[:, k, :], w_in[:, k, :], norm_w[:, k:k + 1], None, ALU.mult)
            ins.then_inc(prep, 1)
            dve.wait_ge(alog_e, 1)
            v.tensor_scalar(neg_a[:], neg_a[:], -1.0, None, ALU.mult).then_inc(route, 1)
            dve.wait_ge(prep, 1)
            dve.wait_ge(route, 1)
            dve.wait_ge(consts, 1)

            def products(p, r):
                dve.wait_ge(qkv_sb, p.prev(B1, 2))
                dve.wait_ge(cx_ok, p.prev(B2, 2))
                v.tensor_tensor(prod[:, r, :, :], qkv[:, group_of(p.unit(B2)), DM:2 * DM],
                                qkv[:, slot_of(p.unit(B2), r), 0:DM].to_broadcast([P, ROWS, DM]), ALU.mult).then_inc(qk_ok, 1)

            def sums(p, r):
                dve.wait_ge(qk_ok, p.prev(B2, 2, r + 1))
                dve.wait_ge(e_ok, p.prev(B2))
                v.tensor_reduce(sc[:, r, :, :].rearrange("p s h -> p (s h)"), prod[:, r, :, :].rearrange("p s (h d) -> p (s h) d", d=AD),
                                AX.X, ALU.add).then_inc(sc_ok, 1)

            def context(p, r):
                dve.wait_ge(pv_ok[r], p.now(B2))
                dve.wait_ge(cxT_ps, p.now(B3))
                v.tensor_reduce(cx[:, r, :], prod[:, r, :, :].rearrange("p s c -> p c s"), AX.X, ALU.add).then_inc(cx_ok, 1)

            def inner(p, r, bank):
                dve.wait_ge(inter_ps, p.prev(A2, 2, r + 1))
                dve.wait_ge(ex_ok, p.now(A2))
                dve.wait_ge(yT_ps, p.now(A3))
                yr = y[:, r, :].rearrange("p (h d) -> p h d", h=NH)
                v.tensor_tensor(yr, bank.rearrange("p (h d) -> p h d", h=NH), ex[:, 1, r, :].unsqueeze(2).to_broadcast([P, NH, HD]),
                                ALU.mult).then_inc(yin_ok, 1)
                dve.wait_ge(intra_ps, p.prev(A2, 2, r + 1))
                dve.wait_ge(yin_ok, p.prev(A2, 2, r + 1))
                v.tensor_tensor(y[:, r, :], pZ[:, 0, :], y[:, r, :], ALU.add).then_inc(ysum_ok, 1)

            def carry(p, r):
                dve.wait_ge(st_ps, p.prev(A2, 2, r + 1))
                dve.wait_ge(hdec, p.prev(A2, 2, r + 1))
                st = state[:, row_of(p.unit(A2), r), :].rearrange("p o n -> p (o n)")
                v.tensor_tensor(st, pZ[:, 1, :], st, ALU.add).then_inc(h_ok, 1)

            def biased(p, r, bank):
                dve.wait_ge(qkv_ps, p.prev(B1, 2, r + 1))
                for t in range(2):
                    dve.wait_ge(pv_ok[t], p.prev(B2))
                v.tensor_tensor(qkv[:, slot_of(p.unit(B1), r), :].rearrange("p o n -> p (o n)"),
                                bank.rearrange("p a n -> p (a n)")[:, 0:3 * DM], qkv_b[:], ALU.add).then_inc(qkv_sb, 1)

            def body(p):
                if p.runs(B1):
                    dve.wait_ge(x1_ok, p.now(B1))
                    dve.wait_ge(xb_ok, p.prev(B1))
                    norm_stats(ln_b, lambda n: p.prev(B1, LN, n), x1, st_b, mv_b, var_b)
                if p.runs(A2):
                    dve.wait_ge(cum_ps, p.now(A2))
                    dve.wait_ge(ex_ok, p.prev(A2))
                    dve.wait_ge(exp_ok, p.prev(A2, 2))
                    v.tensor_copy(sm[:, 1:3, :, :].rearrange("p a r h -> p (a r h)"), pV[:, 0:32]).then_inc(decay, 1)
                if p.runs(A1):
                    dve.wait_ge(xa_in, p.prev(A1, 16, 16))
                    dve.wait_ge(xn_ok, p.prev(A1))
                    norm_stats(ln_a, lambda n: p.prev(A1, LN, n), xa, st_a, mv_a, None)
                if p.runs(A2):
                    dve.wait_ge(decay, p.prev(A2, DECAY, 1))
                    v.tensor_tensor(sm[:, 0, :, :], sm[:, 2, :, :], sm[:, 1, :, :], ALU.subtract)
                    v.tensor_scalar(ncum[:], sm[:, 1, :, :], -1.0, None, ALU.mult).then_inc(decay, 1)
                if p.runs(B2):
                    products(p, 0)
                if p.runs(A1):
                    norm_shift(ln_a, p.prev(A1, LN, 4), nm_a, mv_a[:, :, 0].unsqueeze(1).to_broadcast([P, 2, 2]), rs_a)
                if p.runs(B1):
                    norm_shift(ln_b, p.prev(B1, LN, 4), nm_b, mv_b[:, :, 0], rs_b)
                if p.runs(B2):
                    sums(p, 0)
                    products(p, 1)
                if p.runs(A3):
                    dve.wait_ge(out_ps, p.now(A3))
                    dve.wait_ge(x1_ok, p.prev(A3))
                    dve.wait_ge(x0_ok, p.now(A3))
                    v.tensor_tensor(s1[:].rearrange("p r d -> p (r d)"), pZ[:, 0, :], x0[:].rearrange("p r d -> p (r d)"), ALU.add).then_inc(s1_ok, 1)
                if p.runs(B2):
                    sums(p, 1)
                    dve.wait_ge(sc_ok, p.now(B2, 2))
                    v.tensor_reduce(mx[:], sc[:].rearrange("p r s h -> p r h s"), AX.X, ALU.max).then_inc(mx_ok, 1)
                    dve.wait_ge(mx_ok, p.now(B2))
                    v.tensor_tensor(sc[:], sc[:], mx[:].unsqueeze(2).to_broadcast([P, 2, ROWS, AH]), ALU.subtract).then_inc(scm_ok, 1)
                if p.runs(B4):
                    dve.wait_ge(lg_ps, p.now(B4))
                    v.tensor_tensor(logits[:, unit_slice(p.unit(B4), 2), :], pW[:, 0:2 * EXP].rearrange("p (r e) -> p r e", r=2),
                                    r_b[:].unsqueeze(1).to_broadcast([P, 2, EXP]), ALU.add).then_inc(lg_sb, 1)
                if p.runs(A1):
                    dve.wait_ge(btok_sb, p.now(A1))
                    dve.wait_ge(soft, p.prev(A1, SOFT))
                    v.tensor_tensor(dt_in[:], pZ[:, 0, 0:2 * WTOK].rearrange("p (r w) -> p r w", r=2)[:, :, NST:WTOK],
                                    dt_bias[:].unsqueeze(1).to_broadcast([P, 2, NH]), ALU.add).then_inc(soft, 1)
                if p.runs(B2):
                    dve.wait_ge(e_ok, p.now(B2))
                    v.tensor_reduce(den[:], pr[:].rearrange("p r s h -> p r h s"), AX.X, ALU.add).then_inc(den_ok, 1)
                    dve.wait_ge(den_ok, p.now(B2))
                    v.reciprocal(rden[:], den[:]).then_inc(rden_ok, 1)
                    dve.wait_ge(rden_ok, p.now(B2))
                    v.tensor_tensor(pr[:], pr[:], rden[:].unsqueeze(2).to_broadcast([P, 2, ROWS, AH]), ALU.mult).then_inc(pr_ok, 1)
                    if not p.runs(A2):
                        dve.wait_ge(pr_ok, p.now(B2))
                        weighted(v, p, 1)
                        context(p, 1)
                if p.runs(A3):
                    dve.wait_ge(s1_ok, p.now(A3))
                    norm_stats(ln_c, lambda n: p.prev(A3, LN, n), s1, st_c, mv_c, var_c)
                if p.runs(B3):
                    dve.wait_ge(ao_ps, p.now(B3))
                    dve.wait_ge(x0o_ok, p.now(B3))
                    dve.wait_ge(hg_ok, p.prev(B3))
                    v.tensor_tensor(s2[:].rearrange("p r d -> p (r d)"), pZ[:, 1, :], x0b[:].rearrange("p r d -> p (r d)"), ALU.add).then_inc(s2_ok, 1)
                    dve.wait_ge(s2_ok, p.now(B3))
                    norm_stats(ln_f, lambda n: p.prev(B3, LN, n), s2, st_f, mv_f, var_f)
                if p.runs(A2):
                    mask(dve, v, p, 1)
                if p.runs(B2):
                    context(p, 0)
                if p.runs(A3):
                    norm_shift(ln_c, p.prev(A3, LN, 4), nm_c[:], mv_c[:, :, 0], rs_c[:])
                if p.runs(B3):
                    norm_shift(ln_f, p.prev(B3, LN, 4), nm_f[:], mv_f[:, :, 0], rs_f[:])
                if p.runs(A2):
                    inner(p, 0, pW[:, :])
                if p.runs(B2) and p.runs(A2):
                    context(p, 1)
                if p.runs(A2):
                    carry(p, 0)

                def taps(k):
                    dve.wait_ge(conv, p.prev(A1, TAPS, k + 1))
                    for b in range(XB):
                        ins = v.scalar_tensor_tensor(cv[:, b, :, :], xs[:, b, :, k:k + P], conv_w[:, b, k:k + 1], cv[:, b, :, :],
                                                     ALU.mult, ALU.add)
                    ins.then_inc(conv, 1)

                if p.runs(A1):
                    dve.wait_ge(xs_sb, p.now(A1))
                    dve.wait_ge(halo_in, p.now(A1))
                    taps(0)
                if p.runs(B1):
                    biased(p, 0, pY[:, :, :])
                if p.runs(A2):
                    inner(p, 1, pV[:, :])
                    carry(p, 1)
                if p.runs(A1):
                    dve.wait_ge(soft, p.now(A1, SOFT))
                    dve.wait_ge(arg_ps, p.now(A2, 2))
                    v.tensor_tensor(da[:], dt[:], neg_a[:].unsqueeze(1).to_broadcast([P, 2, NH]), ALU.mult).then_inc(da_ok, 1)
                if p.runs(B1):
                    biased(p, 1, pX[:, :, :])
                if p.runs(A1):
                    taps(1)
                if p.runs(A1):
                    taps(2)
                if p.first == A1:
                    dve.wait_ge(weights_in, 64)
                    for k in range(KC):
                        v.tensor_scalar(w_qkv[:, k, 0:DM], w_qkv[:, k, 0:DM], AD ** -0.5, None, ALU.mult)
                    v.tensor_scalar(qkv_b[:, 0:DM], qkv_b[:, 0:DM], AD ** -0.5, None, ALU.mult).then_inc(prep, 1)

            MAIN.run(dve, body)

            count = [1]

            def then(ins):
                count[0] += 1
                ins.then_inc(route, 1)
                dve.wait_ge(route, count[0])

            TE = TILES * EXP
            te = "p (t e) -> p t e"
            lg = logits[:]
            prob, eq, cand, one1, oneh = part(0), part(1), part(2), part(3), part(5)
            key_b = key[:].unsqueeze(1).to_broadcast([P, TILES, EXP])

            def by_tile(row):
                return row.unsqueeze(2).to_broadcast([P, TILES, EXP])

            dve.wait_ge(lg_sb, UNITS)
            dve.wait_ge(cx_ok, 2 * UNITS)
            P3, EQ3, C3, O3, H3 = (q.rearrange(te, e=EXP) for q in (prob, eq, cand, one1, oneh))
            then(v.tensor_reduce(rt[:, 0, :], lg, AX.X, ALU.max))
            v.tensor_tensor(P3, lg, by_tile(rt[:, 0, :]), ALU.subtract).then_inc(r_exp, 1)
            dve.wait_ge(r_exp, 2)
            then(v.tensor_reduce(rt[:, 0, :], P3, AX.X, ALU.add))
            then(v.reciprocal(rt[:, 1, :], rt[:, 0, :]))
            then(v.tensor_tensor(P3, P3, by_tile(rt[:, 1, :]), ALU.mult))
            then(v.tensor_reduce(rt[:, 2, :], P3, AX.X, ALU.max))
            then(v.tensor_tensor(EQ3, P3, by_tile(rt[:, 2, :]), ALU.is_equal))
            then(v.tensor_tensor(C3, EQ3, key_b, ALU.mult))
            then(v.tensor_reduce(rt[:, 3, :], C3, AX.X, ALU.max))
            then(v.tensor_tensor(O3, key_b, by_tile(rt[:, 3, :]), ALU.is_equal))
            then(v.scalar_tensor_tensor(prob, one1, -2.0, prob, ALU.mult, ALU.add))
            then(v.tensor_reduce(rt[:, 2, :], P3, AX.X, ALU.max))
            then(v.tensor_tensor(EQ3, P3, by_tile(rt[:, 2, :]), ALU.is_equal))
            then(v.tensor_tensor(C3, EQ3, key_b, ALU.mult))
            then(v.tensor_reduce(rt[:, 4, :], C3, AX.X, ALU.max))
            then(v.tensor_tensor(rt[:, 5, :], rt[:, 3, :], rt[:, 4, :], ALU.min))
            v.tensor_tensor(H3, key_b, by_tile(rt[:, 5, :]), ALU.is_equal).then_inc(onehot_ok, 1)
            dve.wait_ge(onehot_ok, 1)
            dve.wait_ge(r_ps, 1)
            tot, incl, rank = part(1), part(2), part(3)
            then(v.tensor_copy(tot, pX[:, 1, :]))
            incl3 = incl.rearrange("p (e t) -> p e t", e=EXP)
            for e in range(EXP):
                ins = v.tensor_tensor_scan(incl3[:, e, :], tot.rearrange(te, e=EXP)[:, :, e], zero[:, 0:TILES], 0.0, ALU.add, ALU.add)
            then(ins)
            then(v.tensor_tensor(rank.rearrange(te, e=EXP), incl.rearrange("p (e t) -> p t e", e=EXP), tot.rearrange(te, e=EXP), ALU.subtract))
            then(v.tensor_tensor(rank, pX[:, 0, :], rank, ALU.add))
            then(v.tensor_copy(re[:, 0, :], incl3[:, :, TILES - 1]))
            cmp3 = part(4).rearrange("p (e t) -> p e t", e=EXP)
            then(v.tensor_tensor(cmp3, re[:, 0, :].unsqueeze(2).to_broadcast([P, EXP, TILES]),
                                 count_f[:, 0:TILES].unsqueeze(1).to_broadcast([P, EXP, TILES]), ALU.is_gt))
            then(v.tensor_reduce(re[:, 1, :], cmp3, AX.X, ALU.add))
            then(v.tensor_tensor_scan(re[:, 2, :], re[:, 1, :], zero[:, 0:EXP], 0.0, ALU.add, ALU.add))
            then(v.tensor_tensor(re[:, 3, :], re[:, 2, :], re[:, 1, :], ALU.subtract))
            then(v.tensor_scalar(re[:, 3, :], re[:, 3, :], float(P), None, ALU.mult))
            then(v.tensor_tensor(rank.rearrange(te, e=EXP), rank.rearrange(te, e=EXP), re[:, 3, :].unsqueeze(1).to_broadcast([P, TILES, EXP]), ALU.add))
            then(v.tensor_tensor(rank, rank, oneh, ALU.mult))
            then(v.tensor_reduce(rt[:, 0, :], rank.rearrange(te, e=EXP), AX.X, ALU.add))
            v.tensor_copy(dest_i[:], rt[:, 0, :]).then_inc(dest_ok, 1)
            then(v.tensor_scalar(re[:, 2, :], re[:, 2, :], float(P), None, ALU.mult))
            cmps = part(6, SORTED * EXP).rearrange(te, e=EXP)
            then(v.tensor_tensor(cmps, count_f[:].unsqueeze(2).to_broadcast([P, SORTED, EXP]),
                                 re[:, 2, :].unsqueeze(1).to_broadcast([P, SORTED, EXP]), ALU.is_ge))
            expert_f = part(4, SORTED)
            then(v.tensor_reduce(expert_f, cmps, AX.X, ALU.add))
            then(v.tensor_scalar(expert_f, expert_f, float(EXP - 1), None, ALU.min))
            v.tensor_copy(expert_i[:], expert_f).then_inc(routed, 1)
            dve.wait_ge(routed, 1)

            def mlp(p):
                def residual(r):
                    dve.wait_ge(gathered[r], p.now(C7, 16))
                    dve.wait_ge(y_fin, p.now(C7))
                    if p.first > C7:
                        dve.wait_ge(out_sent, p.prev(C7, 32, 16 * (r - 1)))
                    v.tensor_tensor(xb[:, r, :], x1[:, r, :], x0b[:, r, :], ALU.add).then_inc(sum_ok, 1)

                if p.runs(C7):
                    residual(0)
                if p.runs(C5):
                    norm_shift(ln_g, p.now(C5, LN, -1), nm_c[:], mv_c[:, :, 0], rs_c[:])
                if p.runs(C6):
                    norm_shift(ln_h, p.now(C6, LN, -1), nm_f[:], mv_f[:, :, 0], rs_f[:])
                if p.runs(C7):
                    residual(1)
                if p.runs(C4):
                    dve.wait_ge(h2_in, p.prev(C4, 16, 16))
                    dve.wait_ge(f2_ps, p.now(C4))
                    dve.wait_ge(s3n_ok, p.now(C5))
                    v.tensor_tensor(s2[:], pY[:, 0, :].rearrange("p (r d) -> p r d", r=2), xr[:], ALU.add).then_inc(s3_ok, 1)
                if p.runs(C4):
                    dve.wait_ge(s3_ok, p.now(C4))
                    norm_stats(ln_g, lambda n: p.prev(C4, LN, n), s2, st_c, mv_c, var_c)
                if p.runs(C5):
                    dve.wait_ge(s3n_ok, p.now(C5))
                    v.tensor_tensor(x0[:], s1[:], ln2_g[:].unsqueeze(1).to_broadcast([P, 2, DM]), ALU.mult).then_inc(l2g_ok, 1)
                    dve.wait_ge(l2g_ok, p.now(C5))
                    dve.wait_ge(y_fin, p.now(C6))
                    v.tensor_tensor(h[:], x0[:], ln2_b[:].unsqueeze(1).to_broadcast([P, 2, DM]), ALU.add).then_inc(l2b_ok, 1)
                    dve.wait_ge(l2b_ok, p.now(C5))
                    norm_stats(ln_h, lambda n: p.prev(C5, LN, n), h, st_f, mv_f, var_f)
            MLP.run(dve, mlp)

        @block.gpsimd
        def _(pool):
            g = nc.gpsimd
            steps = [0]

            def const(ins):
                steps[0] += 1
                ins.then_inc(zeroed, 1)
                pool.wait_ge(zeroed, steps[0])

            g.memset(state[:], 0.0)
            g.memset(halo[:], 0.0)
            g.memset(half[:], -0.5)
            const(g.memset(first_row[:], 0.0))
            g.memset(first_row[0:1, :], 1.0)
            g.memset(zero[:, 0:DM], 0.0)
            const(g.iota(pad_i[:], pattern=[[0, 1]], base=TOKENS, channel_multiplier=1))
            const(g.tensor_copy(zero[:, DM:ROW], pad_i[:]))
            const(g.iota(token_i[:], pattern=[[P, CHUNKS], [SEQ, ROWS]], base=0, channel_multiplier=1))
            const(g.tensor_copy(token_f[:], token_i[:]))
            for e in range(EXP):
                g.memset(key[:, e:e + 1], float(EXP - e))
            g.memset(ones[:], 1.0)
            g.memset(ident[:], 0.0)
            g.memset(ident_h[:], 0.0)
            g.memset(upto[:], 1.0)
            g.memset(before[:], 1.0)
            g.memset(future[:], 0.0)
            const(g.iota(count_i[:], pattern=[[P, SORTED]], base=0, channel_multiplier=0))
            for t in (ident, ident_h):
                g.affine_select(out=t[:], in_=t[:], compare_op=ALU.not_equal, fill=1.0, base=0, pattern=[[-1, P]], channel_multiplier=1)
            g.affine_select(out=upto[:], in_=upto[:], compare_op=ALU.is_ge, fill=0.0, base=0, pattern=[[1, P]], channel_multiplier=-1)
            g.affine_select(out=before[:], in_=before[:], compare_op=ALU.is_ge, fill=0.0, base=-1, pattern=[[1, P]], channel_multiplier=-1)
            g.affine_select(out=future[:], in_=future[:], compare_op=ALU.is_ge, fill=NEG, base=0, pattern=[[1, P]], channel_multiplier=-1)
            g.tensor_copy(count_f[:], count_i[:]).then_inc(consts, 1)
            pool.wait_ge(consts, 1)

            def power(sem, count, out, in_):
                pool.wait_ge(sem, count)
                g.tensor_tensor(out, in_, half[:, 0:2] if len(in_.shape) == 2 else half[:].rearrange("p (a r) -> p a r", a=2),
                                ALU.pow).then_inc(sem, 1)

            def by_heads(t, r):
                return t[:, r, :].rearrange("p (h d) -> p h d", h=NH)

            FILLS = 3

            def body(p):
                if 0 < p.first <= FILLS:
                    tiles = slice((p.first - 1) * SORTED // FILLS, p.first * SORTED // FILLS)
                    pool.dma_start(sorted_n[:, tiles, :], zero[:].unsqueeze(1).to_broadcast([P, SORTED // FILLS, ROW])).then_inc(filled, 16)
                if p.first == 0:
                    pool.dma_start(a["x1_d"][TOKENS:TOKENS + P, :], zero[:, 0:DM]).then_inc(filled, 16)
                if p.runs(A2):
                    waits_apart(pool, (cbT_sb, p.now(A2)), (btok_sb, p.now(A2)), (inter_ps, p.prev(A2, 2)), (st_ps, p.prev(A2, 2)))
                    g.tensor_copy(cb[:], cb_new[:, 0:3:2, :, :]).then_inc(shift_ok, 1)
                if p.runs(B1):
                    power(ln_b, p.prev(B1, LN, 3), rs_b, var_b[:])
                if p.runs(A1):
                    power(ln_a, p.prev(A1, LN, 3), rs_a, var_a[:])
                    waits_apart(pool, (conv, p.prev(A1, TAPS)), (halo_out, p.prev(A1)))
                    g.tensor_copy(xs[:, :, :, 0:TAPS - 1].rearrange("p b r k -> p r b k"), halo[:, rows_of(p.unit(A1)), :, :]).then_inc(halo_in, 1)
                if p.runs(A2):
                    pool.wait_ge(xh_sb, p.now(A2))
                    pool.wait_ge(intra_ps, p.prev(A2, 2))
                    for r in range(2):
                        ins = g.tensor_tensor(by_heads(dtx, r), by_heads(xh, r), dt[:, r, :].unsqueeze(2).to_broadcast([P, NH, HD]), ALU.mult)
                    ins.then_inc(dtx_ok, 1)
                    pool.wait_ge(dtx_ok, p.now(A2))
                    pool.wait_ge(ex_ok, p.now(A2))
                    pool.wait_ge(st_ps, p.prev(A2, 2))
                    for r in range(2):
                        ins = g.tensor_tensor(by_heads(wdtx, r), by_heads(dtx, r), ex[:, 0, r, :].unsqueeze(2).to_broadcast([P, NH, HD]), ALU.mult)
                    ins.then_inc(wdtx_ok, 1)
                    for r in range(2):
                        ins = g.tensor_tensor(by_heads(xh, r), by_heads(xh, r), d_skip[:].unsqueeze(2).to_broadcast([P, NH, HD]), ALU.mult)
                    ins.then_inc(dx_ok, 1)
                if p.runs(B3):
                    pool.wait_ge(x0b_ok, p.now(B3))
                    g.tensor_tensor(x0b[:], x0b[:], o_b[:].unsqueeze(1).to_broadcast([P, 2, DM]), ALU.add).then_inc(x0o_ok, 1)

                def decayed(r):
                    pool.wait_ge(inter_ps, p.prev(A2, 2, r + 1))
                    st = state[:, row_of(p.unit(A2), r), :].rearrange("p o (h d) -> p (o h) d", h=NH)
                    g.tensor_tensor(st, st, ex[:, 2, r, :].unsqueeze(2).to_broadcast([P, NH, HD]), ALU.mult).then_inc(hdec, 1)

                if p.runs(A2):
                    mask(pool, g, p, 0)
                if p.runs(B2):
                    pool.wait_ge(pr_ok, p.now(B2))
                    weighted(g, p, 0)
                if p.runs(A3):
                    power(ln_c, p.prev(A3, LN, 3), rs_c[:], var_c[:])
                if p.runs(B3):
                    power(ln_f, p.prev(B3, LN, 3), rs_f[:], var_f[:])
                if p.runs(B2) and p.runs(A2):
                    weighted(g, p, 1)
                if p.runs(A2):
                    decayed(0)
                if p.runs(A3):
                    pool.wait_ge(s1n_ok, p.now(A3))
                    pool.wait_ge(x1_out, p.prev(A3, 16))
                    pool.wait_ge(xb_ok, p.now(B1))
                    g.tensor_tensor(x1[:], s1[:], xr[:], ALU.add).then_inc(x1_ok, 1)
                if p.runs(A2):
                    decayed(1)
                if p.runs(A1):
                    waits_apart(pool, (xs_sb, p.now(A1)), (halo_in, p.now(A1)))
                    g.tensor_copy(halo[:, rows_of(p.unit(A1)), :, :], xs[:, :, :, P:P + TAPS - 1].rearrange("p b r k -> p r b k")).then_inc(halo_out, 1)
                if p.runs(B3):
                    pool.wait_ge(s2n_ok, p.now(B3))
                    pool.wait_ge(hT_ps, p.now(B4))
                    pool.wait_ge(h_out, p.prev(B3, 16))
                    g.tensor_tensor(h[:], s2[:], ln1_g[:].unsqueeze(1).to_broadcast([P, 2, DM]), ALU.mult).then_inc(hg_ok, 1)
                    pool.wait_ge(hg_ok, p.now(B3))
                    g.tensor_tensor(h[:], h[:], ln1_b[:].unsqueeze(1).to_broadcast([P, 2, DM]), ALU.add).then_inc(hb_ok, 1)
                if p.runs(A2):
                    pool.wait_ge(ysum_ok, p.now(A2, 2))
                    pool.wait_ge(dx_ok, p.now(A2))
                    pool.wait_ge(sz_ok, p.now(A2))
                    g.tensor_tensor(y[:], y[:], xh[:], ALU.add).then_inc(yd_ok, 1)
                    pool.wait_ge(yd_ok, p.now(A2))
                    g.tensor_tensor(y[:], y[:], sz[:], ALU.mult).then_inc(y_ok, 1)

            MAIN.run(pool, body)

            pool.wait_ge(dest_ok, 1)
            pool.wait_ge(filled, 16 * (FILLS + 1))

            def scatter(i):
                for j in range(2):
                    if isinstance(i, int) and j == 1:
                        pool.wait_ge(routed, 1)
                    if not isinstance(i, int):
                        waits_apart(pool, (scattered[j], i * (16 * RING)))
                    tiles = bass.ds((2 * i + j) * RING, RING) if not isinstance(i, int) else slice(j * RING, (j + 1) * RING)
                    g.tensor_copy(idx[:, j * RING:(j + 1) * RING], dest_i[:, tiles]).then_inc(idx_ok, 1)
                    g.tensor_copy(ring[:, j * RING:(j + 1) * RING, DM], token_f[:, tiles]).then_inc(idx_ok, 1)
                    waits_apart(pool, (idx_ok, i * 4 + j * 2 + 2), (hs_in[j], i * 16 + 16))
                    for q in range(j * RING, (j + 1) * RING):
                        g.indirect_dma_start(a["sorted_d"], bass.IndirectOffsetOnAxis(idx[:, q:q + 1], 0), ring[:, q, :], None).then_inc(scattered[j], 16)

            scatter(0)
            with pool.Fori(1, TILES // (2 * RING)) as i:
                scatter(i)

            for j in range(2):
                pool.wait_ge(scattered[j], 16 * (TILES // 2))

            def send(r):
                g.indirect_dma_start(a["out"], bass.IndirectOffsetOnAxis(idx[:, 2 + r:3 + r], 0), xb[:, r, :], None).then_inc(out_sent, 16)

            def fetch(r):
                g.indirect_dma_start(x0b[:, r, :], None, a["x1_d"], bass.IndirectOffsetOnAxis(idx[:, r:r + 1], 0)).then_inc(gathered[r], 16)

            def mlp(p):
                def number(r):
                    g.tensor_copy(idx[:, 2 + r:3 + r], whose[:, one(p.unit(C7) * 2 + r)]).then_inc(idx2_ok, 1)

                if p.runs(C4):
                    waits_apart(pool, (h2_in, p.prev(C4, 16, 16)))
                    g.tensor_copy(whose[:, unit_slice(p.unit(C4), 2)], xr_row[:, :, DM]).then_inc(whose_ok, 1)
                if p.runs(C7):
                    if p.first > C7:
                        waits_apart(pool, (out_sent, p.prev(C7, 32, -16)))
                    number(0)
                    waits_apart(pool, (idx2_ok, p.prev(C7, 2, 1)), (sum_ok, p.prev(C7, 2, 1)), (out_sent, p.prev(C7, 32)))
                    send(0)
                    number(1)
                if p.runs(C6):
                    waits_apart(pool, (gathered[0], p.prev(C6, 16)), (gathered[1], p.prev(C6, 16)), (sum_ok, p.prev(C7, 2, 1)), (whose_ok, p.now(C6)))
                    g.tensor_copy(idx[:, 0:2], whose[:, unit_slice(p.unit(C6), 2)]).then_inc(idx3_ok, 1)
                    waits_apart(pool, (idx3_ok, p.now(C6)))
                    fetch(0)
                if p.runs(C7):
                    waits_apart(pool, (out_sent, p.prev(C7, 32, 16)), (idx2_ok, p.now(C7, 2)), (sum_ok, p.now(C7, 2)))
                    send(1)
                if p.runs(C6):
                    fetch(1)
                if p.runs(C4):
                    power(ln_g, p.prev(C4, LN, 3), rs_c[:], var_c[:])
                if p.runs(C5):
                    power(ln_h, p.prev(C5, LN, 3), rs_f[:], var_f[:])
            MLP.run(pool, mlp)

            pool.wait_ge(out_sent, 16 * SORTED)


def kernel(**inputs):
    import numpy as np
    import concourse.bacc as bacc
    from concourse.bass_utils import run_bass_kernel_spmd

    g = {k.replace("L0_attn_", "a_").replace("L0_ffn_", "f_"): np.asarray(v) for k, v in inputs.items()}

    def blocks(m):
        m = m.reshape(m.shape[:-2] + (m.shape[-2] // P, P, m.shape[-1]))
        return np.ascontiguousarray(np.moveaxis(m, -2, 0))

    wt = g["a_in_proj_w"].T
    state_b, state_c = wt[:, 2 * DI:2 * DI + NST], wt[:, 2 * DI + NST:2 * DI + 2 * NST]
    arrays = {
        "x": g["a_x"],
        "w_in": blocks(np.concatenate([wt[:, :2 * DI], state_c, state_b, wt[:, 2 * DI + 2 * NST:]], axis=1)),
        "w_out": blocks(g["a_out_proj_w"].T),
        "w_qkv": blocks(g["f_in_proj_w"].T),
        "w_o": blocks(g["f_out_w"].T),
        "w_r": blocks(g["f_router_w"].T),
        "w1": blocks(np.swapaxes(g["f_w1"], 1, 2)),
        "w2": blocks(np.swapaxes(g["f_w2"], 1, 2)),
        "b1": g["f_b1"].reshape(-1), "b2": g["f_b2"].reshape(-1),
        "norm_w": g["a_norm_w"].reshape(KC, P).T, "conv_w": np.moveaxis(g["a_conv_w"].reshape(XB, P, TAPS), 1, 0),
        "conv_b": g["a_conv_b"].reshape(XB, P).T, "dt_bias": g["a_dt_bias"], "a_log": g["a_A_log"], "d_skip": g["a_D"],
        "qkv_b": g["f_in_proj_b"], "o_b": g["f_out_b"], "ln1_g": g["f_ln1_g"], "ln1_b": g["f_ln1_b"], "r_b": g["f_router_b"],
        "ln2_g": g["f_ln2_g"], "ln2_b": g["f_ln2_b"],
    }
    arrays = {k: np.ascontiguousarray(v) for k, v in arrays.items()}
    nc = bacc.Bacc("TRN2", target_bir_lowering=False, num_devices=1)
    a = {k: nc.dram_tensor(f"in_{k}", v.shape, mybir.dt.from_np(v.dtype), kind="ExternalInput").ap() for k, v in arrays.items()}
    a["b1"] = a["b1"].rearrange("(e n) -> e n", e=EXP)
    a["b2"] = a["b2"].rearrange("(e n) -> e n", e=EXP)
    a["out"] = nc.dram_tensor("out", (TOKENS + P, DM), F32, kind="ExternalOutput").ap()
    for name, shape in (("x1_d", (TOKENS + P, DM)), ("h_d", (TOKENS, DM)), ("sorted_d", (SORTED * P, ROW))):
        a[name] = nc.dram_tensor(name, shape, F32, kind="Internal").ap()
    program(nc, a)
    r = run_bass_kernel_spmd(nc, [{f"in_{k}": v for k, v in arrays.items()}], core_ids=[0])
    return r.results[0]["out"][:TOKENS].reshape(ROWS, SEQ, DM)
```
